# Optimizing a Trainium2 kernel written in Bass

```python
import numpy as np
import jax
import jax.numpy as jnp

def _softmax(x, axis=-1):
    return jax.nn.softmax(x, axis=axis)

def _gelu(x):
    return jax.nn.gelu(x, approximate=True)

def _silu(x):
    return jax.nn.silu(x)

def _sigmoid(x):
    return jax.nn.sigmoid(x)

def _layernorm(x, axis=-1, eps=1e-05):
    m = jnp.mean(x, axis=axis, keepdims=True)
    v = jnp.var(x, axis=axis, keepdims=True)
    return (x - m) / jnp.sqrt(v + eps)

def _scatter_add(tgt, idx, src, axis=0):
    return tgt.at[idx].add(src)

def _segment_sum(src, seg, n):
    return jax.ops.segment_sum(src, seg, n)
kernel_name = 'mk_flamingo_gated_d1_seqx_r2_8d81c7'

def setup_inputs(seed: int=0):
    np.random.seed(seed)
    _w = jnp.asarray

    def _rec_inputs():
        import jax
        import jax.numpy as jnp
        _rk = jax.random.key(seed)
        x = -0.0002928 + 1 * jax.random.normal(jax.random.fold_in(_rk, 1), (8, 512, 512), jnp.float32)
        _lenS = 512 - jax.random.randint(jax.random.fold_in(_rk, 7), (8,), 0, max(1, 512 // 4) + 1, jnp.int32)
        _lenS2 = 512 - jax.random.randint(jax.random.fold_in(_rk, 8), (8,), 0, max(1, 512 // 4) + 1, jnp.int32)
        _ctx_1024P = jax.random.normal(jax.random.fold_in(_rk, 11), (8, 16, 512), jnp.float32)
        _ctx_1024c = jax.random.dirichlet(jax.random.fold_in(_rk, 511), 0.3 * jnp.ones((16,), jnp.float32), (8, 512))
        _ctx_1024t = jnp.einsum('bsk,bkd->bsd', _ctx_1024c, _ctx_1024P)
        _ctx_1024t = _ctx_1024t * jax.lax.rsqrt(jnp.mean(jnp.square(_ctx_1024t)) + 1e-12) * 0.953939
        ctx_1024 = -1.39393e-06 + 0.999914 * (_ctx_1024t + 0.3 * jax.random.normal(jax.random.fold_in(_rk, 611), (8, 512, 512), jnp.float32))
        _validS = jnp.arange(512)[None, :] < _lenS[:, None]
        _validS2 = jnp.arange(512)[None, :] < _lenS2[:, None]
        _causal = jnp.tril(jnp.ones((512, 512), dtype=bool))
        mask_BxS2_ik0 = jnp.where(jnp.broadcast_to(_validS2[:, :], (8, 512)), 0, 1).astype(jnp.int32)
        _g = jax.random.normal(jax.random.fold_in(_rk, 9001), (2, 1), jnp.float32)
        _g = jnp.sign(_g) * jnp.maximum(jnp.abs(_g), 1.0) + (_g == 0) * 1.0
        g_xattn = _g[0]
        g_ffn = _g[1]
        return (x, ctx_1024, mask_BxS2_ik0, g_xattn, g_ffn)
    x, ctx_1024, mask_BxS2_ik0, g_xattn, g_ffn = _rec_inputs()

    def _L0_xattn_setup():
        import jax, jax.numpy as jnp
        import numpy as np
        EPS = 1e-05

        def layer_norm(x, gamma):
            mu = jnp.mean(x, axis=-1, keepdims=True)
            var = jnp.mean(jnp.square(x - mu), axis=-1, keepdims=True)
            return (x - mu) / jnp.sqrt(var + EPS) * gamma
        key = jax.random.key(seed)
        ks = jax.random.split(key, 10)
        b, n, j = (2, 1024, 1024)
        dim, ctx_dim, heads, dim_head, ff_mult = (512, 512, 16, 64, 4)
        inner = heads * dim_head
        ff_inner = ff_mult * dim
        s = 0.02
        return {'x': jax.random.normal(ks[0], (b, n, dim), jnp.float32), 'context': jax.random.normal(ks[1], (b, j, ctx_dim), jnp.float32), 'mask': jax.random.randint(ks[2], (b, j), 0, 2, jnp.int32), 'gamma': jnp.ones((dim,), jnp.float32), 'ctx_gamma': jnp.ones((ctx_dim,), jnp.float32), 'Wq': jax.random.normal(ks[3], (dim, inner), jnp.float32) * s, 'Wkv': jax.random.normal(ks[4], (ctx_dim, 2 * dim_head), jnp.float32) * s, 'Wout': jax.random.normal(ks[5], (inner, dim), jnp.float32) * s, 'Wff1': jax.random.normal(ks[6], (dim, 2 * ff_inner), jnp.float32) * s, 'Wff2': jax.random.normal(ks[7], (ff_inner, dim), jnp.float32) * s}
    _L0_xattn_all = _L0_xattn_setup()
    _L0_xattn_in = {k: v for k, v in _L0_xattn_all.items() if k in ('gamma', 'ctx_gamma', 'Wq', 'Wkv', 'Wout', 'Wff1', 'Wff2')}
    del _L0_xattn_all

    def _L0_ffn_setup():
        import jax, jax.numpy as jnp
        import numpy as np
        B, L, D = (4, 1024, 512)
        H = 16
        E = 16
        NS = 16
        S = NS // E
        F = 2048
        EPS = 1e-05

        def _layernorm(x, g, b):
            mu = jnp.mean(x, axis=-1, keepdims=True)
            var = jnp.mean(jnp.square(x - mu), axis=-1, keepdims=True)
            return (x - mu) * jax.lax.rsqrt(var + EPS) * g + b

        def _mha(q, k, v, Wq, bq, Wk, bk, Wv, bv, Wo, bo):
            Bq, Lq, Dm = q.shape
            dh = Dm // H
            qh = (q @ Wq + bq).reshape(Bq, Lq, H, dh)
            kh = (k @ Wk + bk).reshape(Bq, -1, H, dh)
            vh = (v @ Wv + bv).reshape(Bq, -1, H, dh)
            scores = jnp.einsum('bqhd,bkhd->bhqk', qh, kh) / jnp.asarray(np.sqrt(dh), q.dtype)
            attn = jax.nn.softmax(scores, axis=-1)
            out = jnp.einsum('bhqk,bkhd->bqhd', attn, vh).reshape(Bq, Lq, Dm)
            return out @ Wo + bo
        key = jax.random.key(seed)
        ks = jax.random.split(key, 32)
        s = 0.02
        d = {}
        d['x'] = jax.random.normal(ks[0], (B, L, D), jnp.float32)
        d['slot_query'] = jax.random.normal(ks[1], (1, NS, D), jnp.float32) * 0.01
        for i, nm in enumerate(['d_Wq', 'd_Wk', 'd_Wv', 'd_Wo']):
            d[nm] = jax.random.normal(ks[2 + i], (D, D), jnp.float32) * s
        for nm in ['d_bq', 'd_bk', 'd_bv', 'd_bo']:
            d[nm] = jnp.zeros((D,), jnp.float32)
        for i, nm in enumerate(['c_Wq', 'c_Wk', 'c_Wv', 'c_Wo']):
            d[nm] = jax.random.normal(ks[6 + i], (D, D), jnp.float32) * s
        for nm in ['c_bq', 'c_bk', 'c_bv', 'c_bo']:
            d[nm] = jnp.zeros((D,), jnp.float32)
        d['e_ln_g'] = jnp.ones((E, D), jnp.float32)
        d['e_ln_b'] = jnp.zeros((E, D), jnp.float32)
        d['e_W1'] = jax.random.normal(ks[10], (E, D, F), jnp.float32) * s
        d['e_b1'] = jnp.zeros((E, F), jnp.float32)
        d['e_Wg'] = jax.random.normal(ks[11], (E, D, F), jnp.float32) * s
        d['e_bg'] = jnp.zeros((E, F), jnp.float32)
        d['e_W2'] = jax.random.normal(ks[12], (E, F, D), jnp.float32) * s
        d['e_b2'] = jnp.zeros((E, D), jnp.float32)
        return d
    _L0_ffn_all = _L0_ffn_setup()
    _L0_ffn_in = {k: v for k, v in _L0_ffn_all.items() if k in ('slot_query', 'd_Wq', 'd_Wk', 'd_Wv', 'd_Wo', 'd_bq', 'd_bk', 'd_bv', 'd_bo', 'c_Wq', 'c_Wk', 'c_Wv', 'c_Wo', 'c_bq', 'c_bk', 'c_bv', 'c_bo', 'e_ln_g', 'e_ln_b', 'e_W1', 'e_b1', 'e_Wg', 'e_bg', 'e_W2', 'e_b2')}
    del _L0_ffn_all
    return {'x': x, 'ctx_1024': ctx_1024, 'mask_BxS2_ik0': mask_BxS2_ik0, 'g_xattn': g_xattn, 'g_ffn': g_ffn, 'L0_xattn_gamma': _L0_xattn_in['gamma'], 'L0_xattn_ctx_gamma': _L0_xattn_in['ctx_gamma'], 'L0_xattn_Wq': _L0_xattn_in['Wq'], 'L0_xattn_Wkv': _L0_xattn_in['Wkv'], 'L0_xattn_Wout': _L0_xattn_in['Wout'], 'L0_xattn_Wff1': _L0_xattn_in['Wff1'], 'L0_xattn_Wff2': _L0_xattn_in['Wff2'], 'L0_ffn_slot_query': _L0_ffn_in['slot_query'], 'L0_ffn_d_Wq': _L0_ffn_in['d_Wq'], 'L0_ffn_d_Wk': _L0_ffn_in['d_Wk'], 'L0_ffn_d_Wv': _L0_ffn_in['d_Wv'], 'L0_ffn_d_Wo': _L0_ffn_in['d_Wo'], 'L0_ffn_d_bq': _L0_ffn_in['d_bq'], 'L0_ffn_d_bk': _L0_ffn_in['d_bk'], 'L0_ffn_d_bv': _L0_ffn_in['d_bv'], 'L0_ffn_d_bo': _L0_ffn_in['d_bo'], 'L0_ffn_c_Wq': _L0_ffn_in['c_Wq'], 'L0_ffn_c_Wk': _L0_ffn_in['c_Wk'], 'L0_ffn_c_Wv': _L0_ffn_in['c_Wv'], 'L0_ffn_c_Wo': _L0_ffn_in['c_Wo'], 'L0_ffn_c_bq': _L0_ffn_in['c_bq'], 'L0_ffn_c_bk': _L0_ffn_in['c_bk'], 'L0_ffn_c_bv': _L0_ffn_in['c_bv'], 'L0_ffn_c_bo': _L0_ffn_in['c_bo'], 'L0_ffn_e_ln_g': _L0_ffn_in['e_ln_g'], 'L0_ffn_e_ln_b': _L0_ffn_in['e_ln_b'], 'L0_ffn_e_W1': _L0_ffn_in['e_W1'], 'L0_ffn_e_b1': _L0_ffn_in['e_b1'], 'L0_ffn_e_Wg': _L0_ffn_in['e_Wg'], 'L0_ffn_e_bg': _L0_ffn_in['e_bg'], 'L0_ffn_e_W2': _L0_ffn_in['e_W2'], 'L0_ffn_e_b2': _L0_ffn_in['e_b2']}

def reference(x, ctx_1024, mask_BxS2_ik0, g_xattn, g_ffn, L0_xattn_gamma, L0_xattn_ctx_gamma, L0_xattn_Wq, L0_xattn_Wkv, L0_xattn_Wout, L0_xattn_Wff1, L0_xattn_Wff2, L0_ffn_slot_query, L0_ffn_d_Wq, L0_ffn_d_Wk, L0_ffn_d_Wv, L0_ffn_d_Wo, L0_ffn_d_bq, L0_ffn_d_bk, L0_ffn_d_bv, L0_ffn_d_bo, L0_ffn_c_Wq, L0_ffn_c_Wk, L0_ffn_c_Wv, L0_ffn_c_Wo, L0_ffn_c_bq, L0_ffn_c_bk, L0_ffn_c_bv, L0_ffn_c_bo, L0_ffn_e_ln_g, L0_ffn_e_ln_b, L0_ffn_e_W1, L0_ffn_e_b1, L0_ffn_e_Wg, L0_ffn_e_bg, L0_ffn_e_W2, L0_ffn_e_b2):
    import jax
    import jax.numpy as jnp

    def _L0_xattn_ref(x, context, mask, gamma, ctx_gamma, Wq, Wkv, Wout, Wff1, Wff2):
        import jax, jax.numpy as jnp
        import numpy as np
        EPS = 1e-05

        def layer_norm(x, gamma):
            mu = jnp.mean(x, axis=-1, keepdims=True)
            var = jnp.mean(jnp.square(x - mu), axis=-1, keepdims=True)
            return (x - mu) / jnp.sqrt(var + EPS) * gamma
        heads, dim_head = (16, 64)
        b, n, dim = x.shape
        scale = dim_head ** (-0.5)
        xn = layer_norm(x, gamma)
        ctx = layer_norm(context, ctx_gamma)
        q = (xn @ Wq).reshape(b, n, heads, dim_head).transpose(0, 2, 1, 3) * scale
        kv = ctx @ Wkv
        k, v = (kv[..., :dim_head], kv[..., dim_head:])
        sim = jnp.einsum('bhid,bjd->bhij', q, k)
        sim = jnp.where((mask == 0)[:, None, None, :], -jnp.inf, sim)
        attn = jax.nn.softmax(sim, axis=-1)
        out = jnp.einsum('bhij,bjd->bhid', attn, v)
        out = out.transpose(0, 2, 1, 3).reshape(b, n, heads * dim_head)
        out = out @ Wout
        h = xn @ Wff1
        ff_inner = Wff2.shape[0]
        a, gate = (h[..., :ff_inner], h[..., ff_inner:])
        out = out + jax.nn.silu(gate) * a @ Wff2
        return out

    def _L0_ffn_ref(x, slot_query, d_Wq, d_Wk, d_Wv, d_Wo, d_bq, d_bk, d_bv, d_bo, c_Wq, c_Wk, c_Wv, c_Wo, c_bq, c_bk, c_bv, c_bo, e_ln_g, e_ln_b, e_W1, e_b1, e_Wg, e_bg, e_W2, e_b2):
        import jax, jax.numpy as jnp
        import numpy as np
        B, L, D = (4, 1024, 512)
        H = 16
        E = 16
        NS = 16
        S = NS // E
        F = 2048
        EPS = 1e-05

        def _layernorm(x, g, b):
            mu = jnp.mean(x, axis=-1, keepdims=True)
            var = jnp.mean(jnp.square(x - mu), axis=-1, keepdims=True)
            return (x - mu) * jax.lax.rsqrt(var + EPS) * g + b

        def _mha(q, k, v, Wq, bq, Wk, bk, Wv, bv, Wo, bo):
            Bq, Lq, Dm = q.shape
            dh = Dm // H
            qh = (q @ Wq + bq).reshape(Bq, Lq, H, dh)
            kh = (k @ Wk + bk).reshape(Bq, -1, H, dh)
            vh = (v @ Wv + bv).reshape(Bq, -1, H, dh)
            scores = jnp.einsum('bqhd,bkhd->bhqk', qh, kh) / jnp.asarray(np.sqrt(dh), q.dtype)
            attn = jax.nn.softmax(scores, axis=-1)
            out = jnp.einsum('bhqk,bkhd->bqhd', attn, vh).reshape(Bq, Lq, Dm)
            return out @ Wo + bo
        Bx = x.shape[0]
        q = jnp.broadcast_to(slot_query, (Bx, NS, D))
        o = q + _mha(q, x, x, d_Wq, d_bq, d_Wk, d_bk, d_Wv, d_bv, d_Wo, d_bo)
        os = o.reshape(Bx, E, S, D)
        h = _layernorm(os, e_ln_g[None, :, None, :], e_ln_b[None, :, None, :])
        u = jax.nn.silu(jnp.einsum('besd,edf->besf', h, e_W1) + e_b1[None, :, None, :])
        g = jax.nn.silu(jnp.einsum('besd,edf->besf', h, e_Wg) + e_bg[None, :, None, :])
        y = jnp.einsum('besf,efd->besd', u * g, e_W2) + e_b2[None, :, None, :]
        o = o + y.reshape(Bx, NS, D)
        out = _mha(x, o, o, c_Wq, c_bq, c_Wk, c_bk, c_Wv, c_bv, c_Wo, c_bo)
        return out
    x = x + jnp.tanh(g_xattn[0]) * _L0_xattn_ref(_layernorm(x, axis=-1), ctx_1024, mask_BxS2_ik0, L0_xattn_gamma, L0_xattn_ctx_gamma, L0_xattn_Wq, L0_xattn_Wkv, L0_xattn_Wout, L0_xattn_Wff1, L0_xattn_Wff2)
    x = x + jnp.tanh(g_ffn[0]) * _L0_ffn_ref(_layernorm(x, axis=-1), L0_ffn_slot_query, L0_ffn_d_Wq, L0_ffn_d_Wk, L0_ffn_d_Wv, L0_ffn_d_Wo, L0_ffn_d_bq, L0_ffn_d_bk, L0_ffn_d_bv, L0_ffn_d_bo, L0_ffn_c_Wq, L0_ffn_c_Wk, L0_ffn_c_Wv, L0_ffn_c_Wo, L0_ffn_c_bq, L0_ffn_c_bk, L0_ffn_c_bv, L0_ffn_c_bo, L0_ffn_e_ln_g, L0_ffn_e_ln_b, L0_ffn_e_W1, L0_ffn_e_b1, L0_ffn_e_Wg, L0_ffn_e_bg, L0_ffn_e_W2, L0_ffn_e_b2)
    return x

_drawn_inputs = setup_inputs


def setup_inputs(seed=0):
    import zlib

    import numpy as np

    out = dict(_drawn_inputs(seed))
    spreads = {'L0_xattn_gamma': (1.0, 0.6),
     'L0_xattn_ctx_gamma': (1.0, 0.6),
     'L0_ffn_d_bq': (0.0, 0.8),
     'L0_ffn_d_bk': (0.0, 2.0),
     'L0_ffn_d_bv': (0.0, 0.779),
     'L0_ffn_d_bo': (0.0, 0.379),
     'L0_ffn_c_bq': (0.0, 0.8),
     'L0_ffn_c_bk': (0.0, 2.0),
     'L0_ffn_c_bv': (0.0, 2.0),
     'L0_ffn_c_bo': (0.0, 2.0),
     'L0_ffn_e_ln_g': (1.0, 0.6),
     'L0_ffn_e_ln_b': (0.0, 0.8),
     'L0_ffn_e_b1': (0.0, 0.8),
     'L0_ffn_e_bg': (0.0, 0.8),
     'L0_ffn_e_b2': (0.0, 0.8)}
    factors = {'L0_xattn_Wq': 5.752,
     'L0_ffn_slot_query': 8.0,
     'L0_ffn_d_Wq': 8.0,
     'L0_ffn_d_Wk': 8.0,
     'L0_ffn_d_Wv': 8.0,
     'L0_ffn_d_Wo': 5.354,
     'L0_ffn_c_Wq': 8.0,
     'L0_ffn_c_Wk': 8.0,
     'L0_ffn_e_W1': 8.0,
     'L0_ffn_e_Wg': 8.0,
     'L0_ffn_e_W2': 8.0}
    for name, (base, spread) in spreads.items():
        noise = np.random.default_rng([zlib.crc32(name.encode()), seed]).standard_normal(out[name].shape)
        drawn = base * np.exp(spread * noise) if base else spread * noise
        out[name] = jnp.asarray(drawn.astype(out[name].dtype))
    for name, factor in factors.items():
        out[name] = (out[name] * factor).astype(out[name].dtype)
    return out
```

```python
import concourse.bass as bass
from concourse import mybir
from contextlib import ExitStack

F32 = mybir.dt.float32
F32R = mybir.dt.float32r
I32 = mybir.dt.int32
ALU = mybir.AluOpType
ACT = mybir.ActivationFunctionType
AX = mybir.AxisListType

P = 128
B, S, D = 8, 512, 512
KT = D // P
TT = S // P
H, DH = 16, 64
HP = H // 2
FF = 2048
NS, E = 16, 16
SH, SD = 16, 32
HS = SH * NS
EPS = 1e-5
MASKED = -1e30
LOWEST = -3e38


def plain(ap):
    return ap.bitcast(F32)


def products(hi_lo_w, hi_lo_m):
    (w_hi, w_lo), (m_hi, m_lo) = hi_lo_w, hi_lo_m
    return ((w_hi, m_hi), (w_hi, m_lo), (w_lo, m_hi))


class Memory:

    def __init__(self, nc, stage, whole):
        self.nc, self.stage, self.whole = nc, stage, whole

    def sbuf(self, name, shape, dtype=F32):
        return self.stage.enter_context(self.nc.sbuf_tensor(name, shape, dtype))

    def bank(self, name):
        return self.stage.enter_context(self.nc.psum_tensor(name, [P, 512], F32))

    def sem(self, name):
        return self.whole.enter_context(self.nc.semaphore(name))


def rows_mean_var(nc, stats, mean, var, half):
    col = lambda i: stats[:, :, i:i + 1].rearrange("p n o -> p (n o)")
    v = nc.vector
    v.tensor_tensor(half, col(1), col(4), ALU.subtract)
    v.tensor_tensor(mean, col(1), col(4), ALU.add)
    v.tensor_tensor(var, col(2), col(5), ALU.add)
    v.drain()
    v.tensor_scalar(mean, mean, 0.5, None, ALU.mult)
    v.tensor_scalar(half, half, 0.5, None, ALU.mult)
    v.tensor_scalar(var, var, 1.0 / D, None, ALU.mult)
    v.drain()
    v.tensor_tensor(half, half, half, ALU.mult)
    v.drain()
    v.tensor_tensor(var, var, half, ALU.add)
    v.drain()


def cross_attention(nc, whole, I, ident, ones, gates, x1_d, xnT_d):
    with ExitStack() as stage:
        mem = Memory(nc, stage, whole)
        x_v = I["x"].rearrange("b (t p) d -> b p t d", p=P)
        c_v = I["ctx_1024"].rearrange("b (t p) d -> b p t d", p=P)
        x1_v = x1_d.rearrange("b (t p) d -> b p t d", p=P)
        mask = I["mask_BxS2_ik0"]

        wq_hi = mem.sbuf("wq_hi", [P, KT, H * DH], F32R)
        wq_lo = mem.sbuf("wq_lo", [P, KT, H * DH], F32R)
        wkv_hi = mem.sbuf("wkv_hi", [P, KT, 4 * DH], F32R)
        wkv_lo = mem.sbuf("wkv_lo", [P, KT, 4 * DH], F32R)
        wo_hi = mem.sbuf("wo_hi", [P, HP, D], F32R)
        wo_lo = mem.sbuf("wo_lo", [P, HP, D], F32R)
        gam = mem.sbuf("gam", [P, 2, KT])
        sel_max = mem.sbuf("sel_max", [P, H, P], F32R)
        sel_sum = mem.sbuf("sel_sum", [P, 2 * P - 1], F32R)
        sel_pair = mem.sbuf("sel_pair", [P, HP, P], F32R)
        key_bias = mem.sbuf("key_bias", [P, B * TT])
        block_bias = mem.sbuf("block_bias", [P, TT])
        live = mem.sbuf("live", [1, B * TT], I32)
        live_f = mem.sbuf("live_f", [1, B * TT])
        mean = mem.sbuf("mean", [P, B * 2 * TT])
        var = mem.sbuf("var", [P, B * 2 * TT])
        rstd = mem.sbuf("rstd", [P, B * 2 * TT])
        spread = mem.sbuf("spread", [P, B * 2 * TT])
        rstd2 = mem.sbuf("rstd2", [P, B * TT])
        cin = mem.sbuf("cin", [P, TT, D])
        xin = mem.sbuf("xin", [P, TT, D])
        nT_hi = mem.sbuf("nT_hi", [P, KT, S], F32R)
        nT_lo = mem.sbuf("nT_lo", [P, KT, S], F32R)
        kk_hi = mem.sbuf("kk_hi", [P, S], F32R)
        kk_lo = mem.sbuf("kk_lo", [P, S], F32R)
        vT = mem.sbuf("vT", [P, S])
        val = mem.sbuf("val", [P, TT, 4, P], F32R)
        qs = mem.sbuf("qs", [P, H, S], F32R)
        oT_hi, oT_lo = qs[:, 0:HP, :], qs[:, HP:H, :]
        mask_b = mem.sbuf("mask_b", [P, S])
        mask_i = mask_b[:, :].bitcast(I32)
        m_rows = mem.sbuf("m_rows", [P, TT, H])
        m_heads = mem.sbuf("m_heads", [P, S], F32R)
        prob = mem.sbuf("prob", [P, 2, S])
        prob_hi = mem.sbuf("prob_hi", [P, 2, S], F32R)
        prob_lo = mem.sbuf("prob_lo", [P, 2, S], F32R)
        acc = mem.sbuf("acc", [P, HP, S])
        acc_sum = mem.sbuf("acc_sum", [P, S])
        inv_hi = mem.sbuf("inv_hi", [P, S], F32R)
        inv_lo = mem.sbuf("inv_lo", [P, S], F32R)
        xres = mem.sbuf("xres", [P, 2, D])
        mask_rows, bias_rows = acc_sum[0:B * TT, 0:P].bitcast(I32), vT[0:B * TT, 0:P]
        stats = prob[:, 1, 0:B * 2 * TT * 6].rearrange("p (n s) -> p n s", s=6)
        raw = [t[:, 2 * i:2 * i + 2, :].rearrange("p t d -> p (t d)") for t in (cin, xin) for i in range(2)]
        RAW = len(raw)

        G = [mem.bank(f"att_general{i}") for i in range(2)]
        SC = [mem.bank(f"att_scores{i}") for i in range(2)]
        OB = [mem.bank(f"att_out{i}") for i in range(2)]
        SUM = mem.bank("att_sum")

        raw_in = [mem.sem(f"raw_in{i}") for i in range(RAW)]
        w_hi_done, w_lo_done = mem.sem("w_hi_done"), mem.sem("w_lo_done")
        small_in, mask_in, masks_ready, masks_turned = (mem.sem(n) for n in ("small_in", "mask_in", "masks_ready", "masks_turned"))
        ident_zero, ident_ready = mem.sem("ident_zero"), mem.sem("ident_ready")
        rows_in, rows_seen = mem.sem("rows_in"), mem.sem("rows_seen")
        var_ready, sd_ready = mem.sem("var_ready"), mem.sem("sd_ready")

        wkv_v = I["L0_xattn_Wkv"].rearrange("(k p) n -> p k n", p=P)
        wo_v = I["L0_xattn_Wout"].rearrange("(i p) n -> p i n", p=P)
        chunks = [(wq_hi[:, k, :], wq_lo[:, k, :]) for k in range(KT)]
        chunks.append((wkv_hi[:, :, :].rearrange("p k n -> p (k n)"), wkv_lo[:, :, :].rearrange("p k n -> p (k n)")))
        chunks += [(wo_hi[:, 2 * i:2 * i + 2, :].rearrange("p i n -> p (i n)"),
                    wo_lo[:, 2 * i:2 * i + 2, :].rearrange("p i n -> p (i n)")) for i in range(HP // 2)]
        arrivals, landed = [0] * RAW, []
        for c in range(len(chunks)):
            arrivals[c % RAW] += 64 if c == KT else 16
            landed.append(arrivals[c % RAW])

        with nc.Block() as block:
            @block.sync
            def _(sp):
                sp.dma_start(gates[:, 0:1], I["g_xattn"].unsqueeze(0).to_broadcast([P, 1])).then_inc(small_in, 16)
                sp.dma_start(gates[:, 1:2], I["g_ffn"].unsqueeze(0).to_broadcast([P, 1])).then_inc(small_in, 16)
                sp.dma_start(gam[:, 0, :], I["L0_xattn_gamma"].rearrange("(k p) -> p k", p=P), allow_slow_non_contiguous=True).then_inc(small_in, 16)
                sp.dma_start(gam[:, 1, :], I["L0_xattn_ctx_gamma"].rearrange("(k p) -> p k", p=P), allow_slow_non_contiguous=True).then_inc(small_in, 16)
                sp.dma_start(mask_rows, mask.rearrange("b (j p) -> (b j) p", p=P)).then_inc(mask_in, 16)
                sp.dma_start(acc[0:1, :, :].bitcast(I32).rearrange("o i s -> o (i s)"),
                             mask.rearrange("b s -> (b s)").unsqueeze(0)).then_inc(mask_in, 16)
                for c in range(len(chunks)):
                    if c >= RAW:
                        sp.wait_ge(w_lo_done, c - RAW + 1)
                    slot = raw[c % RAW]
                    if c < KT:
                        sp.dma_start(slot, I["L0_xattn_Wq"][c * P:(c + 1) * P, :]).then_inc(raw_in[c % RAW], 16)
                    elif c == KT:
                        four = slot.rearrange("p (k n) -> p k n", k=KT)
                        for n in range(4):
                            sp.dma_start(four[:, :, n * DH:(n + 1) * DH],
                                         wkv_v[:, :, (n // 2) * DH:(n // 2 + 1) * DH]).then_inc(raw_in[c % RAW], 16)
                    else:
                        i = 2 * (c - KT - 1)
                        sp.dma_start(slot.rearrange("p (i n) -> p i n", i=2), wo_v[:, i:i + 2, :]).then_inc(raw_in[c % RAW], 16)
                sp.wait_ge(w_lo_done, len(chunks))
                with sp.Fori(0, B) as b:
                    sp.wait_ge(rows_seen, b)
                    sp.dma_start(cin[:, :, :], c_v[bass.ds(b, 1)].rearrange("o p t d -> (o p) t d")).then_inc(rows_in, 16)
                    sp.dma_start(xin[:, :, :], x_v[bass.ds(b, 1)].rearrange("o p t d -> (o p) t d")).then_inc(rows_in, 16)

            @block.gpsimd
            def _(pool):
                nc.gpsimd.memset(ident[:, :], 0.0).then_inc(ident_zero, 1)
                pool.wait_ge(ident_zero, 1)
                nc.gpsimd.affine_select(out=ident[:, :], in_=ident[:, :], compare_op=ALU.not_equal, fill=1.0,
                                        base=0, pattern=[[-1, P]], channel_multiplier=1).then_inc(ident_ready, 1)

            @block.scalar
            def _(act):
                for c, (hi, _) in enumerate(chunks):
                    act.wait_ge(raw_in[c % RAW], landed[c])
                    nc.scalar.copy(hi, raw[c % RAW]).then_inc(w_hi_done, 1)
                act.wait_ge(small_in, 64)
                nc.scalar.activation(gates[:, :], gates[:, :], ACT.Tanh)
                for half in range(2):
                    act.wait_ge(var_ready, half + 1)
                    n = B * 2 * TT if half == 0 else B * TT
                    nc.scalar.activation(spread[:, 0:n], spread[:, 0:n], ACT.Sqrt).then_inc(sd_ready, 1)

            @block.vector
            def _(dve):
                for c, (hi, lo) in enumerate(chunks):
                    dve.wait_ge(w_hi_done, c + 1)
                    nc.vector.tensor_tensor(lo, raw[c % RAW], plain(hi), ALU.subtract).then_inc(w_lo_done, 1)
                dve.wait_ge(mask_in, 32)
                nc.vector.tensor_scalar(bias_rows, mask_rows, 0.0, MASKED, ALU.is_equal, ALU.mult).then_inc(masks_ready, 1)
                flat = acc[0:1, :, :].rearrange("o i s -> o (i s)")
                nc.vector.tensor_scalar(flat, flat.bitcast(I32), 0.0, None, ALU.not_equal)
                nc.vector.drain()
                nc.vector.tensor_reduce(live_f[:, :], flat.rearrange("o (n p) -> o n p", p=P), AX.X, ALU.max)
                nc.vector.drain()
                nc.vector.tensor_copy(live[:, :], live_f[:, :])
                dve.wait_ge(ident_ready, 1)
                nc.vector.memset(ones[:, :], 1.0)
                nc.vector.memset(plain(m_heads[:, :]), 0.0)
                nc.vector.memset(plain(inv_hi[:, :]), 0.0)
                nc.vector.memset(plain(inv_lo[:, :]), 0.0)
                nc.vector.memset(plain(val[:, :, :, :]), 0.0)
                nc.vector.memset(plain(sel_sum[:, :]), 0.0)
                nc.vector.memset(prob[:, 0, 0:P], 0.0)
                nc.vector.drain()
                nc.vector.memset(plain(sel_sum[:, P - 1:P]), 1.0)
                zeros = prob[:, 0, 0:P]
                for h in range(H):
                    nc.vector.tensor_scalar(sel_max[:, h, :], zeros, ident[:, h:h + 1], -1.0, ALU.add, ALU.mult)
                    nc.vector.tensor_scalar(sel_pair[:, h // 2, (h % 2) * DH:(h % 2 + 1) * DH], zeros[:, 0:DH],
                                            ident[:, h:h + 1], None, ALU.add)
                with dve.Fori(0, B) as b:
                    dve.wait_ge(rows_in, b * 32 + 32)
                    for c, src in enumerate((cin, xin)):
                        for t in range(TT):
                            to = stats[:, bass.ds(b * (2 * TT) + (c * TT + t), 1), :].rearrange("p o n -> p (o n)")
                            last = nc.vector.bn_stats(to, src[:, t, :])
                    last.then_inc(rows_seen, 1)
                nc.vector.drain()
                rows_mean_var(nc, stats, mean[:, :], var[:, :], spread[:, :])
                nc.vector.tensor_scalar(spread[:, :], var[:, :], EPS, None, ALU.add).then_inc(var_ready, 1)
                dve.wait_ge(sd_ready, 1)
                nc.vector.reciprocal(rstd[:, :], spread[:, :])
                nc.vector.drain()
                x_of = lambda a: a.rearrange("p (b c t) -> p b c t", c=2, t=TT)[:, :, 1, :]
                half = spread[:, 0:B * TT].rearrange("p (b t) -> p b t", t=TT)
                r2 = rstd2[:, :].rearrange("p (b t) -> p b t", t=TT)
                nc.vector.tensor_tensor(r2, x_of(var[:, :]), x_of(rstd[:, :]), ALU.mult)
                nc.vector.drain()
                nc.vector.tensor_tensor(half, r2, x_of(rstd[:, :]), ALU.mult)
                nc.vector.drain()
                nc.vector.tensor_scalar(half, half, EPS, None, ALU.add).then_inc(var_ready, 1)
                dve.wait_ge(sd_ready, 2)
                nc.vector.reciprocal(r2, half)
                nc.vector.drain()
                nc.vector.tensor_tensor(x_of(rstd[:, :]), x_of(rstd[:, :]), r2, ALU.mult)
                dve.wait_ge(masks_turned, 1)
                nc.vector.tensor_copy(key_bias[:, :], G[0][:, 0:B * TT])

            @block.tensor
            def _(pe):
                pe.wait_ge(masks_ready, 1)
                pe.wait_ge(ident_ready, 1)
                nc.tensor.transpose(G[0][:, 0:B * TT], bias_rows, ident[0:B * TT, 0:B * TT]).then_inc(masks_turned, 1)

        ctx_in, x_in, mask_b_in = (mem.sem(n) for n in ("ctx_in", "x_in", "mask_b_in"))
        xres_in = [mem.sem(f"xres_in{i}") for i in range(2)]
        x1_out = [mem.sem(f"x1_out{i}") for i in range(2)]
        xnT_out = mem.sem("xnT_out")
        normed = mem.sem("normed")
        g_ready, g_free = mem.sem("g_ready"), mem.sem("g_free")
        g_hi = mem.sem("g_hi")
        max_scores, max_taken, m_ready = mem.sem("max_scores"), mem.sem("max_taken"), mem.sem("m_ready")
        max_begun = mem.sem("max_begun")
        scores, exps, low_probs, head_out, out_taken = (
            mem.sem(n) for n in ("scores", "exps", "low_probs", "head_out", "out_taken"))
        acc_clear, inv_ready, o_hi_done, o_lo_done = (
            mem.sem(n) for n in ("acc_clear", "inv_ready", "o_hi_done", "o_lo_done"))

        U_CTX, U_K, U_V, U_VAL, U_X = 0, KT, KT + 1, KT + 2, KT + 3
        U_SPREAD = U_X + KT
        U_OUT = U_SPREAD + HP
        U_Q = U_OUT + TT
        U_MAX = U_Q + HP
        PER = U_MAX + 1
        assert PER % 2 == 0
        HI_CTX, HI_K, HI_VAL, HI_X, HI_Q = 0, KT, KT + 1, KT + 3, 2 * KT + 3
        HI = HI_Q + 2 * HP
        OUTS = HP + 1
        q_scale = DH ** -0.5

        def of(ap, b):
            return ap[b] if isinstance(b, int) else ap[bass.ds(b, 1)].rearrange("o p t d -> (o p) t d")

        def first(b):
            return isinstance(b, int) and b == 0

        with nc.Block() as block:
            @block.sync
            def _(sp):
                def rows(b, nxt):
                    sp.wait_ge(g_ready, b * PER + U_K)
                    sp.dma_start(cin[:, :, :], of(c_v, nxt)).then_inc(ctx_in, 16)
                    sp.wait_ge(g_ready, b * PER + U_SPREAD)
                    sp.dma_start(xin[:, :, :], of(x_v, nxt)).then_inc(x_in, 16)
                    sp.wait_ge(max_taken, (b + 1) * (TT * H))
                    src = mask[nxt:nxt + 1, :] if isinstance(nxt, int) else mask[bass.ds(nxt, 1), :]
                    sp.dma_start(mask_i, src.to_broadcast([P, S])).then_inc(mask_b_in, 16)

                def keep_xnT(b):
                    sp.wait_ge(g_free, b * PER + U_SPREAD)
                    for part, t in enumerate((nT_hi, nT_lo)):
                        sp.dma_start(of(xnT_d[part], b), plain(t[:, :, :])).then_inc(xnT_out, 16)

                def residual(b, prev, t):
                    sp.wait_ge(x1_out[t % 2], ((b - 1) * (TT // 2) + t // 2) * 16)
                    sp.dma_start(xres[:, t % 2, :], of(x_v, prev)[:, t, :]).then_inc(xres_in[t % 2], 16)

                def store(b, prev, t):
                    sp.wait_ge(g_free, b * PER + U_OUT + t + 1)
                    sp.dma_start(of(x1_v, prev)[:, t, :], xres[:, t % 2, :]).then_inc(x1_out[t % 2], 16)

                def tail(b, prev):
                    for t in range(TT):
                        store(b, prev, t)
                        if t + 2 < TT:
                            residual(b, prev, t + 2)

                sp.dma_start(cin[:, :, :], c_v[0]).then_inc(ctx_in, 16)
                sp.dma_start(xin[:, :, :], x_v[0]).then_inc(x_in, 16)
                sp.dma_start(mask_i, mask[0:1, :].to_broadcast([P, S])).then_inc(mask_b_in, 16)
                keep_xnT(0)
                rows(0, 1)
                with sp.Fori(1, B - 1) as b:
                    residual(b, b - 1, 0)
                    residual(b, b - 1, 1)
                    keep_xnT(b)
                    tail(b, b - 1)
                    rows(b, b + 1)
                residual(B - 1, B - 2, 0)
                residual(B - 1, B - 2, 1)
                keep_xnT(B - 1)
                tail(B - 1, B - 2)
                residual(B, B - 1, 0)
                residual(B, B - 1, 1)
                tail(B, B - 1)
                for i in range(2):
                    sp.wait_ge(x1_out[i], B * (TT // 2) * 16)
                sp.wait_ge(xnT_out, B * 32)

            @block.tensor
            def _(pe):
                def claim(b, u):
                    if not (first(b) and u < 2):
                        pe.wait_ge(g_free, b * PER + u - 1)
                    return G[u % 2]

                def turn(b, u, src):
                    for k in range(KT):
                        bank = claim(b, u + k)
                        for t in range(TT):
                            last = nc.tensor.transpose(bank[:, t * P:(t + 1) * P], src[:, t, k * P:(k + 1) * P], ident[:, :])
                        last.then_inc(g_ready, 1)

                def project(bank, cols, w_hi, w_lo):
                    n = 0
                    for k in range(KT):
                        for w, m in products((w_hi, w_lo), (nT_hi, nT_lo)):
                            last = nc.tensor.matmul(bank[:, :], w[:, k, cols], m[:, k, :], start=n == 0, stop=n == 3 * KT - 1)
                            n += 1
                    return last

                def part1(b):
                    pe.wait_ge(normed, 2 * b + 1)
                    turn(b, U_CTX, cin)
                    pe.wait_ge(g_free, b * PER + U_K)
                    for u, c in ((U_K, 0), (U_V, 2 * DH)):
                        project(claim(b, u), slice(c, c + 2 * DH), wkv_hi, wkv_lo).then_inc(g_ready, 1)
                    pe.wait_ge(g_free, b * PER + U_VAL)
                    bank = claim(b, U_VAL)
                    for j in range(TT):
                        last = nc.tensor.transpose(bank[:, j * P:(j + 1) * P], vT[:, j * P:(j + 1) * P], ident[:, :])
                    last.then_inc(g_ready, 1)
                    pe.wait_ge(normed, 2 * b + 2)
                    turn(b, U_X, xin)

                def tail(b):
                    pe.wait_ge(inv_ready, b)
                    for i in range(HP):
                        bank = claim(b, U_SPREAD + i)
                        nc.tensor.matmul(bank[:, :], sel_pair[:, i, :], inv_hi[:, :], start=True, stop=False)
                        nc.tensor.matmul(bank[:, :], sel_pair[:, i, :], inv_lo[:, :], start=False, stop=True).then_inc(g_ready, 1)
                    pe.wait_ge(o_lo_done, b * HP)
                    for t in range(TT):
                        bank = claim(b, U_OUT + t)
                        n = 0
                        for i in range(HP):
                            for o, w in products((oT_hi, oT_lo), (wo_hi, wo_lo)):
                                last = nc.tensor.matmul(bank[:, :], o[:, i, t * P:(t + 1) * P], w[:, i, :],
                                                        start=n == 0, stop=n == 3 * HP - 1)
                                n += 1
                        last.then_inc(g_ready, 1)

                def part2(b, on):
                    for i in range(HP):
                        project(claim(b, U_Q + i), slice(i * P, (i + 1) * P), wq_hi, wq_lo).then_inc(g_ready, 1)
                    pe.wait_ge(g_free, b * PER + U_MAX)
                    pe.wait_ge(exps, b * (TT * H))
                    for j in range(TT):
                        n = b * TT + j
                        with pe.If(on[j] == 1):
                            for h in range(H):
                                pe.wait_ge(max_taken, n * H + max(h - 1, 0))
                                for t in range(TT):
                                    last = nc.tensor.matmul(SC[h % 2][:, t * P:(t + 1) * P], qs[:, h, t * P:(t + 1) * P],
                                                            kk_hi[:, j * P:(j + 1) * P], start=True, stop=True)
                                last.then_inc(max_scores, 1)
                        with pe.Else():
                            pe.drain().then_inc(max_scores, H)
                    pe.wait_ge(m_ready, b + 1)
                    bank = claim(b, U_MAX)
                    for t in range(TT):
                        last = nc.tensor.transpose(bank[0:H, t * P:(t + 1) * P], m_rows[:, t, :], ident[:, :])
                    last.then_inc(g_ready, 1)

                def attend(b, on):
                    pe.wait_ge(g_free, (b + 1) * PER)
                    pe.wait_ge(max_taken, (b + 1) * (TT * H))
                    for j in range(TT):
                        n = b * TT + j
                        keys = slice(j * P, (j + 1) * P)
                        with pe.If(on[j] == 1):
                            for h in range(H + 1):
                                if h < H:
                                    pe.wait_ge(exps, n * H + max(h - 1, 0))
                                    bank = SC[h % 2]
                                    nc.tensor.matmul(bank[:, :], kk_hi[:, keys], qs[:, h, :], start=True, stop=False)
                                    nc.tensor.matmul(bank[:, :], kk_lo[:, keys], qs[:, h, :], start=False, stop=False)
                                    nc.tensor.matmul(bank[:, :], sel_max[:, h, :], m_heads[:, :], start=False, stop=True).then_inc(scores, 1)
                                if h >= 1:
                                    g = h - 1
                                    i, odd, s = g // 2, g % 2, g % 2
                                    pe.wait_ge(low_probs, n * H + g + 1)
                                    if odd == 0:
                                        pe.wait_ge(out_taken, n * OUTS + max(i - 1, 0))
                                    v_hi, v_lo = val[:, j, odd, :], val[:, j, 2 + odd, :]
                                    nc.tensor.matmul(OB[i % 2][:, :], v_hi, prob_hi[:, s, :], start=not odd, stop=False)
                                    nc.tensor.matmul(OB[i % 2][:, :], v_hi, prob_lo[:, s, :], start=False, stop=False)
                                    nc.tensor.matmul(OB[i % 2][:, :], v_lo, prob_hi[:, s, :], start=False, stop=bool(odd))
                                    one = sel_sum[:, P - 1 - g:2 * P - 1 - g]
                                    nc.tensor.matmul(SUM[:, :], one, prob_hi[:, s, :], start=g == 0, stop=False)
                                    nc.tensor.matmul(SUM[:, :], one, prob_lo[:, s, :], start=False, stop=g == H - 1).then_inc(head_out, 1)
                        with pe.Else():
                            pe.drain().then_inc(scores, H)
                            pe.drain().then_inc(head_out, H)

                def flags(b):
                    return [pe.value_load(live[0:1, bass.ds(b * TT + j, 1)]) for j in range(TT)]

                part1(0)
                pe.drain().then_inc(g_ready, U_Q - U_SPREAD)
                on = flags(0)
                part2(0, on)
                attend(0, on)
                with pe.Fori(1, B) as b:
                    part1(b)
                    tail(b)
                    on = flags(b)
                    part2(b, on)
                    attend(b, on)
                pe.drain().then_inc(g_ready, U_SPREAD)
                tail(B)

            @block.scalar
            def _(act):
                def part1(b):
                    if not first(b):
                        act.wait_ge(xnT_out, b * 32)
                    for k in range(KT):
                        act.wait_ge(g_ready, b * PER + U_CTX + k + 1)
                        nc.scalar.activation(nT_hi[:, k, :], G[(U_CTX + k) % 2][:, :], ACT.Copy, scale=gam[:, 1, k:k + 1]).then_inc(g_hi, 1)
                    act.wait_ge(g_ready, b * PER + U_K + 1)
                    nc.scalar.copy(kk_hi[:, :], G[U_K % 2][:, :]).then_inc(g_hi, 1)
                    act.wait_ge(g_ready, b * PER + U_VAL + 1)
                    turned = G[U_VAL % 2][:, :].rearrange("p (j v) -> p j v", j=TT)
                    for odd in range(2):
                        cols = slice(odd * DH, (odd + 1) * DH)
                        nc.scalar.copy(val[:, :, odd, cols], turned[:, :, cols]).then_inc(g_hi, 1)
                    for k in range(KT):
                        act.wait_ge(g_ready, b * PER + U_X + k + 1)
                        nc.scalar.activation(nT_hi[:, k, :], G[(U_X + k) % 2][:, :], ACT.Copy, scale=gam[:, 0, k:k + 1]).then_inc(g_hi, 1)

                def tail(b):
                    for i in range(HP):
                        act.wait_ge(g_free, b * PER + U_SPREAD + i + 1)
                        nc.scalar.copy(oT_hi[:, i, :], acc[:, i, :]).then_inc(o_hi_done, 1)

                def part2(b):
                    for i in range(HP):
                        act.wait_ge(g_ready, b * PER + U_Q + i + 1)
                        for odd in range(2):
                            half = slice(odd * DH, (odd + 1) * DH)
                            nc.scalar.activation(qs[half, 2 * i + odd, :], G[(U_Q + i) % 2][half, :], ACT.Copy, scale=q_scale).then_inc(g_hi, 1)

                def attend(b, on):
                    for j in range(TT):
                        n = b * TT + j
                        with act.If(on[j] == 1):
                            bias = block_bias[:, j:j + 1]
                            nc.scalar.copy(bias, key_bias[:, bass.ds(n, 1)])
                            act.drain()
                            for h in range(H):
                                act.wait_ge(scores, n * H + h + 1)
                                act.wait_ge(head_out, n * H + max(h - 1, 0))
                                nc.scalar.activation(prob[:, h % 2, :], SC[h % 2][:, :], ACT.Exp, bias=bias)
                                nc.scalar.activation(prob_hi[:, h % 2, :], SC[h % 2][:, :], ACT.Exp, bias=bias).then_inc(exps, 1)
                        with act.Else():
                            act.drain().then_inc(exps, H)

                def flags(b):
                    return [act.value_load(live[0:1, bass.ds(b * TT + j, 1)]) for j in range(TT)]

                part1(0)
                part2(0)
                attend(0, flags(0))
                with act.Fori(1, B) as b:
                    part1(b)
                    tail(b)
                    part2(b)
                    attend(b, flags(b))
                tail(B)

            @block.gpsimd
            def _(pool):
                def clear():
                    nc.gpsimd.memset(acc[:, :, :], 0.0).then_inc(acc_clear, 1)

                def tail(b):
                    for i in range(HP):
                        pool.wait_ge(o_hi_done, (b - 1) * HP + i + 1)
                        nc.gpsimd.tensor_tensor(oT_lo[:, i, :], acc[:, i, :], plain(oT_hi[:, i, :]), ALU.subtract).then_inc(o_lo_done, 1)

                def attend(b, on):
                    for j in range(TT):
                        n = b * TT + j
                        with pool.If(on[j] == 1):
                            for h in range(H):
                                pool.wait_ge(exps, n * H + h + 1)
                                nc.gpsimd.tensor_tensor(prob_lo[:, h % 2, :], prob[:, h % 2, :], plain(prob_hi[:, h % 2, :]),
                                                        ALU.subtract).then_inc(low_probs, 1)
                        with pool.Else():
                            pool.drain().then_inc(low_probs, H)

                def flags(b):
                    return [pool.value_load(live[0:1, bass.ds(b * TT + j, 1)]) for j in range(TT)]

                clear()
                attend(0, flags(0))
                with pool.Fori(1, B) as b:
                    tail(b)
                    pool.drain()
                    clear()
                    attend(b, flags(b))
                tail(B)

            @block.vector
            def _(dve):
                def norm(b, src, arrived, c):
                    dve.wait_ge(arrived, b * 16 + 16)
                    for t in range(TT):
                        n = b * (2 * TT) + c * TT + t
                        last = nc.vector.tensor_scalar(src[:, t, :], src[:, t, :], mean[:, bass.ds(n, 1)], rstd[:, bass.ds(n, 1)], ALU.subtract, ALU.mult)
                    last.then_inc(normed, 1)

                def part1(b):
                    for k in range(KT):
                        dve.wait_ge(g_hi, b * HI + HI_CTX + k + 1)
                        nc.vector.scalar_tensor_tensor(nT_lo[:, k, :], G[(U_CTX + k) % 2][:, :], gam[:, 1, k:k + 1],
                                                       plain(nT_hi[:, k, :]), ALU.mult, ALU.subtract).then_inc(g_free, 1)
                    dve.wait_ge(g_hi, b * HI + HI_K + 1)
                    nc.vector.tensor_tensor(kk_lo[:, :], G[U_K % 2][:, :], plain(kk_hi[:, :]), ALU.subtract).then_inc(g_free, 1)
                    dve.wait_ge(g_ready, b * PER + U_V + 1)
                    nc.vector.tensor_copy(vT[:, :], G[U_V % 2][:, :]).then_inc(g_free, 1)
                    dve.wait_ge(g_hi, b * HI + HI_VAL + 2)
                    turned = G[U_VAL % 2][:, :].rearrange("p (j v) -> p j v", j=TT)
                    for odd in range(2):
                        cols = slice(odd * DH, (odd + 1) * DH)
                        last = nc.vector.tensor_tensor(val[:, :, 2 + odd, cols], turned[:, :, cols], plain(val[:, :, odd, cols]), ALU.subtract)
                    last.then_inc(g_free, 1)
                    for k in range(KT):
                        dve.wait_ge(g_hi, b * HI + HI_X + k + 1)
                        nc.vector.scalar_tensor_tensor(nT_lo[:, k, :], G[(U_X + k) % 2][:, :], gam[:, 0, k:k + 1],
                                                       plain(nT_hi[:, k, :]), ALU.mult, ALU.subtract).then_inc(g_free, 1)

                def tail(b):
                    for i in range(HP):
                        dve.wait_ge(g_ready, b * PER + U_SPREAD + i + 1)
                        nc.vector.tensor_tensor(acc[:, i, :], acc[:, i, :], G[(U_SPREAD + i) % 2][:, :], ALU.mult).then_inc(g_free, 1)
                    for t in range(TT):
                        dve.wait_ge(g_ready, b * PER + U_OUT + t + 1)
                        dve.wait_ge(xres_in[t % 2], ((b - 1) * (TT // 2) + t // 2 + 1) * 16)
                        nc.vector.scalar_tensor_tensor(xres[:, t % 2, :], G[(U_OUT + t) % 2][:, :], gates[:, 0:1], xres[:, t % 2, :],
                                                       ALU.mult, ALU.add).then_inc(g_free, 1)

                def part2(b, on):
                    for i in range(HP):
                        dve.wait_ge(g_hi, b * HI + HI_Q + 2 * i + 2)
                        bank = G[(U_Q + i) % 2]
                        for odd in range(2):
                            here, there = slice(odd * DH, (odd + 1) * DH), slice((1 - odd) * DH, (2 - odd) * DH)
                            last = nc.vector.scalar_tensor_tensor(qs[there, 2 * i + odd, :], bank[here, :], q_scale,
                                                                  plain(qs[here, 2 * i + odd, :]), ALU.mult, ALU.subtract)
                        last.then_inc(g_free, 1)
                    dve.wait_ge(mask_b_in, b * 16 + 16)
                    nc.vector.tensor_scalar(mask_b[:, :], mask_i, 0.0, MASKED, ALU.is_equal, ALU.mult)
                    nc.vector.memset(m_rows[:, :, :], LOWEST)
                    nc.vector.drain()
                    for j in range(TT):
                        n = b * TT + j
                        with dve.If(on[j] == 1):
                            for h in range(H):
                                dve.wait_ge(max_scores, n * H + h + 1)
                                dve.sem_inc(max_begun, 1)
                                for t in range(TT):
                                    here = SC[h % 2][:, t * P:(t + 1) * P]
                                    m = m_rows[:, t, h:h + 1]
                                    last = nc.vector.tensor_tensor_reduce(here, here, mask_b[:, j * P:(j + 1) * P], 1.0, m,
                                                                          ALU.add, ALU.max, m)
                                last.then_inc(max_taken, 1)
                            nc.vector.drain()
                        with dve.Else():
                            nc.vector.drain().then_inc(max_taken, H)
                    nc.vector.drain().then_inc(m_ready, 1)
                    dve.wait_ge(g_ready, (b + 1) * PER)
                    nc.vector.tensor_copy(m_heads[0:H, :], G[U_MAX % 2][0:H, :]).then_inc(g_free, 1)

                def attend(b, on):
                    dve.wait_ge(acc_clear, b + 1)
                    nc.vector.memset(acc_sum[0:H, :], 0.0)
                    nc.vector.drain()
                    for j in range(TT):
                        n = b * TT + j
                        with dve.If(on[j] == 1):
                            for i in range(HP):
                                dve.wait_ge(head_out, n * H + 2 * i + 2)
                                nc.vector.tensor_tensor(acc[:, i, :], acc[:, i, :], OB[i % 2][:, :], ALU.add).then_inc(out_taken, 1)
                            nc.vector.tensor_tensor(acc_sum[0:H, :], acc_sum[0:H, :], SUM[0:H, :], ALU.add).then_inc(out_taken, 1)
                            nc.vector.drain()
                        with dve.Else():
                            nc.vector.drain().then_inc(out_taken, OUTS)
                    nc.vector.reciprocal(acc_sum[0:H, :], acc_sum[0:H, :])
                    nc.vector.drain()
                    nc.vector.tensor_copy(inv_hi[0:H, :], acc_sum[0:H, :])
                    nc.vector.drain()
                    nc.vector.tensor_tensor(inv_lo[0:H, :], acc_sum[0:H, :], plain(inv_hi[0:H, :]), ALU.subtract).then_inc(inv_ready, 1)
                    nc.vector.drain()

                def flags(b):
                    return [dve.value_load(live[0:1, bass.ds(b * TT + j, 1)]) for j in range(TT)]

                def rows(b):
                    norm(b, cin, ctx_in, 0)
                    norm(b, xin, x_in, 1)

                rows(0)
                part1(0)
                nc.vector.drain().then_inc(g_free, U_Q - U_SPREAD)
                on = flags(0)
                part2(0, on)
                rows(1)
                attend(0, on)
                with dve.Fori(1, B - 1) as b:
                    part1(b)
                    tail(b)
                    on = flags(b)
                    part2(b, on)
                    rows(b + 1)
                    attend(b, on)
                part1(B - 1)
                tail(B - 1)
                on = flags(B - 1)
                part2(B - 1, on)
                attend(B - 1, on)
                nc.vector.drain().then_inc(g_free, U_SPREAD)
                tail(B)


def feed_forward(nc, whole, I, gates, x_stats, x1_d, xnT_d):
    with ExitStack() as stage:
        mem = Memory(nc, stage, whole)
        x_v = x1_d.rearrange("b (t p) d -> b p t d", p=P)
        Q = 4
        FT = FF // P // Q
        FQ = FT * P
        w1_v = I["L0_xattn_Wff1"].rearrange("(k p) (g q n) -> k q g p n", p=P, g=2, q=Q)
        w2_v = I["L0_xattn_Wff2"].rearrange("(q f p) n -> f q p n", p=P, q=Q)
        PAIRS = B // 2

        w1 = [[mem.sbuf(f"w1_{part}{i}", [P, KT, 2, FQ], F32R) for part in ("hi", "lo")] for i in range(2)]
        w2 = [[mem.sbuf(f"w2_{part}{i}", [P, FT, D], F32R) for part in ("hi", "lo")] for i in range(2)]
        raw = mem.sbuf("ff_raw", [P, 3, FQ])
        nT = [[mem.sbuf(f"ff_nT_{part}{i}", [P, KT, S], F32R) for part in ("hi", "lo")] for i in range(2)]
        u = [[mem.sbuf(f"u_{part}{i}", [P, FT, S], F32R) for part in ("hi", "lo")] for i in range(2)]
        sig = mem.sbuf("ff_sig", [P, 2, S])
        u32 = mem.sbuf("u32", [P, 2, S])
        xs = [mem.sbuf(f"ff_x{i}", [P, TT, D]) for i in range(2)]
        UP = [[mem.bank(f"ff_{n}{i}") for n in ("a", "gate")] for i in range(2)]
        DN = [mem.bank(f"ff_down{i}") for i in range(2)]

        raw_in = [mem.sem(f"ff_raw_in{i}") for i in range(3)]
        raw_hi, raw_lo = mem.sem("ff_raw_hi"), mem.sem("ff_raw_lo")
        nT_in = [mem.sem(f"ff_nT_in{i}") for i in range(2)]
        x_in = [mem.sem(f"ff_x_in{i}") for i in range(2)]
        x_out = [mem.sem(f"ff_x_out{i}") for i in range(2)]
        up_ready, sig_ready, u_ready, u_hi_done, u_lo_done = (
            mem.sem(f"ff_{n}") for n in ("up_ready", "sig_ready", "u_ready", "u_hi_done", "u_lo_done"))
        down_ready, down_taken, rows_seen = (mem.sem(f"ff_{n}") for n in ("down_ready", "down_taken", "rows_seen"))

        def chunk(q, k, c):
            one = lambda ap: ap[k] if isinstance(k, int) else ap[bass.ds(k, 1)].rearrange("o a b -> (o a) b")
            to = lambda t: t[:, k] if isinstance(k, int) else t[:, bass.ds(k, 1)].rearrange("p o n -> p (o n)")
            if c < 2:
                return one(w1_v[:, q, c]), [to(t[:, :, c, :]) for t in w1[q % 2]]
            return one(w2_v[:, q]), [to(t[:, :, :]) for t in w2[q % 2]]

        with nc.Block() as block:
            @block.sync
            def _(sp):
                def load_weights(q, k, n):
                    for c in range(3):
                        sp.wait_ge(raw_lo, n * 3)
                        sp.dma_start(raw[:, c, :], chunk(q, k, c)[0]).then_inc(raw_in[c], 16)

                def load_rows(b, i):
                    for part in range(2):
                        src = xnT_d[part]
                        src = src[b] if isinstance(b, int) else src[bass.ds(b, 1)].rearrange("o p k s -> (o p) k s")
                        sp.dma_start(plain(nT[i][part][:, :, :]), src).then_inc(nT_in[i], 16)

                def load_x(b, i):
                    src = x_v[b] if isinstance(b, int) else x_v[bass.ds(b, 1)].rearrange("o p t d -> (o p) t d")
                    sp.dma_start(xs[i][:, :, :], src).then_inc(x_in[i], 16)

                def store_x(b, i):
                    dst = x_v[b] if isinstance(b, int) else x_v[bass.ds(b, 1)].rearrange("o p t d -> (o p) t d")
                    sp.dma_start(dst, xs[i][:, :, :]).then_inc(x_out[i], 16)

                def step(q, pair, following):
                    n = pair + q * PAIRS
                    here = [pair * 2 + i for i in range(2)]
                    there = [following * 2 + i for i in range(2)] if following is not None else None
                    if q + 1 < Q:
                        load_weights(q + 1, pair, n + PAIRS)
                    for i in range(2):
                        sp.wait_ge(x_out[i], n * 16)
                        load_x(here[i], i)
                    if there is not None:
                        for i in range(2):
                            sp.wait_ge(up_ready, n * (2 * FT) + (i + 1) * FT)
                            load_rows(there[i], i)
                    for i in range(2):
                        if q == Q - 1:
                            sp.wait_ge(rows_seen, here[i] + 1)
                        else:
                            sp.wait_ge(down_taken, (n * 2 + i + 1) * TT)
                        store_x(here[i], i)

                load_rows(0, 0)
                for k in range(PAIRS):
                    load_weights(0, k, k)
                load_rows(1, 1)
                for q in range(Q):
                    with sp.Fori(0, PAIRS - 1) as pair:
                        step(q, pair, pair + 1)
                    step(q, PAIRS - 1, 0 if q + 1 < Q else None)
                for i in range(2):
                    sp.wait_ge(x_out[i], Q * PAIRS * 16)

            @block.tensor
            def _(pe):
                def up(q, n, i):
                    pe.wait_ge(nT_in[i], (n + 1) * 32)
                    for f in range(FT):
                        m = n * (2 * FT) + i * FT + f
                        if f >= 2:
                            pe.wait_ge(u_ready, m - 1)
                        else:
                            pe.wait_ge(u_ready, n * (2 * FT) + i * FT)
                        for g in (1, 0):
                            c = 0
                            for k in range(KT):
                                for w, m_ in products([t[:, k, g, f * P:(f + 1) * P] for t in w1[q % 2]], [t[:, k, :] for t in nT[i]]):
                                    last = nc.tensor.matmul(UP[f % 2][g][:, :], w, m_, start=c == 0, stop=c == 3 * KT - 1)
                                    c += 1
                        last.then_inc(up_ready, 1)

                def down(q, n, i):
                    pe.wait_ge(u_lo_done, n * (2 * FT) + (i + 1) * FT)
                    for t in range(TT):
                        m = n * (2 * TT) + i * TT
                        pe.wait_ge(down_taken, m + max(t - 1, 0))
                        c = 0
                        for f in range(FT):
                            for a, w in products([x[:, f, t * P:(t + 1) * P] for x in u[i]], [x[:, f, :] for x in w2[q % 2]]):
                                last = nc.tensor.matmul(DN[t % 2][:, :], a, w, start=c == 0, stop=c == 3 * FT - 1)
                                c += 1
                        last.then_inc(down_ready, 1)

                for q in range(Q):
                    pe.wait_ge(raw_lo, (q + 1) * PAIRS * 3)
                    with pe.Fori(0, PAIRS) as pair:
                        n = pair + q * PAIRS
                        up(q, n, 0)
                        up(q, n, 1)
                        down(q, n, 0)
                        down(q, n, 1)

            @block.scalar
            def _(act):
                def split_weights(q, k, n):
                    for c in range(3):
                        act.wait_ge(raw_in[c], (n + 1) * 16)
                        nc.scalar.copy(chunk(q, k, c)[1][0], raw[:, c, :]).then_inc(raw_hi, 1)

                def hidden(n, i):
                    for f in range(FT):
                        m = n * (2 * FT) + i * FT + f
                        act.wait_ge(up_ready, m + 1)
                        if f >= 2:
                            act.wait_ge(u_ready, m - 1)
                        nc.scalar.activation(sig[:, f % 2, :], UP[f % 2][1][:, :], ACT.Silu).then_inc(sig_ready, 1)
                        act.wait_ge(u_ready, m + 1)
                        if f == 0:
                            act.wait_ge(down_ready, n * (2 * TT))
                        nc.scalar.copy(u[i][0][:, f, :], u32[:, f % 2, :]).then_inc(u_hi_done, 1)

                for k in range(PAIRS):
                    split_weights(0, k, k)
                for q in range(Q):
                    with act.Fori(0, PAIRS) as pair:
                        n = pair + q * PAIRS
                        hidden(n, 0)
                        if q + 1 < Q:
                            split_weights(q + 1, pair, n + PAIRS)
                        hidden(n, 1)

            @block.gpsimd
            def _(pool):
                def split_weights(q, k, n):
                    for c in range(3):
                        pool.wait_ge(raw_hi, n * 3 + c + 1)
                        hi, lo = chunk(q, k, c)[1]
                        nc.gpsimd.tensor_tensor(lo, raw[:, c, :], plain(hi), ALU.subtract).then_inc(raw_lo, 1)

                for k in range(PAIRS):
                    split_weights(0, k, k)
                for q in range(Q - 1):
                    with pool.Fori(0, PAIRS) as pair:
                        split_weights(q + 1, pair, pair + (q + 1) * PAIRS)

            @block.vector
            def _(dve):
                def hidden(n, i):
                    for f in range(FT):
                        m = n * (2 * FT) + i * FT + f
                        dve.wait_ge(sig_ready, m + 1)
                        dve.wait_ge(u_lo_done, n * (2 * FT) + i * FT + max(f - 1, 0))
                        nc.vector.tensor_tensor(u32[:, f % 2, :], sig[:, f % 2, :], UP[f % 2][0][:, :], ALU.mult).then_inc(u_ready, 1)
                        dve.wait_ge(u_hi_done, m + 1)
                        nc.vector.tensor_tensor(u[i][1][:, f, :], u32[:, f % 2, :], plain(u[i][0][:, f, :]), ALU.subtract).then_inc(u_lo_done, 1)

                def residual(q, n, i, b):
                    dve.wait_ge(x_in[i], (n + 1) * 16)
                    for t in range(TT):
                        dve.wait_ge(down_ready, n * (2 * TT) + i * TT + t + 1)
                        nc.vector.scalar_tensor_tensor(xs[i][:, t, :], DN[t % 2][:, :], gates[:, 0:1], xs[i][:, t, :],
                                                       ALU.mult, ALU.add).then_inc(down_taken, 1)
                    if q == Q - 1:
                        nc.vector.drain()
                        for t in range(TT):
                            last = nc.vector.bn_stats(x_stats[:, bass.ds(b * TT + t, 1), :].rearrange("p o n -> p (o n)"), xs[i][:, t, :])
                        last.then_inc(rows_seen, 1)

                for q in range(Q):
                    with dve.Fori(0, PAIRS) as pair:
                        n = pair + q * PAIRS
                        hidden(n, 0)
                        hidden(n, 1)
                        residual(q, n, 0, pair * 2)
                        residual(q, n, 1, pair * 2 + 1)


def slot_attention(nc, whole, I, ident, ones, x_stats, o1, hT, x1_d, yT_d):
    with ExitStack() as stage:
        mem = Memory(nc, stage, whole)
        x_v = x1_d.rearrange("b (t p) d -> b p t d", p=P)
        by_rows = lambda w: w.rearrange("(k p) n -> p k n", p=P)
        wq, wk, wv, wo = (mem.sbuf(f"d_w{n}", [P, KT, D]) for n in "qkvo")
        bias = {n: mem.sbuf(f"d_b{n}", [1, D]) for n in "qvo"}
        bk_col = mem.sbuf("d_bk_col", [P, KT])
        sq = mem.sbuf("sq", [NS, D])
        sqT = mem.sbuf("sqT", [P, KT, NS])
        q16 = mem.sbuf("q16", [NS, D])
        q_diag = mem.sbuf("q_diag", [P, KT, 4 * NS])
        wkT = mem.sbuf("wkT", [P, KT, D])
        A = [mem.sbuf(f"A_{part}", [P, KT, HS], F32R) for part in ("hi", "lo")]
        shift = mem.sbuf("shift", [P, 2])
        every = mem.sbuf("every", [NS, P])
        mean, var, rstd, half = (mem.sbuf(f"y_{n}", [P, B * TT]) for n in ("mean", "var", "rstd", "half"))
        xin = mem.sbuf("y_xin", [P, TT, D])
        y = mem.sbuf("y", [P, TT, D])
        yn = [mem.sbuf(f"yn_{part}", [P, 2, TT, D], F32R) for part in ("hi", "lo")]
        yT = [mem.sbuf(f"yT_{part}", [P, KT, S], F32R) for part in ("hi", "lo")]
        pT = [mem.sbuf(f"pT_{part}", [P, TT, HS], F32R) for part in ("hi", "lo")]
        prob = mem.sbuf("d_prob", [P, 2, S])
        top, nb, total, inv = (mem.sbuf(f"d_{n}", [P, 2]) for n in ("top", "nb", "total", "inv"))
        z = mem.sbuf("z", [P, 2, D])
        zT = mem.sbuf("zT", [P, KT, SH, B, NS])
        G = [mem.bank(f"slot_general{i}") for i in range(5)]
        SC = [mem.bank(f"slot_scores{i}") for i in range(2)]

        weights_in, small_in = mem.sem("d_weights_in"), mem.sem("d_small_in")
        pe_step, dve_step, act_step = (mem.sem(f"d_{n}_step") for n in ("pe", "dve", "act"))
        sd_ready = mem.sem("d_sd_ready")
        with nc.Block() as block:
            @block.sync
            def _(sp):
                sp.dma_start(sq[:, :], I["L0_ffn_slot_query"].rearrange("o s d -> (o s) d")).then_inc(small_in, 16)
                sp.dma_start(bk_col[:, :], I["L0_ffn_d_bk"].rearrange("(k p) -> p k", p=P), allow_slow_non_contiguous=True).then_inc(small_in, 16)
                for n in "qvo":
                    sp.dma_start(bias[n][:, :], I[f"L0_ffn_d_b{n}"].unsqueeze(0)).then_inc(small_in, 16)
                for n, w in zip("qkvo", (wq, wk, wv, wo)):
                    sp.dma_start(w[:, :, :], by_rows(I[f"L0_ffn_d_W{n}"])).then_inc(weights_in, 16)
                sp.wait_ge(weights_in, 64)

            @block.tensor
            def _(pe):
                pe.wait_ge(small_in, 80)
                for k in range(KT):
                    last = nc.tensor.transpose(G[0][:, k * NS:(k + 1) * NS], sq[:, k * P:(k + 1) * P], ident[0:NS, 0:NS])
                last.then_inc(pe_step, 1)
                pe.wait_ge(weights_in, 64)
                pe.wait_ge(dve_step, 1)
                nc.tensor.matmul(G[1][0:NS, :], ones[0:1, 0:NS], bias["q"][:, :], start=True, stop=False)
                for k in range(KT):
                    last = nc.tensor.matmul(G[1][0:NS, :], sqT[:, k, :], wq[:, k, :], start=False, stop=k == KT - 1)
                last.then_inc(pe_step, 1)
                for c in range(KT):
                    if c >= 2:
                        pe.wait_ge(act_step, c - 1)
                    for k in range(KT):
                        last = nc.tensor.transpose(G[2 + c % 2][:, k * P:(k + 1) * P], wk[:, k, c * P:(c + 1) * P], ident[:, :])
                    last.then_inc(pe_step, 1)
                pe.wait_ge(dve_step, 2)
                for k in range(KT):
                    last = nc.tensor.transpose(G[0][:, k * NS:(k + 1) * NS], q16[:, k * P:(k + 1) * P], ident[0:NS, 0:NS])
                last.then_inc(pe_step, 1)
                pe.wait_ge(dve_step, 3)
                pe.wait_ge(act_step, KT)
                for k in range(KT):
                    for c in range(KT):
                        at = (k % 2) * HS + c * 4 * NS
                        last = nc.tensor.matmul(SC[k // 2][:, at:at + 4 * NS], wkT[:, c, k * P:(k + 1) * P], q_diag[:, c, :], start=True, stop=True)
                for c in range(KT):
                    at = (c % 2) * 4 * NS
                    last = nc.tensor.matmul(G[4][at:at + 4 * NS, c // 2:c // 2 + 1], q_diag[:, c, :], bk_col[:, c:c + 1], start=True, stop=True)
                last.then_inc(pe_step, 1)

            @block.scalar
            def _(act):
                for c in range(KT):
                    act.wait_ge(pe_step, 3 + c)
                    nc.scalar.copy(wkT[:, c, :], G[2 + c % 2][:, :]).then_inc(act_step, 1)
                act.wait_ge(dve_step, 4)
                nc.scalar.activation(rstd[:, :], var[:, :], ACT.Sqrt).then_inc(sd_ready, 1)
                act.wait_ge(pe_step, KT + 4)
                for i in range(2):
                    nc.scalar.copy(A[0][:, 2 * i:2 * i + 2, :].rearrange("p k n -> p (k n)"), SC[i][:, :]).then_inc(act_step, 1)

            @block.vector
            def _(dve):
                nc.vector.memset(q_diag[:, :, :], 0.0)
                dve.wait_ge(pe_step, 1)
                nc.vector.tensor_copy(sqT[:, :, :].rearrange("p k s -> p (k s)"), G[0][:, 0:KT * NS]).then_inc(dve_step, 1)
                dve.wait_ge(pe_step, 2)
                nc.vector.tensor_scalar(q16[:, :], G[1][0:NS, :], SD ** -0.5, None, ALU.mult).then_inc(dve_step, 1)
                dve.wait_ge(pe_step, KT + 3)
                for g in range(4):
                    rows = slice(g * SD, (g + 1) * SD)
                    last = nc.vector.tensor_copy(q_diag[rows, :, g * NS:(g + 1) * NS], G[0][rows, 0:KT * NS].rearrange("p (k s) -> p k s", k=KT))
                last.then_inc(dve_step, 1)
                rows_mean_var(nc, x_stats[:, :, :], mean[:, :], var[:, :], half[:, :])
                nc.vector.tensor_scalar(var[:, :], var[:, :], EPS, None, ALU.add).then_inc(dve_step, 1)
                for b in range(B):
                    nc.vector.tensor_copy(every[:, b * NS:(b + 1) * NS], ident[0:NS, 0:NS])
                dve.wait_ge(sd_ready, 1)
                nc.vector.reciprocal(rstd[:, :], rstd[:, :])
                dve.wait_ge(pe_step, KT + 4)
                nc.vector.tensor_copy(shift[:, :], G[4][:, 0:2])
                for i in range(2):
                    dve.wait_ge(act_step, KT + i + 1)
                    nc.vector.tensor_tensor(A[1][:, 2 * i:2 * i + 2, :].rearrange("p k n -> p (k n)"), SC[i][:, :],
                                            plain(A[0][:, 2 * i:2 * i + 2, :].rearrange("p k n -> p (k n)")), ALU.subtract)

        x_in, y_ready, yn_hi_done, yn_lo_done, yT_out = (mem.sem(f"d_{n}") for n in ("x_in", "y_ready", "yn_hi", "yn_lo", "yT_out"))
        g_ready, g_hi, g_free = (mem.sem(f"d_{n}") for n in ("g_ready", "g_hi", "g_free"))
        scored, nb_ready, exps = (mem.sem(f"d_{n}") for n in ("scored", "nb_ready", "exps"))
        U_Y, U_P, U_Z, U_ZT, PER = 0, KT, KT + 2, KT + 4, KT + 6
        NG = len(G)
        assert PER % NG == 0
        HI = KT + 2

        def of(ap, b):
            return ap[b] if isinstance(b, int) else ap[bass.ds(b, 1)].rearrange("o p t d -> (o p) t d")

        def slot(t, b):
            return t[:, b % 2] if isinstance(b, int) else t[:, bass.ds(b % 2, 1)].rearrange("p o t d -> p (o t) d")

        with nc.Block() as block:
            @block.sync
            def _(sp):
                def keep(b):
                    sp.wait_ge(g_free, b * PER + U_P)
                    for part in range(2):
                        sp.dma_start(of(yT_d[part], b), plain(yT[part][:, :, :])).then_inc(yT_out, 16)

                sp.dma_start(xin[:, :, :], x_v[0]).then_inc(x_in, 16)
                with sp.Fori(0, B - 1) as b:
                    sp.wait_ge(y_ready, b + 1)
                    sp.dma_start(xin[:, :, :], of(x_v, b + 1)).then_inc(x_in, 16)
                    keep(b)
                keep(B - 1)
                sp.wait_ge(yT_out, B * 32)

            @block.tensor
            def _(pe):
                def claim(b, u):
                    if not (isinstance(b, int) and b == 0 and u < NG):
                        pe.wait_ge(g_free, b * PER + u - (NG - 1))
                    return G[u % NG]

                def turn_rows(b):
                    pe.wait_ge(y_ready, b + 1)
                    for k in range(KT):
                        bank = claim(b, U_Y + k)
                        for t in range(TT):
                            last = nc.tensor.transpose(bank[:, t * P:(t + 1) * P], y[:, t, k * P:(k + 1) * P], ident[:, :])
                        last.then_inc(g_ready, 1)

                def score(b):
                    pe.wait_ge(g_free, b * PER + U_P)
                    pe.wait_ge(exps, b * 2)
                    for i in range(2):
                        n = 0
                        for k in range(KT):
                            for a, m in products([t[:, k, i * P:(i + 1) * P] for t in A], [t[:, k, :] for t in yT]):
                                last = nc.tensor.matmul(SC[i][:, :], a, m, start=n == 0, stop=n == 3 * KT - 1)
                                n += 1
                        last.then_inc(scored, 1)

                def turn_probs(b):
                    pe.wait_ge(exps, b * 2)
                    for half_ in range(2):
                        bank = claim(b, U_P + half_)
                        for t in range(2):
                            for i in range(2):
                                tok = (2 * half_ + t) * P
                                last = nc.tensor.transpose(bank[:, t * HS + i * P:t * HS + (i + 1) * P], prob[:, i, tok:tok + P], ident[:, :])
                        last.then_inc(g_ready, 1)

                def sums(b, prev):
                    pe.wait_ge(g_free, b * PER + U_Z)
                    pe.wait_ge(yn_lo_done, b)
                    for i in range(2):
                        bank = claim(b, U_Z + i)
                        n = 0
                        for t in range(TT):
                            for a, m in products([x[:, t, i * P:(i + 1) * P] for x in pT], [slot(x, prev) for x in yn]):
                                last = nc.tensor.matmul(bank[:, :], a, m[:, t, :], start=n == 0, stop=n == 3 * TT - 1)
                                n += 1
                        last.then_inc(g_ready, 1)
                    pe.wait_ge(g_free, b * PER + U_ZT)
                    for half_ in range(2):
                        bank = claim(b, U_ZT + half_)
                        for k in range(2):
                            for i in range(2):
                                d = (2 * half_ + k) * P
                                last = nc.tensor.transpose(bank[:, k * HS + i * P:k * HS + (i + 1) * P], z[:, i, d:d + P], ident[:, :])
                        last.then_inc(g_ready, 1)

                turn_rows(0)
                pe.drain().then_inc(g_ready, PER - U_P)
                score(0)
                with pe.Fori(1, B) as b:
                    turn_rows(b)
                    turn_probs(b)
                    score(b)
                    sums(b, b - 1)
                pe.drain().then_inc(g_ready, U_P)
                turn_probs(B)
                sums(B, B - 1)

            @block.scalar
            def _(act):
                def front(b):
                    act.wait_ge(y_ready, b + 1)
                    if not (isinstance(b, int) and b == 0):
                        act.wait_ge(g_ready, (b - 1) * PER + U_ZT)
                    nc.scalar.copy(slot(yn[0], b), y[:, :, :]).then_inc(yn_hi_done, 1)
                    if not (isinstance(b, int) and b == 0):
                        act.wait_ge(yT_out, b * 32)
                        act.wait_ge(scored, b * 2)
                    for k in range(KT):
                        act.wait_ge(g_ready, b * PER + U_Y + k + 1)
                        nc.scalar.copy(yT[0][:, k, :], G[(U_Y + k) % NG][:, :]).then_inc(g_hi, 1)

                def probs(b):
                    for i in range(2):
                        act.wait_ge(g_ready, b * PER + U_P + i + 1)
                        nc.scalar.copy(pT[0][:, 2 * i:2 * i + 2, :].rearrange("p t n -> p (t n)"), G[(U_P + i) % NG][:, :]).then_inc(g_hi, 1)

                def exp(b):
                    act.wait_ge(nb_ready, b + 1)
                    for i in range(2):
                        nc.scalar.activation(prob[:, i, :], SC[i][:, :], ACT.Exp, bias=nb[:, i:i + 1], accum_out=total[:, i:i + 1]).then_inc(exps, 1)

                front(0)
                act.drain().then_inc(g_hi, 2)
                exp(0)
                with act.Fori(1, B) as b:
                    front(b)
                    probs(b)
                    exp(b)
                act.drain().then_inc(g_hi, KT)
                probs(B)

            @block.gpsimd
            def _(pool):
                with pool.Fori(0, B) as b:
                    pool.wait_ge(yn_hi_done, b + 1)
                    nc.gpsimd.tensor_tensor(slot(yn[1], b), y[:, :, :], plain(slot(yn[0], b)), ALU.subtract).then_inc(yn_lo_done, 1)

            @block.vector
            def _(dve):
                def norm(b):
                    dve.wait_ge(x_in, b * 16 + 16)
                    dve.wait_ge(yn_lo_done, b)
                    for t in range(TT):
                        n = b * TT + t
                        last = nc.vector.tensor_scalar(y[:, t, :], xin[:, t, :], mean[:, bass.ds(n, 1)], rstd[:, bass.ds(n, 1)], ALU.subtract, ALU.mult)
                    last.then_inc(y_ready, 1)

                def front(b):
                    for k in range(KT):
                        dve.wait_ge(g_hi, b * HI + k + 1)
                        nc.vector.tensor_tensor(yT[1][:, k, :], G[(U_Y + k) % NG][:, :], plain(yT[0][:, k, :]), ALU.subtract).then_inc(g_free, 1)

                def probs(b):
                    for i in range(2):
                        dve.wait_ge(g_hi, b * HI + KT + i + 1)
                        flat = lambda x: x[:, 2 * i:2 * i + 2, :].rearrange("p t n -> p (t n)")
                        nc.vector.tensor_tensor(flat(pT[1]), G[(U_P + i) % NG][:, :], plain(flat(pT[0])), ALU.subtract).then_inc(g_free, 1)

                def maxima(b):
                    for i in range(2):
                        dve.wait_ge(scored, b * 2 + i + 1)
                        nc.vector.tensor_reduce(top[:, i:i + 1], SC[i][:, :], AX.X, ALU.max)
                    nc.vector.drain()
                    nc.vector.tensor_tensor(top[:, :], top[:, :], shift[:, :], ALU.add)
                    nc.vector.drain()
                    nc.vector.tensor_tensor(nb[:, :], shift[:, :], top[:, :], ALU.subtract).then_inc(nb_ready, 1)

                def inverse(b):
                    dve.wait_ge(exps, b * 2)
                    nc.vector.reciprocal(inv[:, :], total[:, :])
                    nc.vector.drain()

                def sums(b, prev):
                    for i in range(2):
                        dve.wait_ge(g_ready, b * PER + U_Z + i + 1)
                        nc.vector.tensor_scalar(z[:, i, :], G[(U_Z + i) % NG][:, :], inv[:, i:i + 1], None, ALU.mult).then_inc(g_free, 1)
                    for i in range(2):
                        dve.wait_ge(g_ready, b * PER + U_ZT + i + 1)
                        to = zT[:, 2 * i:2 * i + 2, :, prev, :] if isinstance(prev, int) else \
                            zT[:, 2 * i:2 * i + 2, :, bass.ds(prev, 1), :].rearrange("p k h o s -> p k h (o s)")
                        nc.vector.tensor_copy(to, G[(U_ZT + i) % NG][:, :].rearrange("p (k h s) -> p k h s", k=2, h=SH)).then_inc(g_free, 1)

                norm(0)
                front(0)
                nc.vector.drain().then_inc(g_free, PER - U_P)
                norm(1)
                maxima(0)
                with dve.Fori(1, B - 1) as b:
                    front(b)
                    inverse(b)
                    probs(b)
                    norm(b + 1)
                    maxima(b)
                    sums(b, b - 1)
                front(B - 1)
                inverse(B - 1)
                probs(B - 1)
                maxima(B - 1)
                sums(B - 1, B - 2)
                nc.vector.drain().then_inc(g_free, U_P)
                inverse(B)
                probs(B)
                sums(B, B - 1)

        o_att, oT = mem.sbuf("o_att", [P, D]), mem.sbuf("oT_s", [P, KT, P])
        stat1, mv, sd = mem.sbuf("o_stats", [P, 6]), mem.sbuf("o_mv", [P, 2]), mem.sbuf("o_sd", [P, 1])
        e_gain, e_shift, h_in = (mem.sbuf(n, [P, D]) for n in ("e_gain", "e_shift", "h_in"))
        gains_in, pe2, dve2, act2 = (mem.sem(f"d2_{n}") for n in ("gains_in", "pe", "dve", "act"))
        with nc.Block() as block:
            @block.sync
            def _(sp):
                for b in range(B):
                    sp.dma_start(e_gain[b * NS:(b + 1) * NS, :], I["L0_ffn_e_ln_g"]).then_inc(gains_in, 16)
                    sp.dma_start(e_shift[b * NS:(b + 1) * NS, :], I["L0_ffn_e_ln_b"]).then_inc(gains_in, 16)
                sp.wait_ge(gains_in, 2 * B * 16)

            @block.tensor
            def _(pe):
                nc.tensor.matmul(G[0][:, :], ones[0:1, :], bias["v"][:, :], start=True, stop=False)
                for h in range(SH):
                    cols = slice(h * SD, (h + 1) * SD)
                    for k in range(KT):
                        last = nc.tensor.matmul(G[0][:, cols], zT[:, k, h, :, :].rearrange("p b s -> p (b s)"), wv[:, k, cols],
                                                start=False, stop=h == SH - 1 and k == KT - 1)
                last.then_inc(pe2, 1)
                pe.wait_ge(dve2, 1)
                for k in range(KT):
                    last = nc.tensor.transpose(G[1][:, k * P:(k + 1) * P], o_att[:, k * P:(k + 1) * P], ident[:, :])
                last.then_inc(pe2, 1)
                pe.wait_ge(dve2, 2)
                nc.tensor.matmul(G[2][:, :], ones[0:1, :], bias["o"][:, :], start=True, stop=False)
                nc.tensor.matmul(G[2][:, :], every[:, :], sq[:, :], start=False, stop=False)
                for k in range(KT):
                    last = nc.tensor.matmul(G[2][:, :], oT[:, k, :], wo[:, k, :], start=False, stop=k == KT - 1)
                last.then_inc(pe2, 1)
                pe.wait_ge(dve2, 4)
                for k in range(KT):
                    last = nc.tensor.transpose(G[3][:, k * P:(k + 1) * P], h_in[:, :].rearrange("r (p k) -> r k p", k=KT)[:, k, :], ident[:, :])
                last.then_inc(pe2, 1)

            @block.scalar
            def _(act):
                act.wait_ge(dve2, 3)
                nc.scalar.activation(sd[:, :], sd[:, :], ACT.Sqrt).then_inc(act2, 1)

            @block.vector
            def _(dve):
                dve.wait_ge(pe2, 1)
                nc.vector.tensor_copy(o_att[:, :], G[0][:, :]).then_inc(dve2, 1)
                dve.wait_ge(pe2, 2)
                nc.vector.tensor_copy(oT[:, :, :].rearrange("p k n -> p (k n)"), G[1][:, :]).then_inc(dve2, 1)
                dve.wait_ge(pe2, 3)
                nc.vector.tensor_copy(o1[:, :], G[2][:, :])
                nc.vector.drain()
                nc.vector.bn_stats(stat1[:, :], o1[:, :])
                nc.vector.drain()
                nc.vector.bn_aggr(mv[:, :], stat1[:, :])
                nc.vector.drain()
                nc.vector.tensor_scalar(sd[:, :], mv[:, 1:2], EPS, None, ALU.add).then_inc(dve2, 1)
                dve.wait_ge(act2, 1)
                nc.vector.reciprocal(sd[:, :], sd[:, :])
                nc.vector.drain()
                nc.vector.tensor_scalar(h_in[:, :], o1[:, :], mv[:, 0:1], sd[:, 0:1], ALU.subtract, ALU.mult)
                dve.wait_ge(gains_in, 2 * B * 16)
                nc.vector.drain()
                nc.vector.tensor_tensor(h_in[:, :], h_in[:, :], e_gain[:, :], ALU.mult)
                nc.vector.drain()
                nc.vector.tensor_tensor(h_in[:, :], h_in[:, :], e_shift[:, :], ALU.add).then_inc(dve2, 1)
                dve.wait_ge(pe2, 4)
                for k in range(KT):
                    nc.vector.tensor_copy(hT[:, k, :, :], G[3][:, k * P:(k + 1) * P].rearrange("p (b e) -> p e b", e=E))


def experts(nc, whole, I, ident, hT, y_d):
    with ExitStack() as stage:
        mem = Memory(nc, stage, whole)
        FT = FF // P
        Q, QW = 4, 32
        C = FF // Q
        J = C // P
        w1 = [mem.sbuf(f"e_w1_{i}", [P, KT, FF]) for i in range(2)]
        wg = [mem.sbuf(f"e_wg_{i}", [P, KT, FF]) for i in range(2)]
        w2 = [mem.sbuf(f"e_w2_{i}", [P, FT, D]) for i in range(2)]
        bias_rows = [w2[1][0:E, 4 * i:4 * i + 4, :].rearrange("e a n -> e (a n)") for i in range(2)]
        block_at = [q * C + j * P for j in range(J) for q in range(Q)]
        biasT = [mem.sbuf(f"e_{n}T", [P, FT, E]) for n in ("b1", "bg")]
        h = mem.sbuf("e_h", [P, KT, QW])
        rows = [mem.sbuf(f"e_{n}_rows", [P, C]) for n in "ug"]
        pre = rows[0][:, 0:2 * FT * B].rearrange("p (n f b) -> p n f b", n=2, f=FT)
        ug = mem.sbuf("e_ug", [P, FT, QW])
        y_parts = mem.sbuf("e_y_parts", [P, D])
        ys = y_parts[0:B, :]
        fold = mem.sbuf("e_fold", [P, B])
        UP = [mem.bank(f"e_{n}") for n in "ug"]
        TB = [mem.bank(f"e_turned{i}") for i in range(2)]
        YB, YS = mem.bank("e_down"), mem.bank("e_folded")

        bias_in, bias_turned, bias_ready, fold_ready = (mem.sem(f"e_{n}") for n in ("bias_in", "bias_turned", "bias_ready", "fold_ready"))
        w1_in, wg_in, w2_in = ([mem.sem(f"e_{n}_in{i}") for i in range(2)] for n in ("w1", "wg", "w2"))
        h_ready, u_ready, g_ready, u_taken, g_taken, turned, pre_ready, silu_ready, ug_ready = (
            mem.sem(f"e_{n}") for n in ("h_ready", "u_ready", "g_ready", "u_taken", "g_taken", "turned", "pre_ready",
                                        "silu_ready", "ug_ready"))
        down_ready, parts_taken, folded, y_done, y_out = (
            mem.sem(f"e_{n}") for n in ("down_ready", "parts_taken", "folded", "y_done", "y_out"))

        def of(ap, e):
            return ap[e] if isinstance(e, int) else ap[bass.ds(e, 1)].rearrange("o a b -> (o a) b")

        def arrived(e, i):
            return e * 8 + (16 - 8 * i)

        def skewed(eng, start, body, finish):
            start(0, 0)
            with eng.Fori(0, E // 2 - 1) as pair:
                for i in range(2):
                    body(pair * 2 + i, i)
            body(E - 2, 0)
            finish(E - 1, 1)

        with nc.Block() as block:
            @block.sync
            def _(sp):
                def load(e, i, turn):
                    later = not (isinstance(turn, int) and turn == 0)
                    if later:
                        sp.wait_ge(u_ready, turn * 2 + (i - 1))
                    sp.dma_start(w1[i][:, :, :].rearrange("p k n -> p (k n)"), of(I["L0_ffn_e_W1"], e).rearrange("(p k) n -> p (k n)", k=KT)).then_inc(w1_in[i], 16)
                    if later:
                        sp.wait_ge(g_ready, turn * 2 + (i - 1))
                    sp.dma_start(wg[i][:, :, :].rearrange("p k n -> p (k n)"), of(I["L0_ffn_e_Wg"], e).rearrange("(p k) n -> p (k n)", k=KT)).then_inc(wg_in[i], 16)
                    if later:
                        sp.wait_ge(down_ready, turn * 2 + (i - 1))
                    elif i == 1:
                        sp.wait_ge(bias_turned, 2)
                    sp.dma_start(w2[i][:, :, :], of(I["L0_ffn_e_W2"], e).rearrange("(f p) n -> p f n", p=P)).then_inc(w2_in[i], 16)

                def store(e):
                    sp.wait_ge(y_done, e + 1)
                    sp.dma_start(of(y_d, e), ys).then_inc(y_out, 16)

                for i, n in enumerate(("b1", "bg")):
                    sp.dma_start(bias_rows[i], I[f"L0_ffn_e_{n}"]).then_inc(bias_in, 16)
                load(0, 0, 0)
                load(1, 1, 0)
                with sp.Fori(1, E // 2) as turn:
                    for i in range(2):
                        load(turn * 2 + i, i, turn)
                        store(turn * 2 + (i - 2))
                store(E - 2)
                store(E - 1)
                sp.wait_ge(y_out, E * 16)

            @block.tensor
            def _(pe):
                def grow(e, i):
                    pe.wait_ge(h_ready, e + 1)
                    for bank, w, arrival, taken, ready in ((UP[0], w1[i], w1_in[i], u_taken, u_ready), (UP[1], wg[i], wg_in[i], g_taken, g_ready)):
                        pe.wait_ge(arrival, arrived(e, i))
                        pe.wait_ge(taken, e)
                        for k in range(KT):
                            for q in range(Q):
                                last = nc.tensor.matmul(bank[q * QW:(q + 1) * QW, :], h[:, k, :], w[:, k, q * C:(q + 1) * C], start=k == 0, stop=k == KT - 1)
                        last.then_inc(ready, 1)

                def turn(e):
                    pe.wait_ge(pre_ready, e)
                    for n, taken in enumerate((u_taken, g_taken)):
                        pe.wait_ge(taken, e + 1)
                        for j in range(J):
                            last = nc.tensor.transpose(TB[n][:, j * P:(j + 1) * P], rows[n][:, j * P:(j + 1) * P], ident[:, :])
                    last.then_inc(turned, 1)

                def shrink(e, i):
                    pe.wait_ge(ug_ready, e + 1)
                    pe.wait_ge(w2_in[i], arrived(e, i))
                    pe.wait_ge(parts_taken, e)
                    for j in range(J):
                        for q in range(Q):
                            last = nc.tensor.matmul(YB[q * QW:(q + 1) * QW, :], ug[:, j * Q + q, :], w2[i][:, q * J + j, :], start=j == 0, stop=j == J - 1)
                    last.then_inc(down_ready, 1)

                def add_parts(e):
                    pe.wait_ge(parts_taken, e + 1)
                    pe.wait_ge(y_done, e)
                    nc.tensor.matmul(YS[0:B, :], fold[:, :], y_parts[:, :], start=True, stop=True).then_inc(folded, 1)

                def both(e, i):
                    grow(e + 1, 1 - i)
                    shrink(e, i)
                    turn(e + 1)
                    add_parts(e)

                def start(e, i):
                    grow(e, i)
                    turn(e)

                def finish(e, i):
                    shrink(e, i)
                    add_parts(e)

                pe.wait_ge(bias_in, 32)
                for n in range(2):
                    for f, at in enumerate(block_at):
                        last = nc.tensor.transpose(TB[n][:, f * E:(f + 1) * E], bias_rows[n][:, at:at + P], ident[0:E, 0:E])
                    last.then_inc(bias_turned, 1)
                pe.wait_ge(bias_ready, 2)
                pe.wait_ge(fold_ready, 1)
                skewed(pe, start, both, finish)

            @block.scalar
            def _(act):
                def start(e, i):
                    act.wait_ge(u_ready, e + 1)
                    act.wait_ge(ug_ready, e)
                    nc.scalar.copy(rows[0][:, :], UP[0][:, :]).then_inc(u_taken, 1)

                def finish(e, i):
                    act.wait_ge(down_ready, e + 1)
                    act.wait_ge(y_out, e * 16)
                    nc.scalar.copy(y_parts[:, :], YB[:, :]).then_inc(parts_taken, 1)

                def gates_of(e):
                    act.wait_ge(pre_ready, e + 1)
                    nc.scalar.activation(pre, pre, ACT.Silu).then_inc(silu_ready, 1)

                def both(e, i):
                    start(e + 1, 1 - i)
                    finish(e, i)
                    gates_of(e + 1)

                def first(e, i):
                    start(e, i)
                    gates_of(e)

                skewed(act, first, both, finish)

            @block.vector
            def _(dve):
                def take_h(e):
                    src = hT[:, :, e, :] if isinstance(e, int) else hT[:, :, bass.ds(e, 1), :].rearrange("p k o b -> p k (o b)")
                    nc.vector.tensor_copy(h[:, :, 0:B], src).then_inc(h_ready, 1)

                def start(e, i):
                    dve.wait_ge(g_ready, e + 1)
                    dve.wait_ge(turned, e)
                    nc.vector.tensor_copy(rows[1][:, :], UP[1][:, :]).then_inc(g_taken, 1)
                    if not (isinstance(e, int) and e == E - 1):
                        take_h(e + 1)

                def product(e):
                    dve.wait_ge(turned, e + 1)
                    for n in range(2):
                        cols = TB[n][:, :].rearrange("p (f r) -> p f r", r=QW)[:, :, 0:B]
                        add = biasT[n][:, :, e:e + 1] if isinstance(e, int) else biasT[n][:, :, bass.ds(e, 1)]
                        last = nc.vector.tensor_tensor(pre[:, n, :, :], cols, add.to_broadcast([P, FT, B]), ALU.add)
                    last.then_inc(pre_ready, 1)
                    dve.wait_ge(silu_ready, e + 1)
                    dve.wait_ge(down_ready, e)
                    nc.vector.tensor_tensor(ug[:, :, 0:B], pre[:, 0, :, :], pre[:, 1, :, :], ALU.mult).then_inc(ug_ready, 1)

                def finish(e, i):
                    dve.wait_ge(folded, e + 1)
                    nc.vector.tensor_copy(ys, YS[0:B, :]).then_inc(y_done, 1)

                def both(e, i):
                    start(e + 1, 1 - i)
                    product(e + 1)
                    finish(e, i)

                def first(e, i):
                    start(e, i)
                    product(e)

                nc.vector.memset(h[:, :, :], 0.0)
                nc.vector.memset(ug[:, :, :], 0.0)
                nc.vector.tensor_tensor(fold[:, :], ident[:, 0:B], ident[:, QW:QW + B], ALU.add)
                for q in range(2, Q):
                    nc.vector.drain()
                    last = nc.vector.tensor_tensor(fold[:, :], fold[:, :], ident[:, q * QW:q * QW + B], ALU.add)
                last.then_inc(fold_ready, 1)
                take_h(0)
                for n in range(2):
                    dve.wait_ge(bias_turned, n + 1)
                    nc.vector.tensor_copy(biasT[n][:, :, :].rearrange("p f e -> p (f e)"), TB[n][:, 0:FT * E]).then_inc(bias_ready, 1)
                skewed(dve, first, both, finish)


def token_attention(nc, whole, I, ident, gates, o1, x1_d, yT_d, y_d, out):
    with ExitStack() as stage:
        mem = Memory(nc, stage, whole)
        HT = HS // P
        CH = P // SD
        x_v = x1_d.rearrange("b (t p) d -> b p t d", p=P)
        out_v = out.rearrange("b (t p) d -> b p t d", p=P)
        by_rows = lambda w: w.rearrange("(k p) n -> p k n", p=P)
        WK = [mem.sbuf(f"WK_{part}", [P, KT, B, HS], F32R) for part in ("hi", "lo")]
        VW_hi = mem.sbuf("VW_hi", [P, B, HT, D], F32R)
        with nc.sbuf_tensor("c_lent", [P, 4, KT, D], F32) as lent:
            wq, wk, wv = (lent[:, i, :, :] for i in range(3))
            o2, o2T, y_rows, b2_rows = (lent[:, 3, i, :] for i in range(4))
        VW = [VW_hi, mem.sbuf("VW_lo", [P, B, HT, D], F32R)]
        bias_k = mem.sbuf("bias_k", [P, B, HS])
        bo_gate = mem.sbuf("bo_gate", [P, D])

        slots_in, c_small_in, c_weights_in = (mem.sem(f"c_{n}") for n in ("slots_in", "small_in", "weights_in"))
        o2_ready, blocks_zero, w_ready, w_hi, w_free = (mem.sem(f"c_{n}") for n in ("o2_ready", "blocks_zero", "w_ready", "w_hi", "w_free"))
        with ExitStack() as early:
            first = Memory(nc, early, whole)
            wo, wqT = first.sbuf("c_wo", [P, KT, D]), first.sbuf("c_wqT", [P, KT, D])
            k_diag = first.sbuf("k_diag", [P, KT, B, CH * NS])
            v_diag = first.sbuf("v_diag", [P, KT, B, P])
            bias = {n: first.sbuf(f"c_b{n}_col", [P, KT]) for n in "qkv"}
            banks = [first.bank(f"c_general{i}") for i in range(8)]
            U_WQ, U_O2, U_K, U_V, U_BK = 0, KT, KT + 1, KT + 2, KT + 3
            U_WK = U_BK + KT
            U_VW = U_WK + KT * KT
            of_bank = lambda u: banks[u % 8]

            with nc.Block() as block:
                @block.sync
                def _(sp):
                    sp.dma_start(wq, by_rows(I["L0_ffn_c_Wq"])).then_inc(c_weights_in, 16)
                    for b in range(B):
                        sp.dma_start(y_rows[b * NS:(b + 1) * NS, :], y_d[:, b, :]).then_inc(slots_in, 16)
                        sp.dma_start(b2_rows[b * NS:(b + 1) * NS, :], I["L0_ffn_e_b2"]).then_inc(slots_in, 16)
                    for n in "qkv":
                        sp.dma_start(bias[n][:, :], I[f"L0_ffn_c_b{n}"].rearrange("(k p) -> p k", p=P), allow_slow_non_contiguous=True).then_inc(c_small_in, 16)
                    sp.dma_start(bo_gate[:, :], I["L0_ffn_c_bo"].unsqueeze(0).to_broadcast([P, D])).then_inc(c_small_in, 16)
                    sp.wait_ge(c_weights_in, 16)
                    for n, w in zip("kvo", (wk, wv, wo)):
                        dst = w if n != "o" else w[:, :, :]
                        sp.dma_start(dst, by_rows(I[f"L0_ffn_c_W{n}"])).then_inc(c_weights_in, 16)

                @block.tensor
                def _(pe):
                    def claim(u):
                        if u >= 8:
                            pe.wait_ge(w_free, u - 7)
                        return of_bank(u)

                    pe.wait_ge(c_weights_in, 16)
                    for c in range(KT):
                        bank = claim(U_WQ + c)
                        for k in range(KT):
                            last = nc.tensor.transpose(bank[:, k * P:(k + 1) * P], wq[:, k, c * P:(c + 1) * P], ident[:, :])
                        last.then_inc(w_ready, 1)
                    pe.wait_ge(o2_ready, 1)
                    bank = claim(U_O2)
                    for k in range(KT):
                        last = nc.tensor.transpose(bank[:, k * P:(k + 1) * P], o2[:, k * P:(k + 1) * P], ident[:, :])
                    last.then_inc(w_ready, 1)
                    pe.wait_ge(c_weights_in, 64)
                    pe.wait_ge(w_free, U_O2 + 1)
                    for u, w in ((U_K, wk), (U_V, wv)):
                        bank = claim(u)
                        for c in range(KT):
                            for k in range(KT):
                                last = nc.tensor.matmul(bank[:, c * P:(c + 1) * P], w[:, k, c * P:(c + 1) * P], o2T[:, k * P:(k + 1) * P],
                                                        start=k == 0, stop=k == KT - 1)
                        last.then_inc(w_ready, 1)
                    pe.wait_ge(w_free, U_K + 1)
                    keys = lambda c: k_diag[:, c, :, :].rearrange("p b n -> p (b n)")
                    for c in range(KT):
                        nc.tensor.matmul(claim(U_BK + c)[:, :], bias["q"][:, c:c + 1].to_broadcast([P, P]), keys(c), start=True, stop=True).then_inc(w_ready, 1)
                    for k in range(KT):
                        for c in range(KT):
                            nc.tensor.matmul(claim(U_WK + k * KT + c)[:, :], wqT[:, c, k * P:(k + 1) * P], keys(c), start=True, stop=True).then_inc(w_ready, 1)
                    for b in range(B):
                        for t in range(HT):
                            bank = claim(U_VW + b * HT + t)
                            for c in (2 * t, 2 * t + 1):
                                last = nc.tensor.matmul(bank[:, :], v_diag[:, c, b, :], wo[:, c, :], start=c == 2 * t, stop=c == 2 * t + 1)
                            last.then_inc(w_ready, 1)

                def split_places():
                    for k in range(KT):
                        for c in range(KT):
                            cols = slice(c * CH * NS, (c + 1) * CH * NS)
                            yield U_WK + k * KT + c, [t[:, k, :, cols] for t in WK], True
                    for b in range(B):
                        for t in range(HT):
                            yield U_VW + b * HT + t, [x[:, b, t, :] for x in VW], False

                def as_place(u, heads):
                    return of_bank(u)[:, :].rearrange("p (b n) -> p b n", b=B) if heads else of_bank(u)[:, :]

                @block.gpsimd
                def _(pool):
                    nc.gpsimd.memset(k_diag[:, :, :, :], 0.0).then_inc(blocks_zero, 1)
                    nc.gpsimd.memset(v_diag[:, :, :, :], 0.0).then_inc(blocks_zero, 1)

                @block.scalar
                def _(act):
                    for u, (hi, _), heads in split_places():
                        act.wait_ge(w_ready, u + 1)
                        nc.scalar.copy(hi, as_place(u, heads)).then_inc(w_hi, 1)

                @block.vector
                def _(dve):
                    for c in range(KT):
                        dve.wait_ge(w_ready, U_WQ + c + 1)
                        nc.vector.tensor_copy(wqT[:, c, :], of_bank(U_WQ + c)[:, :]).then_inc(w_free, 1)
                    dve.wait_ge(slots_in, 2 * B * 16)
                    nc.vector.tensor_tensor(o2, o1[:, :], y_rows, ALU.add)
                    nc.vector.drain()
                    nc.vector.tensor_tensor(o2, o2, b2_rows, ALU.add).then_inc(o2_ready, 1)
                    dve.wait_ge(c_small_in, 4 * 16)
                    nc.vector.tensor_scalar(bo_gate[:, :], bo_gate[:, :], gates[:, 1:2], None, ALU.mult)
                    dve.wait_ge(w_ready, U_O2 + 1)
                    nc.vector.tensor_copy(o2T, of_bank(U_O2)[:, :]).then_inc(w_free, 1)
                    dve.wait_ge(blocks_zero, 2)
                    for u, n in ((U_K, "k"), (U_V, "v")):
                        dve.wait_ge(w_ready, u + 1)
                        for c in range(KT):
                            for g in range(CH):
                                rows = slice(g * SD, (g + 1) * SD)
                                src = of_bank(u)[rows, c * P:(c + 1) * P].rearrange("p (b s) -> p b s", b=B)
                                add = bias[n][rows, c:c + 1]
                                if n == "k":
                                    last = nc.vector.tensor_scalar(k_diag[rows, c, :, g * NS:(g + 1) * NS], src, add, SD ** -0.5, ALU.add, ALU.mult)
                                else:
                                    at = (c % 2) * CH * NS + g * NS
                                    last = nc.vector.tensor_scalar(v_diag[rows, c, :, at:at + NS], src, add, None, ALU.add)
                        last.then_inc(w_free, 1)
                    for c in range(KT):
                        dve.wait_ge(w_ready, U_BK + c + 1)
                        nc.vector.tensor_copy(bias_k[:, :, c * CH * NS:(c + 1) * CH * NS], as_place(U_BK + c, True)).then_inc(w_free, 1)
                    for n, (u, (hi, lo), heads) in enumerate(split_places()):
                        dve.wait_ge(w_hi, n + 1)
                        nc.vector.tensor_tensor(lo, as_place(u, heads), plain(hi), ALU.subtract).then_inc(w_free, 1)

        PB = TT // 2
        yT = [[mem.sbuf(f"c_yT_{part}{i}", [P, KT, S], F32R) for part in ("hi", "lo")] for i in range(2)]
        xs = [mem.sbuf(f"c_x{i}", [P, TT, D]) for i in range(2)]
        prob = [mem.sbuf(f"c_prob{i}", [P, PB, 2, HS]) for i in range(2)]
        pT = [mem.sbuf(f"c_pT_{part}", [P, PB, 2, HT, P], F32R) for part in ("hi", "lo")]
        top, total = (mem.sbuf(f"c_{n}", [P, PB, 2 * SH]) for n in ("top", "total"))
        SC = [mem.bank(f"c_scores{i}") for i in range(PB)]
        TB = [mem.bank(f"c_turned{i}") for i in range(PB)]
        OB = [mem.bank(f"c_out{i}") for i in range(TT)]
        yT_in, x_in, x_out = ([mem.sem(f"c_{n}{i}") for i in range(2)] for n in ("yT_in", "x_in", "x_out"))
        scored, shifted, exps, probs_ready, turned, p_hi, p_lo = (
            mem.sem(f"c_{n}") for n in ("scored", "shifted", "exps", "probs_ready", "turned", "p_hi", "p_lo"))
        bo_added, summed, x_done = (mem.sem(f"c_{n}") for n in ("bo_added", "summed", "x_done"))

        def of(ap, b):
            return ap[b] if isinstance(b, int) else ap[bass.ds(b, 1)].rearrange("o p t d -> (o p) t d")

        def arrived(b, i, size):
            return b * (size // 2) + (size - (size // 2) * i)

        def skewed(eng, front, back):
            front(0, 0)
            with eng.Fori(0, B // 2 - 1) as pair:
                for i in range(2):
                    front(pair * 2 + i + 1, 1 - i)
                    back(pair * 2 + i, i)
            front(B - 1, 1)
            back(B - 2, 0)
            back(B - 1, 1)

        with nc.Block() as block:
            @block.sync
            def _(sp):
                def load_y(b, i):
                    for part in range(2):
                        sp.dma_start(plain(yT[i][part][:, :, :]), of(yT_d[part], b)).then_inc(yT_in[i], 16)

                def load_x(b, i):
                    sp.dma_start(xs[i][:, :, :], of(x_v, b)).then_inc(x_in[i], 16)

                def after(b, i):
                    again, ahead = b + 2, b + 3
                    if not (isinstance(b, int) and ahead >= B):
                        sp.wait_ge(scored, (b + 2) * PB)
                        load_y(ahead, 1 - i)
                    sp.wait_ge(x_done, (b + 1) * TT)
                    sp.dma_start(of(out_v, b), xs[i][:, :, :]).then_inc(x_out[i], 16)
                    if not (isinstance(b, int) and again >= B):
                        sp.wait_ge(x_out[i], arrived(b, i, 16))
                        load_x(again, i)

                for i in range(2):
                    load_y(i, i)
                    load_x(i, i)
                sp.wait_ge(scored, PB)
                load_y(2, 0)
                with sp.Fori(0, B // 2 - 2) as pair:
                    for i in range(2):
                        after(pair * 2 + i, i)
                for b in range(B - 4, B):
                    after(b, b % 2)
                for i in range(2):
                    sp.wait_ge(x_out[i], B // 2 * 16)

            @block.gpsimd
            def _(pool):
                with pool.Fori(0, B // 2) as pair:
                    for i in range(2):
                        pool.wait_ge(x_in[i], pair * 16 + 16)
                        nc.gpsimd.tensor_tensor(xs[i][:, :, :], xs[i][:, :, :], bo_gate[:, :].unsqueeze(1).to_broadcast([P, TT, D]), ALU.add).then_inc(bo_added, 1)

            @block.tensor
            def _(pe):
                def scores(b, i):
                    pe.wait_ge(yT_in[i], arrived(b, i, 32))
                    for j in range(PB):
                        if not (isinstance(b, int) and b == 0):
                            pe.wait_ge(shifted, (b - 1) * PB + j + 1)
                        for t in range(2):
                            n = 0
                            tok = (2 * j + t) * P
                            for k in range(KT):
                                of_b = [w[:, k, b, :] if isinstance(b, int) else w[:, k, bass.ds(b, 1), :].rearrange("p o n -> p (o n)") for w in WK]
                                for a, w in products([y[:, k, tok:tok + P] for y in yT[i]], of_b):
                                    last = nc.tensor.matmul(SC[j][:, t * HS:(t + 1) * HS], a, w, start=n == 0, stop=n == 3 * KT - 1)
                                    n += 1
                        last.then_inc(scored, 1)

                def sums(b, i):
                    pe.wait_ge(p_lo, b * PB)
                    for j in range(PB):
                        pe.wait_ge(probs_ready, b * PB + j + 1)
                        for t in range(2):
                            for r in range(HT):
                                at = (t * HT + r) * P
                                last = nc.tensor.transpose(TB[j][:, at:at + P], prob[i][:, j, t, r * P:(r + 1) * P], ident[:, :])
                        last.then_inc(turned, 1)
                    pe.wait_ge(x_done, b * TT)
                    for t in range(TT):
                        j = t // 2
                        pe.wait_ge(p_lo, b * PB + j + 1)
                        n = 0
                        for r in range(HT):
                            of_b = [w[:, b, r, :] if isinstance(b, int) else w[:, bass.ds(b, 1), r, :].rearrange("p o n -> p (o n)") for w in VW]
                            for a, w in products([p[:, j, t % 2, r, :] for p in pT], of_b):
                                last = nc.tensor.matmul(OB[t][:, :], a, w, start=n == 0, stop=n == 3 * HT - 1)
                                n += 1
                        last.then_inc(summed, 1)

                skewed(pe, scores, sums)

            @block.scalar
            def _(act):
                def exp(b, i):
                    for j in range(PB):
                        act.wait_ge(shifted, b * PB + j + 1)
                        nc.scalar.activation(prob[i][:, j, :, :], prob[i][:, j, :, :], ACT.Exp).then_inc(exps, 1)

                def split(b, i):
                    if not (isinstance(b, int) and b == 0):
                        act.wait_ge(summed, b * TT)
                    for j in range(PB):
                        act.wait_ge(turned, b * PB + j + 1)
                        nc.scalar.copy(pT[0][:, j, :, :, :].rearrange("p t r n -> p (t r n)"), TB[j][:, :]).then_inc(p_hi, 1)

                skewed(act, exp, split)

            @block.vector
            def _(dve):
                by_head = lambda j, i: prob[i][:, j, :, :].rearrange("p t (h s) -> p (t h) s", s=NS)
                per_slot = lambda a: a.unsqueeze(2).to_broadcast([P, 2 * SH, NS])

                def shift(b, i):
                    for j in range(PB):
                        dve.wait_ge(scored, b * PB + j + 1)
                        add = bias_k[:, b:b + 1, :] if isinstance(b, int) else bias_k[:, bass.ds(b, 1), :]
                        nc.vector.tensor_tensor(prob[i][:, j, :, :], SC[j][:, :].rearrange("p (t n) -> p t n", t=2),
                                                add.to_broadcast([P, 2, HS]), ALU.add)
                        nc.vector.drain()
                        nc.vector.tensor_reduce(top[:, j, :], by_head(j, i), AX.X, ALU.max)
                        nc.vector.drain()
                        nc.vector.tensor_tensor(by_head(j, i), by_head(j, i), per_slot(top[:, j, :]), ALU.subtract).then_inc(shifted, 1)

                def normalise(b, i):
                    for j in range(PB):
                        dve.wait_ge(exps, b * PB + j + 1)
                        nc.vector.tensor_reduce(total[:, j, :], by_head(j, i), AX.X, ALU.add)
                        nc.vector.drain()
                        nc.vector.reciprocal(total[:, j, :], total[:, j, :])
                        nc.vector.drain()
                        nc.vector.tensor_tensor(by_head(j, i), by_head(j, i), per_slot(total[:, j, :]), ALU.mult).then_inc(probs_ready, 1)

                def finish(b, i):
                    for j in range(PB):
                        dve.wait_ge(p_hi, b * PB + j + 1)
                        flat = [p[:, j, :, :, :].rearrange("p t r n -> p (t r n)") for p in pT]
                        nc.vector.tensor_tensor(flat[1], TB[j][:, :], plain(flat[0]), ALU.subtract).then_inc(p_lo, 1)
                    dve.wait_ge(bo_added, b + 1)
                    for t in range(TT):
                        dve.wait_ge(summed, b * TT + t + 1)
                        nc.vector.scalar_tensor_tensor(xs[i][:, t, :], OB[t][:, :], gates[:, 1:2], xs[i][:, t, :], ALU.mult, ALU.add).then_inc(x_done, 1)

                shift(0, 0)
                normalise(0, 0)
                with dve.Fori(0, B // 2 - 1) as pair:
                    for i in range(2):
                        shift(pair * 2 + i + 1, 1 - i)
                        finish(pair * 2 + i, i)
                        normalise(pair * 2 + i + 1, 1 - i)
                shift(B - 1, 1)
                finish(B - 2, 0)
                normalise(B - 1, 1)
                finish(B - 1, 1)


def gated_block(nc, I, out):
    scratch = lambda name, shape: nc.dram_tensor(name, shape, F32, kind="Internal").ap()
    x1_d = scratch("x1", [B, S, D])
    xnT_d = scratch("xnT", [2, B, P, KT, S])
    y_d = scratch("slot_y", [E, B, D])
    with ExitStack() as whole:
        sbuf = lambda stack, name, shape: stack.enter_context(nc.sbuf_tensor(name, shape, F32))
        ident, ones, gates = sbuf(whole, "ident", [P, P]), sbuf(whole, "ones", [1, P]), sbuf(whole, "gates", [P, 2])
        cross_attention(nc, whole, I, ident, ones, gates, x1_d, xnT_d)
        o1 = sbuf(whole, "o1", [P, D])
        with ExitStack() as until_experts:
            hT = sbuf(until_experts, "hT", [P, KT, E, B])
            with ExitStack() as until_slots:
                x_stats = sbuf(until_slots, "x_stats", [P, B * TT, 6])
                feed_forward(nc, whole, I, gates, x_stats, x1_d, xnT_d)
                slot_attention(nc, whole, I, ident, ones, x_stats, o1, hT, x1_d, xnT_d)
            experts(nc, whole, I, ident, hT, y_d)
        token_attention(nc, whole, I, ident, gates, o1, x1_d, xnT_d, y_d, out)


INPUTS = ["x", "ctx_1024", "mask_BxS2_ik0", "g_xattn", "g_ffn"] + [f"L0_xattn_{n}" for n in (
    "gamma", "ctx_gamma", "Wq", "Wkv", "Wout", "Wff1", "Wff2")] + ["L0_ffn_slot_query"] + [
    f"L0_ffn_{a}_{w}{n}" for a in "dc" for w in "Wb" for n in "qkvo"] + [
    f"L0_ffn_e_{n}" for n in ("ln_g", "ln_b", "W1", "b1", "Wg", "bg", "W2", "b2")]


def kernel(**inputs):
    import numpy as np
    import concourse.bacc as bacc
    from concourse.bass_utils import run_bass_kernel_spmd

    nc = bacc.Bacc("TRN2", target_bir_lowering=False, num_devices=1)
    arrays, I = {}, {}
    for name in INPUTS:
        a = np.ascontiguousarray(inputs[name])
        arrays[f"in_{name}"] = a
        I[name] = nc.dram_tensor(f"in_{name}", a.shape, mybir.dt.from_np(a.dtype), kind="ExternalInput").ap()
    out = nc.dram_tensor("out", [B, S, D], F32, kind="ExternalOutput").ap()
    gated_block(nc, I, out)
    return run_bass_kernel_spmd(nc, [arrays], core_ids=[0]).results[0]["out"]
```

```python
import concourse.bass as bass
from concourse import mybir
from contextlib import ExitStack

F32 = mybir.dt.float32
F32R = mybir.dt.float32r
I32 = mybir.dt.int32
ALU = mybir.AluOpType
ACT = mybir.ActivationFunctionType
AX = mybir.AxisListType

P = 128
B, S, D = 8, 512, 512
KT = D // P
TT = S // P
H, DH = 16, 64
HP = H // 2
FF = 2048
NS, E = 16, 16
SH, SD = 16, 32
HS = SH * NS
EPS = 1e-5
MASKED = -1e30
LOWEST = -3e38


def plain(ap):
    return ap.bitcast(F32)


def products(hi_lo_w, hi_lo_m):
    (w_hi, w_lo), (m_hi, m_lo) = hi_lo_w, hi_lo_m
    return ((w_hi, m_hi), (w_hi, m_lo), (w_lo, m_hi))


class Memory:

    def __init__(self, nc, stage, whole):
        self.nc, self.stage, self.whole = nc, stage, whole

    def sbuf(self, name, shape, dtype=F32):
        return self.stage.enter_context(self.nc.sbuf_tensor(name, shape, dtype))

    def bank(self, name):
        return self.stage.enter_context(self.nc.psum_tensor(name, [P, 512], F32))

    def sem(self, name):
        return self.whole.enter_context(self.nc.semaphore(name))


def rows_mean_var(nc, stats, mean, var, half):
    col = lambda i: stats[:, :, i:i + 1].rearrange("p n o -> p (n o)")
    v = nc.vector
    v.tensor_tensor(half, col(1), col(4), ALU.subtract)
    v.tensor_tensor(mean, col(1), col(4), ALU.add)
    v.tensor_tensor(var, col(2), col(5), ALU.add)
    v.drain()
    v.tensor_scalar(mean, mean, 0.5, None, ALU.mult)
    v.tensor_scalar(half, half, 0.5, None, ALU.mult)
    v.tensor_scalar(var, var, 1.0 / D, None, ALU.mult)
    v.drain()
    v.tensor_tensor(half, half, half, ALU.mult)
    v.drain()
    v.tensor_tensor(var, var, half, ALU.add)
    v.drain()


def cross_attention(nc, whole, I, ident, ones, gates, x1_d, xnT_d):
    with ExitStack() as stage:
        mem = Memory(nc, stage, whole)
        x_v = I["x"].rearrange("b (t p) d -> b p t d", p=P)
        c_v = I["ctx_1024"].rearrange("b (t p) d -> b p t d", p=P)
        x1_v = x1_d.rearrange("b (t p) d -> b p t d", p=P)
        mask = I["mask_BxS2_ik0"]

        wq_hi = mem.sbuf("wq_hi", [P, KT, H * DH], F32R)
        wq_lo = mem.sbuf("wq_lo", [P, KT, H * DH], F32R)
        wkv_hi = mem.sbuf("wkv_hi", [P, KT, 4 * DH], F32R)
        wkv_lo = mem.sbuf("wkv_lo", [P, KT, 4 * DH], F32R)
        wo_hi = mem.sbuf("wo_hi", [P, HP, D], F32R)
        wo_lo = mem.sbuf("wo_lo", [P, HP, D], F32R)
        gam = mem.sbuf("gam", [P, 2, KT])
        sel_max = mem.sbuf("sel_max", [P, H, P], F32R)
        sel_sum = mem.sbuf("sel_sum", [P, 2 * P - 1], F32R)
        sel_pair = mem.sbuf("sel_pair", [P, HP, P], F32R)
        key_bias = mem.sbuf("key_bias", [P, B * TT])
        block_bias = mem.sbuf("block_bias", [P, TT])
        live = mem.sbuf("live", [1, B * TT], I32)
        live_f = mem.sbuf("live_f", [1, B * TT])
        stats = mem.sbuf("stats", [P, 2 * TT, 6])
        mean, var, spread, rstd = (mem.sbuf(n, [P, 2 * TT]) for n in ("mean", "var", "spread", "rstd"))
        cin = mem.sbuf("cin", [P, TT, D])
        xin = mem.sbuf("xin", [P, TT, D])
        nT_hi = mem.sbuf("nT_hi", [P, KT, S], F32R)
        nT_lo = mem.sbuf("nT_lo", [P, KT, S], F32R)
        kk_hi = mem.sbuf("kk_hi", [P, S], F32R)
        kk_lo = mem.sbuf("kk_lo", [P, S], F32R)
        vT = mem.sbuf("vT", [P, S])
        val = mem.sbuf("val", [P, TT, 4, P], F32R)
        qs = mem.sbuf("qs", [P, H, S], F32R)
        oT_hi, oT_lo = qs[:, 0:HP, :], qs[:, HP:H, :]
        mask_b = mem.sbuf("mask_b", [P, S])
        mask_i = mask_b[:, :].bitcast(I32)
        m_rows = mem.sbuf("m_rows", [P, TT, H])
        m_heads = mem.sbuf("m_heads", [P, S], F32R)
        prob = mem.sbuf("prob", [P, 2, S])
        prob_hi = mem.sbuf("prob_hi", [P, 2, S], F32R)
        prob_lo = mem.sbuf("prob_lo", [P, 2, S], F32R)
        acc = mem.sbuf("acc", [P, HP, S])
        acc_sum = mem.sbuf("acc_sum", [P, S])
        inv_hi = mem.sbuf("inv_hi", [P, S], F32R)
        inv_lo = mem.sbuf("inv_lo", [P, S], F32R)
        xres = mem.sbuf("xres", [P, 2, D])
        mask_rows, bias_rows = acc_sum[0:B * TT, 0:P].bitcast(I32), vT[0:B * TT, 0:P]
        x_rows = [xres[:, 0, :], xres[:, 1, :], prob[:, 0, :], prob[:, 1, :]]
        raw = [t[:, 2 * i:2 * i + 2, :].rearrange("p t d -> p (t d)") for t in (cin, xin) for i in range(2)]
        RAW = len(raw)

        G = [mem.bank(f"att_general{i}") for i in range(3)]
        SC = [mem.bank(f"att_scores{i}") for i in range(2)]
        OB = [mem.bank(f"att_out{i}") for i in range(2)]
        SUM = mem.bank("att_sum")
        OUT = OB + [SUM, SC[1]]
        MX = SC + OB

        raw_in = [mem.sem(f"raw_in{i}") for i in range(RAW)]
        w_hi_done, w_lo_done = mem.sem("w_hi_done"), mem.sem("w_lo_done")
        small_in, mask_in, masks_ready, masks_turned = (mem.sem(n) for n in ("small_in", "mask_in", "masks_ready", "masks_turned"))
        ident_zero, ident_ready = mem.sem("ident_zero"), mem.sem("ident_ready")

        wkv_v = I["L0_xattn_Wkv"].rearrange("(k p) n -> p k n", p=P)
        wo_v = I["L0_xattn_Wout"].rearrange("(i p) n -> p i n", p=P)
        chunks = [(wq_hi[:, k, :], wq_lo[:, k, :]) for k in range(KT)]
        chunks.append((wkv_hi[:, :, :].rearrange("p k n -> p (k n)"), wkv_lo[:, :, :].rearrange("p k n -> p (k n)")))
        chunks += [(wo_hi[:, 2 * i:2 * i + 2, :].rearrange("p i n -> p (i n)"),
                    wo_lo[:, 2 * i:2 * i + 2, :].rearrange("p i n -> p (i n)")) for i in range(HP // 2)]
        arrivals, landed = [0] * RAW, []
        for c in range(len(chunks)):
            arrivals[c % RAW] += 64 if c == KT else 16
            landed.append(arrivals[c % RAW])

        with nc.Block() as block:
            @block.sync
            def _(sp):
                sp.dma_start(gates[:, 0:1], I["g_xattn"].unsqueeze(0).to_broadcast([P, 1])).then_inc(small_in, 16)
                sp.dma_start(gates[:, 1:2], I["g_ffn"].unsqueeze(0).to_broadcast([P, 1])).then_inc(small_in, 16)
                sp.dma_start(gam[:, 0, :], I["L0_xattn_gamma"].rearrange("(k p) -> p k", p=P), allow_slow_non_contiguous=True).then_inc(small_in, 16)
                sp.dma_start(gam[:, 1, :], I["L0_xattn_ctx_gamma"].rearrange("(k p) -> p k", p=P), allow_slow_non_contiguous=True).then_inc(small_in, 16)
                sp.dma_start(mask_rows, mask.rearrange("b (j p) -> (b j) p", p=P)).then_inc(mask_in, 16)
                sp.dma_start(acc[0:1, :, :].bitcast(I32).rearrange("o i s -> o (i s)"),
                             mask.rearrange("b s -> (b s)").unsqueeze(0)).then_inc(mask_in, 16)
                for c in range(len(chunks)):
                    if c >= RAW:
                        sp.wait_ge(w_lo_done, c - RAW + 1)
                    slot = raw[c % RAW]
                    if c < KT:
                        sp.dma_start(slot, I["L0_xattn_Wq"][c * P:(c + 1) * P, :]).then_inc(raw_in[c % RAW], 16)
                    elif c == KT:
                        four = slot.rearrange("p (k n) -> p k n", k=KT)
                        for n in range(4):
                            sp.dma_start(four[:, :, n * DH:(n + 1) * DH],
                                         wkv_v[:, :, (n // 2) * DH:(n // 2 + 1) * DH]).then_inc(raw_in[c % RAW], 16)
                    else:
                        i = 2 * (c - KT - 1)
                        sp.dma_start(slot.rearrange("p (i n) -> p i n", i=2), wo_v[:, i:i + 2, :]).then_inc(raw_in[c % RAW], 16)
                sp.wait_ge(w_lo_done, len(chunks))

            @block.gpsimd
            def _(pool):
                nc.gpsimd.memset(ident[:, :], 0.0).then_inc(ident_zero, 1)
                pool.wait_ge(ident_zero, 1)
                nc.gpsimd.affine_select(out=ident[:, :], in_=ident[:, :], compare_op=ALU.not_equal, fill=1.0,
                                        base=0, pattern=[[-1, P]], channel_multiplier=1).then_inc(ident_ready, 1)

            @block.scalar
            def _(act):
                for c, (hi, _) in enumerate(chunks):
                    act.wait_ge(raw_in[c % RAW], landed[c])
                    nc.scalar.copy(hi, raw[c % RAW]).then_inc(w_hi_done, 1)
                act.wait_ge(small_in, 64)
                nc.scalar.activation(gates[:, :], gates[:, :], ACT.Tanh)

            @block.vector
            def _(dve):
                for c, (hi, lo) in enumerate(chunks):
                    dve.wait_ge(w_hi_done, c + 1)
                    nc.vector.tensor_tensor(lo, raw[c % RAW], plain(hi), ALU.subtract).then_inc(w_lo_done, 1)
                dve.wait_ge(mask_in, 32)
                nc.vector.tensor_scalar(bias_rows, mask_rows, 0.0, MASKED, ALU.is_equal, ALU.mult).then_inc(masks_ready, 1)
                flat = acc[0:1, :, :].rearrange("o i s -> o (i s)")
                nc.vector.tensor_scalar(flat, flat.bitcast(I32), 0.0, None, ALU.not_equal)
                nc.vector.drain()
                nc.vector.tensor_reduce(live_f[:, :], flat.rearrange("o (n p) -> o n p", p=P), AX.X, ALU.max)
                nc.vector.drain()
                nc.vector.tensor_copy(live[:, :], live_f[:, :])
                dve.wait_ge(ident_ready, 1)
                nc.vector.memset(ones[:, :], 1.0)
                nc.vector.memset(plain(m_heads[:, :]), 0.0)
                nc.vector.memset(plain(inv_hi[:, :]), 0.0)
                nc.vector.memset(plain(inv_lo[:, :]), 0.0)
                nc.vector.memset(plain(val[:, :, :, :]), 0.0)
                nc.vector.memset(plain(sel_sum[:, :]), 0.0)
                nc.vector.memset(prob[:, 0, 0:P], 0.0)
                nc.vector.drain()
                nc.vector.memset(plain(sel_sum[:, P - 1:P]), 1.0)
                zeros = prob[:, 0, 0:P]
                for h in range(H):
                    nc.vector.tensor_scalar(sel_max[:, h, :], zeros, ident[:, h:h + 1], -1.0, ALU.add, ALU.mult)
                    nc.vector.tensor_scalar(sel_pair[:, h // 2, (h % 2) * DH:(h % 2 + 1) * DH], zeros[:, 0:DH],
                                            ident[:, h:h + 1], None, ALU.add)
                dve.wait_ge(masks_turned, 1)
                nc.vector.tensor_copy(key_bias[:, :], G[0][:, 0:B * TT])

            @block.tensor
            def _(pe):
                pe.wait_ge(masks_ready, 1)
                pe.wait_ge(ident_ready, 1)
                nc.tensor.transpose(G[0][:, 0:B * TT], bias_rows, ident[0:B * TT, 0:B * TT]).then_inc(masks_turned, 1)

        ctx_in, x_in, mask_b_in = (mem.sem(n) for n in ("ctx_in", "x_in", "mask_b_in"))
        xres_in, x1_out, xnT_out = (mem.sem(n) for n in ("xres_in", "x1_out", "xnT_out"))
        var_ready, sd_ready, rstd_ready, norm_begun = (mem.sem(n) for n in ("var_ready", "sd_ready", "rstd_ready", "norm_begun"))
        normed = mem.sem("normed")
        g_ready, g_free = mem.sem("g_ready"), mem.sem("g_free")
        g_hi = mem.sem("g_hi")
        max_scores, max_taken, m_ready, m_turned, m_heads_ready = (
            mem.sem(n) for n in ("max_scores", "max_taken", "m_ready", "m_turned", "m_heads_ready"))
        max_begun = mem.sem("max_begun")
        scores, exps, low_probs, head_out, out_taken = (
            mem.sem(n) for n in ("scores", "exps", "low_probs", "head_out", "out_taken"))
        acc_begun, acc_clear, inv_ready, o_hi_done, o_lo_done, out_ready, x_added = (
            mem.sem(n) for n in ("acc_begun", "acc_clear", "inv_ready", "o_hi_done", "o_lo_done", "out_ready", "x_added"))

        U_V, U_VAL = 0, 3
        U_SPREAD = [1, 2, 4, 6, 8, 10, 12, 13]
        U_X = [5, 7, 9, 11]
        U_Q = 14
        U_CTX = U_Q + HP
        U_K = U_CTX + KT
        PER = U_K + 1
        NG = len(G)
        assert PER % NG == 0
        HI_K, HI_VAL, HI_X, HI_Q = 0, 1, 3, 3 + KT
        HI_CTX = HI_Q + 2 * HP
        HI = HI_CTX + KT
        OUTS = HP + 1
        q_scale = DH ** -0.5

        def of(ap, b):
            return ap[b] if isinstance(b, int) else ap[bass.ds(b, 1)].rearrange("o p t d -> (o p) t d")

        def first(b):
            return isinstance(b, int) and b == 0

        def last_batch(b):
            return isinstance(b, int) and b == B - 1

        def used(b, u):
            return (b + 1) * PER + u

        def tail_steps(begin, end, values, x):
            begin(0)
            begin(1)
            values()
            for i in range(HP):
                end(i)
                if i + 2 < HP:
                    begin(i + 2)
                if i < KT:
                    x(i)

        with nc.Block() as block:
            @block.sync
            def _(sp):
                def context(b, nxt):
                    sp.wait_ge(g_ready, used(b, U_K))
                    sp.dma_start(cin[:, :, :], of(c_v, nxt)).then_inc(ctx_in, 16)

                def rows(b, nxt):
                    sp.wait_ge(g_ready, used(b, U_X[-1] + 1))
                    sp.dma_start(xin[:, :, :], of(x_v, nxt)).then_inc(x_in, 16)

                def next_mask(b, nxt):
                    sp.wait_ge(max_taken, (b + 1) * (TT * HP))
                    src = mask[nxt:nxt + 1, :] if isinstance(nxt, int) else mask[bass.ds(nxt, 1), :]
                    sp.dma_start(mask_i, src.to_broadcast([P, S])).then_inc(mask_b_in, 16)

                def keep_xnT(b):
                    sp.wait_ge(g_free, used(b, U_X[-1] + 1))
                    for part, t in enumerate((nT_hi, nT_lo)):
                        sp.dma_start(of(xnT_d[part], b), plain(t[:, :, :])).then_inc(xnT_out, 16)

                def residual(b, prev):
                    sp.wait_ge(out_taken, b * (TT * OUTS))
                    for t in range(TT):
                        sp.dma_start(x_rows[t], of(x_v, prev)[:, t, :]).then_inc(xres_in, 16)

                def store(b, prev):
                    for t in range(TT):
                        sp.wait_ge(x_added, (b - 1) * TT + t + 1)
                        sp.dma_start(of(x1_v, prev)[:, t, :], x_rows[t]).then_inc(x1_out, 16)

                sp.dma_start(cin[:, :, :], c_v[0]).then_inc(ctx_in, 16)
                sp.dma_start(xin[:, :, :], x_v[0]).then_inc(x_in, 16)
                sp.dma_start(mask_i, mask[0:1, :].to_broadcast([P, S])).then_inc(mask_b_in, 16)
                context(-1, 1)
                rows(0, 1)
                keep_xnT(0)
                context(0, 2)
                next_mask(0, 1)
                with sp.Fori(1, B - 2) as b:
                    residual(b, b - 1)
                    rows(b, b + 1)
                    keep_xnT(b)
                    store(b, b - 1)
                    context(b, b + 2)
                    next_mask(b, b + 1)
                residual(B - 2, B - 3)
                rows(B - 2, B - 1)
                keep_xnT(B - 2)
                store(B - 2, B - 3)
                next_mask(B - 2, B - 1)
                residual(B - 1, B - 2)
                keep_xnT(B - 1)
                store(B - 1, B - 2)
                residual(B, B - 1)
                store(B, B - 1)
                sp.wait_ge(x1_out, B * (TT * 16))
                sp.wait_ge(xnT_out, B * 32)

            @block.tensor
            def _(pe):
                def claim(b, u):
                    pe.wait_ge(g_free, used(b, u - (NG - 1)))
                    return G[u % NG]

                def skip(uses):
                    pe.drain().then_inc(g_ready, uses)

                def turn(b, u, src, k):
                    bank = claim(b, u)
                    for t in range(TT):
                        last = nc.tensor.transpose(bank[:, t * P:(t + 1) * P], src[:, t, k * P:(k + 1) * P], ident[:, :])
                    last.then_inc(g_ready, 1)

                def project(bank, cols, w_hi, w_lo):
                    n = 0
                    for k in range(KT):
                        for w, m in products((w_hi, w_lo), (nT_hi, nT_lo)):
                            last = nc.tensor.matmul(bank[:, :], w[:, k, cols], m[:, k, :], start=n == 0, stop=n == 3 * KT - 1)
                            n += 1
                    return last

                def context(b):
                    pe.wait_ge(normed, 2 * b + 3)
                    for k in range(KT):
                        turn(b, U_CTX + k, cin, k)

                def keys(b):
                    pe.wait_ge(g_free, used(b, U_K))
                    project(claim(b, U_K), slice(0, 2 * DH), wkv_hi, wkv_lo).then_inc(g_ready, 1)

                def values(b):
                    project(claim(b, U_V), slice(2 * DH, 4 * DH), wkv_hi, wkv_lo).then_inc(g_ready, 1)

                def tail(b):
                    def spread_inverse(i):
                        if first(b):
                            skip(1)
                            return
                        if i == 0:
                            pe.wait_ge(inv_ready, b)
                        bank = claim(b, U_SPREAD[i])
                        nc.tensor.matmul(bank[:, :], sel_pair[:, i, :], inv_hi[:, :], start=True, stop=False)
                        nc.tensor.matmul(bank[:, :], sel_pair[:, i, :], inv_lo[:, :], start=False, stop=True).then_inc(g_ready, 1)

                    def output(i):
                        if first(b):
                            return
                        pe.wait_ge(o_lo_done, (b - 1) * HP + i + 1)
                        for t in range(TT):
                            for n, (o, w) in enumerate(products((oT_hi, oT_lo), (wo_hi, wo_lo))):
                                last = nc.tensor.matmul(OUT[t][:, :], o[:, i, t * P:(t + 1) * P], w[:, i, :],
                                                        start=i == 0 and n == 0, stop=i == HP - 1 and n == 2)
                        if i == HP - 1:
                            last.then_inc(out_ready, 1)

                    def turn_values():
                        if b is B:
                            skip(1)
                            return
                        bank = claim(b, U_VAL)
                        for j in range(TT):
                            last = nc.tensor.transpose(bank[:, j * P:(j + 1) * P], vT[:, j * P:(j + 1) * P], ident[:, :])
                        last.then_inc(g_ready, 1)

                    def turn_x(k):
                        if b is B:
                            skip(1)
                            return
                        if k == 0:
                            pe.wait_ge(normed, 2 * b + 2)
                        turn(b, U_X[k], xin, k)

                    tail_steps(spread_inverse, output, turn_values, turn_x)

                def queries(b):
                    pe.wait_ge(g_free, used(b, U_X[-1] + 1))
                    for i in range(HP):
                        project(claim(b, U_Q + i), slice(i * P, (i + 1) * P), wq_hi, wq_lo).then_inc(g_ready, 1)

                def maxima(b, on):
                    pe.wait_ge(exps, b * (TT * H))
                    if not first(b):
                        pe.wait_ge(x_added, b * TT)
                    for j in range(TT):
                        n = b * TT + j
                        with pe.If(on[j] == 1):
                            for i in range(HP):
                                pe.wait_ge(g_free, used(b, U_Q + i + 1))
                                pe.wait_ge(max_taken, n * HP + max(i - 1, 0))
                                for h in (2 * i, 2 * i + 1):
                                    for t in range(TT):
                                        last = nc.tensor.matmul(MX[h % 4][:, t * P:(t + 1) * P], qs[:, h, t * P:(t + 1) * P],
                                                                kk_hi[:, j * P:(j + 1) * P], start=True, stop=True)
                                last.then_inc(max_scores, 1)
                        with pe.Else():
                            pe.drain().then_inc(max_scores, HP)
                            pe.drain().then_inc(max_taken, HP)

                def turn_maxima(b):
                    pe.wait_ge(m_ready, b + 1)
                    for t in range(TT):
                        last = nc.tensor.transpose(SC[0][0:H, t * P:(t + 1) * P], m_rows[:, t, :], ident[:, :])
                    last.then_inc(m_turned, 1)

                def attend(b, on):
                    pe.wait_ge(m_heads_ready, b + 1)
                    pe.wait_ge(max_taken, (b + 1) * (TT * HP))
                    for j in range(TT):
                        n = b * TT + j
                        keys = slice(j * P, (j + 1) * P)
                        with pe.If(on[j] == 1):
                            for h in range(H + 1):
                                if h < H:
                                    pe.wait_ge(exps, n * H + max(h - 1, 0))
                                    bank = SC[h % 2]
                                    nc.tensor.matmul(bank[:, :], kk_hi[:, keys], qs[:, h, :], start=True, stop=False)
                                    nc.tensor.matmul(bank[:, :], kk_lo[:, keys], qs[:, h, :], start=False, stop=False)
                                    nc.tensor.matmul(bank[:, :], sel_max[:, h, :], m_heads[:, :], start=False, stop=True).then_inc(scores, 1)
                                if h >= 1:
                                    g = h - 1
                                    i, odd, s = g // 2, g % 2, g % 2
                                    pe.wait_ge(low_probs, n * H + g + 1)
                                    if odd == 0:
                                        pe.wait_ge(out_taken, n * OUTS + max(i - 1, 0))
                                    v_hi, v_lo = val[:, j, odd, :], val[:, j, 2 + odd, :]
                                    nc.tensor.matmul(OB[i % 2][:, :], v_hi, prob_hi[:, s, :], start=not odd, stop=False)
                                    nc.tensor.matmul(OB[i % 2][:, :], v_hi, prob_lo[:, s, :], start=False, stop=False)
                                    nc.tensor.matmul(OB[i % 2][:, :], v_lo, prob_hi[:, s, :], start=False, stop=bool(odd))
                                    one = sel_sum[:, P - 1 - g:2 * P - 1 - g]
                                    nc.tensor.matmul(SUM[:, :], one, prob_hi[:, s, :], start=g == 0, stop=False)
                                    nc.tensor.matmul(SUM[:, :], one, prob_lo[:, s, :], start=False, stop=g == H - 1).then_inc(head_out, 1)
                        with pe.Else():
                            pe.drain().then_inc(scores, H)
                            pe.drain().then_inc(head_out, H)

                def flags(b):
                    return [pe.value_load(live[0:1, bass.ds(b * TT + j, 1)]) for j in range(TT)]

                def batch(b):
                    values(b)
                    tail(b)
                    on = flags(b)
                    queries(b)
                    if last_batch(b):
                        skip(KT + 1)
                    else:
                        context(b)
                    maxima(b, on)
                    if not last_batch(b):
                        keys(b)
                    turn_maxima(b)
                    attend(b, on)

                skip(U_CTX)
                context(-1)
                keys(-1)
                batch(0)
                with pe.Fori(1, B - 1) as b:
                    batch(b)
                batch(B - 1)
                skip(1)
                tail(B)

            @block.scalar
            def _(act):
                def context(b):
                    if not (isinstance(b, int) and b < 0):
                        act.wait_ge(xnT_out, (b + 1) * 32)
                    for k in range(KT):
                        act.wait_ge(g_ready, used(b, U_CTX + k + 1))
                        nc.scalar.activation(nT_hi[:, k, :], G[(U_CTX + k) % NG][:, :], ACT.Copy, scale=gam[:, 1, k:k + 1]).then_inc(g_hi, 1)

                def keys(b):
                    act.wait_ge(g_ready, used(b, U_V + 1))
                    nc.scalar.copy(kk_hi[:, :], G[U_K % NG][:, :]).then_inc(g_hi, 1)

                def tail(b):
                    def high(i):
                        if first(b):
                            return
                        act.wait_ge(g_free, used(b, U_SPREAD[i] + 1))
                        nc.scalar.copy(oT_hi[:, i, :], acc[:, i, :]).then_inc(o_hi_done, 1)

                    def values():
                        if b is B:
                            return
                        act.wait_ge(g_ready, used(b, U_VAL + 1))
                        turned = G[U_VAL % NG][:, :].rearrange("p (j v) -> p j v", j=TT)
                        for odd in range(2):
                            cols = slice(odd * DH, (odd + 1) * DH)
                            nc.scalar.copy(val[:, :, odd, cols], turned[:, :, cols]).then_inc(g_hi, 1)

                    def x(k):
                        if b is B:
                            return
                        act.wait_ge(g_ready, used(b, U_X[k] + 1))
                        nc.scalar.activation(nT_hi[:, k, :], G[U_X[k] % NG][:, :], ACT.Copy, scale=gam[:, 0, k:k + 1]).then_inc(g_hi, 1)

                    tail_steps(high, lambda i: None, values, x)

                def deviations(b):
                    act.wait_ge(var_ready, b + 1)
                    nc.scalar.activation(spread[:, :], spread[:, :], ACT.Sqrt).then_inc(sd_ready, 1)

                def queries(b):
                    for i in range(HP):
                        if i == HP - 1 and not first(b):
                            act.wait_ge(x1_out, b * (TT * 16))
                        act.wait_ge(g_ready, used(b, U_Q + i + 1))
                        for odd in range(2):
                            half = slice(odd * DH, (odd + 1) * DH)
                            nc.scalar.activation(qs[half, 2 * i + odd, :], G[(U_Q + i) % NG][half, :], ACT.Copy, scale=q_scale).then_inc(g_hi, 1)

                def attend(b, on):
                    for j in range(TT):
                        n = b * TT + j
                        with act.If(on[j] == 1):
                            bias = block_bias[:, j:j + 1]
                            nc.scalar.copy(bias, key_bias[:, bass.ds(n, 1)])
                            act.drain()
                            for h in range(H):
                                act.wait_ge(scores, n * H + h + 1)
                                act.wait_ge(head_out, n * H + max(h - 1, 0))
                                nc.scalar.activation(prob[:, h % 2, :], SC[h % 2][:, :], ACT.Exp, bias=bias)
                                nc.scalar.activation(prob_hi[:, h % 2, :], SC[h % 2][:, :], ACT.Exp, bias=bias).then_inc(exps, 1)
                        with act.Else():
                            act.drain().then_inc(exps, H)

                def flags(b):
                    return [act.value_load(live[0:1, bass.ds(b * TT + j, 1)]) for j in range(TT)]

                def batch(b):
                    keys(b)
                    tail(b)
                    if not last_batch(b):
                        deviations(b + 1)
                    queries(b)
                    if not last_batch(b):
                        context(b)
                    attend(b, flags(b))

                act.drain().then_inc(g_hi, HI_CTX)
                deviations(0)
                context(-1)
                batch(0)
                with act.Fori(1, B - 1) as b:
                    batch(b)
                batch(B - 1)
                tail(B)

            @block.gpsimd
            def _(pool):
                def clear():
                    nc.gpsimd.memset(acc[:, :, :], 0.0).then_inc(acc_clear, 1)

                def norm(b):
                    pool.wait_ge(rstd_ready, b + 1)
                    pool.sem_inc(norm_begun, 1)
                    for c, src in enumerate((cin, xin)):
                        for t in range(TT):
                            n = c * TT + t
                            last = nc.gpsimd.tensor_scalar(src[:, t, :], src[:, t, :], mean[:, n:n + 1], rstd[:, n:n + 1], ALU.subtract, ALU.mult)
                        last.then_inc(normed, 1)

                def clear_after(b):
                    pool.wait_ge(o_lo_done, b * HP)
                    pool.sem_inc(acc_begun, 1)
                    clear()

                clear()
                norm(0)
                norm(1)
                with pool.Fori(1, B - 1) as b:
                    clear_after(b)
                    norm(b + 1)
                clear_after(B - 1)

            @block.vector
            def _(dve):
                def statistics(b):
                    dve.wait_ge(ctx_in, b * 16 + 16)
                    for t in range(TT):
                        nc.vector.bn_stats(stats[:, t, :], cin[:, t, :])
                    dve.wait_ge(x_in, b * 16 + 16)
                    for t in range(TT):
                        nc.vector.bn_stats(stats[:, TT + t, :], xin[:, t, :])
                    nc.vector.drain()
                    rows_mean_var(nc, stats[:, :, :], mean[:, :], var[:, :], spread[:, :])
                    nc.vector.tensor_scalar(spread[:, 0:TT], var[:, 0:TT], EPS, None, ALU.add)
                    nc.vector.tensor_scalar(spread[:, TT:2 * TT], var[:, TT:2 * TT], 1 + EPS, EPS * EPS, ALU.mult, ALU.add).then_inc(var_ready, 1)

                def deviations(b):
                    dve.wait_ge(sd_ready, b + 1)
                    nc.vector.reciprocal(rstd[:, :], spread[:, :]).then_inc(rstd_ready, 1)

                def context(b):
                    for k in range(KT):
                        dve.wait_ge(g_hi, (b + 1) * HI + HI_CTX + k + 1)
                        nc.vector.scalar_tensor_tensor(nT_lo[:, k, :], G[(U_CTX + k) % NG][:, :], gam[:, 1, k:k + 1],
                                                       plain(nT_hi[:, k, :]), ALU.mult, ALU.subtract).then_inc(g_free, 1)

                def inverse(b):
                    nc.vector.reciprocal(acc_sum[0:H, :], acc_sum[0:H, :])
                    nc.vector.drain()
                    nc.vector.tensor_copy(inv_hi[0:H, :], acc_sum[0:H, :])
                    nc.vector.drain()
                    nc.vector.tensor_tensor(inv_lo[0:H, :], acc_sum[0:H, :], plain(inv_hi[0:H, :]), ALU.subtract).then_inc(inv_ready, 1)
                    nc.vector.drain()

                def keys_values(b):
                    dve.wait_ge(g_hi, (b + 1) * HI + HI_K + 1)
                    nc.vector.tensor_tensor(kk_lo[:, :], G[U_K % NG][:, :], plain(kk_hi[:, :]), ALU.subtract).then_inc(g_free, 1)
                    dve.wait_ge(g_ready, used(b, U_V + 1))
                    nc.vector.tensor_copy(vT[:, :], G[U_V % NG][:, :]).then_inc(g_free, 1)

                def skip(uses):
                    nc.vector.drain().then_inc(g_free, uses)

                def tail(b):
                    def normalise(i):
                        if first(b):
                            skip(1)
                            return
                        dve.wait_ge(g_ready, used(b, U_SPREAD[i] + 1))
                        nc.vector.tensor_tensor(acc[:, i, :], acc[:, i, :], G[U_SPREAD[i] % NG][:, :], ALU.mult).then_inc(g_free, 1)
                        for pair in {0: (), 1: (0, 1)}.get(i, (i,)):
                            low(pair)

                    def low(i):
                        dve.wait_ge(o_hi_done, (b - 1) * HP + i + 1)
                        nc.vector.tensor_tensor(oT_lo[:, i, :], acc[:, i, :], plain(oT_hi[:, i, :]), ALU.subtract).then_inc(o_lo_done, 1)

                    def values():
                        if b is B:
                            skip(1)
                            return
                        dve.wait_ge(g_hi, (b + 1) * HI + HI_VAL + 2)
                        turned = G[U_VAL % NG][:, :].rearrange("p (j v) -> p j v", j=TT)
                        for odd in range(2):
                            cols = slice(odd * DH, (odd + 1) * DH)
                            last = nc.vector.tensor_tensor(val[:, :, 2 + odd, cols], turned[:, :, cols], plain(val[:, :, odd, cols]), ALU.subtract)
                        last.then_inc(g_free, 1)

                    def x(k):
                        if b is B:
                            skip(1)
                            return
                        dve.wait_ge(g_hi, (b + 1) * HI + HI_X + k + 1)
                        nc.vector.scalar_tensor_tensor(nT_lo[:, k, :], G[U_X[k] % NG][:, :], gam[:, 0, k:k + 1],
                                                       plain(nT_hi[:, k, :]), ALU.mult, ALU.subtract).then_inc(g_free, 1)

                    tail_steps(normalise, lambda i: None, values, x)

                def add_rows(b):
                    dve.wait_ge(xres_in, b * (TT * 16))
                    dve.wait_ge(out_ready, b)
                    for t in range(TT):
                        nc.vector.scalar_tensor_tensor(x_rows[t], OUT[t][:, :], gates[:, 0:1], x_rows[t], ALU.mult, ALU.add).then_inc(x_added, 1)

                def queries(b):
                    for i in range(HP):
                        dve.wait_ge(g_hi, (b + 1) * HI + HI_Q + 2 * i + 2)
                        bank = G[(U_Q + i) % NG]
                        for odd in range(2):
                            here, there = slice(odd * DH, (odd + 1) * DH), slice((1 - odd) * DH, (2 - odd) * DH)
                            last = nc.vector.scalar_tensor_tensor(qs[there, 2 * i + odd, :], bank[here, :], q_scale,
                                                                  plain(qs[here, 2 * i + odd, :]), ALU.mult, ALU.subtract)
                        last.then_inc(g_free, 1)

                def maxima(b, on):
                    dve.wait_ge(mask_b_in, b * 16 + 16)
                    nc.vector.tensor_scalar(mask_b[:, :], mask_i, 0.0, MASKED, ALU.is_equal, ALU.mult)
                    nc.vector.memset(m_rows[:, :, :], LOWEST)
                    nc.vector.drain()
                    for j in range(TT):
                        n = b * TT + j
                        with dve.If(on[j] == 1):
                            for i in range(HP):
                                dve.wait_ge(max_scores, n * HP + i + 1)
                                dve.sem_inc(max_begun, 1)
                                for h in (2 * i, 2 * i + 1):
                                    for t in range(TT):
                                        here = MX[h % 4][:, t * P:(t + 1) * P]
                                        m = m_rows[:, t, h:h + 1]
                                        last = nc.vector.tensor_tensor_reduce(here, here, mask_b[:, j * P:(j + 1) * P], 1.0, m,
                                                                              ALU.add, ALU.max, m)
                                last.then_inc(max_taken, 1)
                            nc.vector.drain()
                    nc.vector.drain().then_inc(m_ready, 1)

                def maxima_by_head(b):
                    dve.wait_ge(m_turned, b + 1)
                    nc.vector.tensor_copy(m_heads[0:H, :], SC[0][0:H, :]).then_inc(m_heads_ready, 1)

                def attend(b, on):
                    dve.wait_ge(acc_clear, b + 1)
                    nc.vector.memset(acc_sum[0:H, :], 0.0)
                    nc.vector.drain()
                    for j in range(TT):
                        n = b * TT + j
                        with dve.If(on[j] == 1):
                            def add(i):
                                dve.wait_ge(head_out, n * H + 2 * i + 2)
                                nc.vector.tensor_tensor(acc[:, i, :], acc[:, i, :], OB[i % 2][:, :], ALU.add).then_inc(out_taken, 1)

                            for h in range(H):
                                dve.wait_ge(exps, n * H + h + 1)
                                nc.vector.tensor_tensor(prob_lo[:, h % 2, :], prob[:, h % 2, :], plain(prob_hi[:, h % 2, :]),
                                                        ALU.subtract).then_inc(low_probs, 1)
                                if h >= 2 and h % 2 == 0:
                                    add(h // 2 - 1)
                            add(HP - 1)
                            nc.vector.tensor_tensor(acc_sum[0:H, :], acc_sum[0:H, :], SUM[0:H, :], ALU.add).then_inc(out_taken, 1)
                            nc.vector.drain()
                        with dve.Else():
                            nc.vector.drain().then_inc(low_probs, H)
                            nc.vector.drain().then_inc(out_taken, OUTS)

                def flags(b):
                    return [dve.value_load(live[0:1, bass.ds(b * TT + j, 1)]) for j in range(TT)]

                def batch(b):
                    if not first(b):
                        inverse(b - 1)
                    keys_values(b)
                    tail(b)
                    if not last_batch(b):
                        statistics(b + 1)
                    if not first(b):
                        add_rows(b)
                    if not last_batch(b):
                        deviations(b + 1)
                    on = flags(b)
                    queries(b)
                    if last_batch(b):
                        skip(KT + 1)
                    else:
                        context(b)
                    maxima(b, on)
                    maxima_by_head(b)
                    attend(b, on)

                skip(U_CTX)
                statistics(0)
                deviations(0)
                context(-1)
                batch(0)
                with dve.Fori(1, B - 1) as b:
                    batch(b)
                batch(B - 1)
                inverse(B - 1)
                skip(1)
                tail(B)
                add_rows(B)


def feed_forward(nc, whole, I, gates, x_stats, x1_d, xnT_d):
    with ExitStack() as stage:
        mem = Memory(nc, stage, whole)
        x_v = x1_d.rearrange("b (t p) d -> b p t d", p=P)
        Q = 4
        FT = FF // P // Q
        FQ = FT * P
        w1_v = I["L0_xattn_Wff1"].rearrange("(k p) (g q n) -> k q g p n", p=P, g=2, q=Q)
        w2_v = I["L0_xattn_Wff2"].rearrange("(q f p) n -> f q p n", p=P, q=Q)
        PAIRS = B // 2

        w1 = [[mem.sbuf(f"w1_{part}{i}", [P, KT, 2, FQ], F32R) for part in ("hi", "lo")] for i in range(2)]
        w2 = [[mem.sbuf(f"w2_{part}{i}", [P, FT, D], F32R) for part in ("hi", "lo")] for i in range(2)]
        raw = mem.sbuf("ff_raw", [P, 3, FQ])
        nT = [[mem.sbuf(f"ff_nT_{part}{i}", [P, KT, S], F32R) for part in ("hi", "lo")] for i in range(2)]
        u = [[mem.sbuf(f"u_{part}{i}", [P, FT, S], F32R) for part in ("hi", "lo")] for i in range(2)]
        sig = mem.sbuf("ff_sig", [P, 2, S])
        u32 = mem.sbuf("u32", [P, 2, S])
        xs = [mem.sbuf(f"ff_x{i}", [P, TT, D]) for i in range(2)]
        UP = [[mem.bank(f"ff_{n}{i}") for n in ("a", "gate")] for i in range(2)]
        DN = [mem.bank(f"ff_down{i}") for i in range(2)]

        raw_in = [mem.sem(f"ff_raw_in{i}") for i in range(3)]
        raw_hi, raw_lo = mem.sem("ff_raw_hi"), mem.sem("ff_raw_lo")
        nT_in = [mem.sem(f"ff_nT_in{i}") for i in range(2)]
        x_in = [mem.sem(f"ff_x_in{i}") for i in range(2)]
        x_out = [mem.sem(f"ff_x_out{i}") for i in range(2)]
        up_ready, sig_ready, u_ready, u_hi_done, u_lo_done = (
            mem.sem(f"ff_{n}") for n in ("up_ready", "sig_ready", "u_ready", "u_hi_done", "u_lo_done"))
        down_ready, down_taken, rows_seen = (mem.sem(f"ff_{n}") for n in ("down_ready", "down_taken", "rows_seen"))

        def chunk(q, k, c):
            one = lambda ap: ap[k] if isinstance(k, int) else ap[bass.ds(k, 1)].rearrange("o a b -> (o a) b")
            to = lambda t: t[:, k] if isinstance(k, int) else t[:, bass.ds(k, 1)].rearrange("p o n -> p (o n)")
            if c < 2:
                return one(w1_v[:, q, c]), [to(t[:, :, c, :]) for t in w1[q % 2]]
            return one(w2_v[:, q]), [to(t[:, :, :]) for t in w2[q % 2]]

        with nc.Block() as block:
            @block.sync
            def _(sp):
                def load_weights(q, k, n):
                    for c in range(3):
                        sp.wait_ge(raw_lo, n * 3)
                        sp.dma_start(raw[:, c, :], chunk(q, k, c)[0]).then_inc(raw_in[c], 16)

                def load_rows(b, i):
                    for part in range(2):
                        src = xnT_d[part]
                        src = src[b] if isinstance(b, int) else src[bass.ds(b, 1)].rearrange("o p k s -> (o p) k s")
                        sp.dma_start(plain(nT[i][part][:, :, :]), src).then_inc(nT_in[i], 16)

                def load_x(b, i):
                    src = x_v[b] if isinstance(b, int) else x_v[bass.ds(b, 1)].rearrange("o p t d -> (o p) t d")
                    sp.dma_start(xs[i][:, :, :], src).then_inc(x_in[i], 16)

                def store_x(b, i):
                    dst = x_v[b] if isinstance(b, int) else x_v[bass.ds(b, 1)].rearrange("o p t d -> (o p) t d")
                    sp.dma_start(dst, xs[i][:, :, :]).then_inc(x_out[i], 16)

                def step(q, pair, following):
                    n = pair + q * PAIRS
                    here = [pair * 2 + i for i in range(2)]
                    there = [following * 2 + i for i in range(2)] if following is not None else None
                    if q + 1 < Q:
                        load_weights(q + 1, pair, n + PAIRS)
                    for i in range(2):
                        sp.wait_ge(x_out[i], n * 16)
                        load_x(here[i], i)
                    if there is not None:
                        for i in range(2):
                            sp.wait_ge(up_ready, n * (2 * FT) + (i + 1) * FT)
                            load_rows(there[i], i)
                    for i in range(2):
                        if q == Q - 1:
                            sp.wait_ge(rows_seen, here[i] + 1)
                        else:
                            sp.wait_ge(down_taken, (n * 2 + i + 1) * TT)
                        store_x(here[i], i)

                load_rows(0, 0)
                for k in range(PAIRS):
                    load_weights(0, k, k)
                load_rows(1, 1)
                for q in range(Q):
                    with sp.Fori(0, PAIRS - 1) as pair:
                        step(q, pair, pair + 1)
                    step(q, PAIRS - 1, 0 if q + 1 < Q else None)
                for i in range(2):
                    sp.wait_ge(x_out[i], Q * PAIRS * 16)

            @block.tensor
            def _(pe):
                def up(q, n, i):
                    pe.wait_ge(nT_in[i], (n + 1) * 32)
                    for f in range(FT):
                        m = n * (2 * FT) + i * FT + f
                        if f >= 2:
                            pe.wait_ge(u_ready, m - 1)
                        else:
                            pe.wait_ge(u_ready, n * (2 * FT) + i * FT)
                        for g in (1, 0):
                            c = 0
                            for k in range(KT):
                                for w, m_ in products([t[:, k, g, f * P:(f + 1) * P] for t in w1[q % 2]], [t[:, k, :] for t in nT[i]]):
                                    last = nc.tensor.matmul(UP[f % 2][g][:, :], w, m_, start=c == 0, stop=c == 3 * KT - 1)
                                    c += 1
                        last.then_inc(up_ready, 1)

                def down(q, n, i):
                    pe.wait_ge(u_lo_done, n * (2 * FT) + (i + 1) * FT)
                    for t in range(TT):
                        m = n * (2 * TT) + i * TT
                        pe.wait_ge(down_taken, m + max(t - 1, 0))
                        c = 0
                        for f in range(FT):
                            for a, w in products([x[:, f, t * P:(t + 1) * P] for x in u[i]], [x[:, f, :] for x in w2[q % 2]]):
                                last = nc.tensor.matmul(DN[t % 2][:, :], a, w, start=c == 0, stop=c == 3 * FT - 1)
                                c += 1
                        last.then_inc(down_ready, 1)

                for q in range(Q):
                    pe.wait_ge(raw_lo, (q + 1) * PAIRS * 3)
                    with pe.Fori(0, PAIRS) as pair:
                        n = pair + q * PAIRS
                        up(q, n, 0)
                        up(q, n, 1)
                        down(q, n, 0)
                        down(q, n, 1)

            @block.scalar
            def _(act):
                def split_weights(q, k, n):
                    for c in range(3):
                        act.wait_ge(raw_in[c], (n + 1) * 16)
                        nc.scalar.copy(chunk(q, k, c)[1][0], raw[:, c, :]).then_inc(raw_hi, 1)

                def hidden(n, i):
                    for f in range(FT):
                        m = n * (2 * FT) + i * FT + f
                        act.wait_ge(up_ready, m + 1)
                        if f >= 2:
                            act.wait_ge(u_ready, m - 1)
                        nc.scalar.activation(sig[:, f % 2, :], UP[f % 2][1][:, :], ACT.Silu).then_inc(sig_ready, 1)
                        act.wait_ge(u_ready, m + 1)
                        if f == 0:
                            act.wait_ge(down_ready, n * (2 * TT))
                        nc.scalar.copy(u[i][0][:, f, :], u32[:, f % 2, :]).then_inc(u_hi_done, 1)

                for k in range(PAIRS):
                    split_weights(0, k, k)
                for q in range(Q):
                    with act.Fori(0, PAIRS) as pair:
                        n = pair + q * PAIRS
                        hidden(n, 0)
                        if q + 1 < Q:
                            split_weights(q + 1, pair, n + PAIRS)
                        hidden(n, 1)

            @block.gpsimd
            def _(pool):
                def split_weights(q, k, n):
                    for c in range(3):
                        pool.wait_ge(raw_hi, n * 3 + c + 1)
                        hi, lo = chunk(q, k, c)[1]
                        nc.gpsimd.tensor_tensor(lo, raw[:, c, :], plain(hi), ALU.subtract).then_inc(raw_lo, 1)

                for k in range(PAIRS):
                    split_weights(0, k, k)
                for q in range(Q - 1):
                    with pool.Fori(0, PAIRS) as pair:
                        split_weights(q + 1, pair, pair + (q + 1) * PAIRS)

            @block.vector
            def _(dve):
                def hidden(n, i):
                    for f in range(FT):
                        m = n * (2 * FT) + i * FT + f
                        dve.wait_ge(sig_ready, m + 1)
                        dve.wait_ge(u_lo_done, n * (2 * FT) + i * FT + max(f - 1, 0))
                        nc.vector.tensor_tensor(u32[:, f % 2, :], sig[:, f % 2, :], UP[f % 2][0][:, :], ALU.mult).then_inc(u_ready, 1)
                        dve.wait_ge(u_hi_done, m + 1)
                        nc.vector.tensor_tensor(u[i][1][:, f, :], u32[:, f % 2, :], plain(u[i][0][:, f, :]), ALU.subtract).then_inc(u_lo_done, 1)

                def residual(q, n, i, b):
                    dve.wait_ge(x_in[i], (n + 1) * 16)
                    for t in range(TT):
                        dve.wait_ge(down_ready, n * (2 * TT) + i * TT + t + 1)
                        nc.vector.scalar_tensor_tensor(xs[i][:, t, :], DN[t % 2][:, :], gates[:, 0:1], xs[i][:, t, :],
                                                       ALU.mult, ALU.add).then_inc(down_taken, 1)
                    if q == Q - 1:
                        nc.vector.drain()
                        for t in range(TT):
                            last = nc.vector.bn_stats(x_stats[:, bass.ds(b * TT + t, 1), :].rearrange("p o n -> p (o n)"), xs[i][:, t, :])
                        last.then_inc(rows_seen, 1)

                for q in range(Q):
                    with dve.Fori(0, PAIRS) as pair:
                        n = pair + q * PAIRS
                        hidden(n, 0)
                        hidden(n, 1)
                        residual(q, n, 0, pair * 2)
                        residual(q, n, 1, pair * 2 + 1)


def slot_attention(nc, whole, I, ident, ones, x_stats, o1, hT, x1_d, yT_d):
    with ExitStack() as stage:
        mem = Memory(nc, stage, whole)
        x_v = x1_d.rearrange("b (t p) d -> b p t d", p=P)
        by_rows = lambda w: w.rearrange("(k p) n -> p k n", p=P)
        wq, wk, wv, wo = (mem.sbuf(f"d_w{n}", [P, KT, D]) for n in "qkvo")
        bias = {n: mem.sbuf(f"d_b{n}", [1, D]) for n in "qvo"}
        bk_col = mem.sbuf("d_bk_col", [P, KT])
        sq = mem.sbuf("sq", [NS, D])
        sqT = mem.sbuf("sqT", [P, KT, NS])
        q16 = mem.sbuf("q16", [NS, D])
        q_diag = mem.sbuf("q_diag", [P, KT, 4 * NS])
        wkT = mem.sbuf("wkT", [P, KT, D])
        A = [mem.sbuf(f"A_{part}", [P, KT, HS], F32R) for part in ("hi", "lo")]
        shift = mem.sbuf("shift", [P, 2])
        every = mem.sbuf("every", [NS, P])
        mean, var, rstd, half = (mem.sbuf(f"y_{n}", [P, B * TT]) for n in ("mean", "var", "rstd", "half"))
        xin = mem.sbuf("y_xin", [P, TT, D])
        y = mem.sbuf("y", [P, TT, D])
        yn = [mem.sbuf(f"yn_{part}", [P, 2, TT, D], F32R) for part in ("hi", "lo")]
        yT = [mem.sbuf(f"yT_{part}", [P, KT, S], F32R) for part in ("hi", "lo")]
        pT = [mem.sbuf(f"pT_{part}", [P, TT, HS], F32R) for part in ("hi", "lo")]
        prob = mem.sbuf("d_prob", [P, 2, S])
        top, nb, total, inv = (mem.sbuf(f"d_{n}", [P, 2]) for n in ("top", "nb", "total", "inv"))
        z = mem.sbuf("z", [P, 2, D])
        zT = mem.sbuf("zT", [P, KT, SH, B, NS])
        G = [mem.bank(f"slot_general{i}") for i in range(5)]
        SC = [mem.bank(f"slot_scores{i}") for i in range(2)]

        weights_in, small_in = mem.sem("d_weights_in"), mem.sem("d_small_in")
        pe_step, dve_step, act_step = (mem.sem(f"d_{n}_step") for n in ("pe", "dve", "act"))
        sd_ready = mem.sem("d_sd_ready")
        with nc.Block() as block:
            @block.sync
            def _(sp):
                sp.dma_start(sq[:, :], I["L0_ffn_slot_query"].rearrange("o s d -> (o s) d")).then_inc(small_in, 16)
                sp.dma_start(bk_col[:, :], I["L0_ffn_d_bk"].rearrange("(k p) -> p k", p=P), allow_slow_non_contiguous=True).then_inc(small_in, 16)
                for n in "qvo":
                    sp.dma_start(bias[n][:, :], I[f"L0_ffn_d_b{n}"].unsqueeze(0)).then_inc(small_in, 16)
                for n, w in zip("qkvo", (wq, wk, wv, wo)):
                    sp.dma_start(w[:, :, :], by_rows(I[f"L0_ffn_d_W{n}"])).then_inc(weights_in, 16)
                sp.wait_ge(weights_in, 64)

            @block.tensor
            def _(pe):
                pe.wait_ge(small_in, 80)
                for k in range(KT):
                    last = nc.tensor.transpose(G[0][:, k * NS:(k + 1) * NS], sq[:, k * P:(k + 1) * P], ident[0:NS, 0:NS])
                last.then_inc(pe_step, 1)
                pe.wait_ge(weights_in, 64)
                pe.wait_ge(dve_step, 1)
                nc.tensor.matmul(G[1][0:NS, :], ones[0:1, 0:NS], bias["q"][:, :], start=True, stop=False)
                for k in range(KT):
                    last = nc.tensor.matmul(G[1][0:NS, :], sqT[:, k, :], wq[:, k, :], start=False, stop=k == KT - 1)
                last.then_inc(pe_step, 1)
                for c in range(KT):
                    if c >= 2:
                        pe.wait_ge(act_step, c - 1)
                    for k in range(KT):
                        last = nc.tensor.transpose(G[2 + c % 2][:, k * P:(k + 1) * P], wk[:, k, c * P:(c + 1) * P], ident[:, :])
                    last.then_inc(pe_step, 1)
                pe.wait_ge(dve_step, 2)
                for k in range(KT):
                    last = nc.tensor.transpose(G[0][:, k * NS:(k + 1) * NS], q16[:, k * P:(k + 1) * P], ident[0:NS, 0:NS])
                last.then_inc(pe_step, 1)
                pe.wait_ge(dve_step, 3)
                pe.wait_ge(act_step, KT)
                for k in range(KT):
                    for c in range(KT):
                        at = (k % 2) * HS + c * 4 * NS
                        last = nc.tensor.matmul(SC[k // 2][:, at:at + 4 * NS], wkT[:, c, k * P:(k + 1) * P], q_diag[:, c, :], start=True, stop=True)
                for c in range(KT):
                    at = (c % 2) * 4 * NS
                    last = nc.tensor.matmul(G[4][at:at + 4 * NS, c // 2:c // 2 + 1], q_diag[:, c, :], bk_col[:, c:c + 1], start=True, stop=True)
                last.then_inc(pe_step, 1)

            @block.scalar
            def _(act):
                for c in range(KT):
                    act.wait_ge(pe_step, 3 + c)
                    nc.scalar.copy(wkT[:, c, :], G[2 + c % 2][:, :]).then_inc(act_step, 1)
                act.wait_ge(dve_step, 4)
                nc.scalar.activation(rstd[:, :], var[:, :], ACT.Sqrt).then_inc(sd_ready, 1)
                act.wait_ge(pe_step, KT + 4)
                for i in range(2):
                    nc.scalar.copy(A[0][:, 2 * i:2 * i + 2, :].rearrange("p k n -> p (k n)"), SC[i][:, :]).then_inc(act_step, 1)

            @block.vector
            def _(dve):
                nc.vector.memset(q_diag[:, :, :], 0.0)
                dve.wait_ge(pe_step, 1)
                nc.vector.tensor_copy(sqT[:, :, :].rearrange("p k s -> p (k s)"), G[0][:, 0:KT * NS]).then_inc(dve_step, 1)
                dve.wait_ge(pe_step, 2)
                nc.vector.tensor_scalar(q16[:, :], G[1][0:NS, :], SD ** -0.5, None, ALU.mult).then_inc(dve_step, 1)
                dve.wait_ge(pe_step, KT + 3)
                for g in range(4):
                    rows = slice(g * SD, (g + 1) * SD)
                    last = nc.vector.tensor_copy(q_diag[rows, :, g * NS:(g + 1) * NS], G[0][rows, 0:KT * NS].rearrange("p (k s) -> p k s", k=KT))
                last.then_inc(dve_step, 1)
                rows_mean_var(nc, x_stats[:, :, :], mean[:, :], var[:, :], half[:, :])
                nc.vector.tensor_scalar(var[:, :], var[:, :], EPS, None, ALU.add).then_inc(dve_step, 1)
                for b in range(B):
                    nc.vector.tensor_copy(every[:, b * NS:(b + 1) * NS], ident[0:NS, 0:NS])
                dve.wait_ge(sd_ready, 1)
                nc.vector.reciprocal(rstd[:, :], rstd[:, :])
                dve.wait_ge(pe_step, KT + 4)
                nc.vector.tensor_copy(shift[:, :], G[4][:, 0:2])
                for i in range(2):
                    dve.wait_ge(act_step, KT + i + 1)
                    nc.vector.tensor_tensor(A[1][:, 2 * i:2 * i + 2, :].rearrange("p k n -> p (k n)"), SC[i][:, :],
                                            plain(A[0][:, 2 * i:2 * i + 2, :].rearrange("p k n -> p (k n)")), ALU.subtract)

        x_in, y_ready, yn_hi_done, yn_lo_done, yT_out = (mem.sem(f"d_{n}") for n in ("x_in", "y_ready", "yn_hi", "yn_lo", "yT_out"))
        g_ready, g_hi, g_free = (mem.sem(f"d_{n}") for n in ("g_ready", "g_hi", "g_free"))
        scored, nb_ready, exps = (mem.sem(f"d_{n}") for n in ("scored", "nb_ready", "exps"))
        U_Y, U_P, U_Z, U_ZT, PER = 0, KT, KT + 2, KT + 4, KT + 6
        NG = len(G)
        assert PER % NG == 0
        HI = KT + 2

        def of(ap, b):
            return ap[b] if isinstance(b, int) else ap[bass.ds(b, 1)].rearrange("o p t d -> (o p) t d")

        def slot(t, b):
            return t[:, b % 2] if isinstance(b, int) else t[:, bass.ds(b % 2, 1)].rearrange("p o t d -> p (o t) d")

        with nc.Block() as block:
            @block.sync
            def _(sp):
                def keep(b):
                    sp.wait_ge(g_free, b * PER + U_P)
                    for part in range(2):
                        sp.dma_start(of(yT_d[part], b), plain(yT[part][:, :, :])).then_inc(yT_out, 16)

                sp.dma_start(xin[:, :, :], x_v[0]).then_inc(x_in, 16)
                with sp.Fori(0, B - 1) as b:
                    sp.wait_ge(y_ready, b + 1)
                    sp.dma_start(xin[:, :, :], of(x_v, b + 1)).then_inc(x_in, 16)
                    keep(b)
                keep(B - 1)
                sp.wait_ge(yT_out, B * 32)

            @block.tensor
            def _(pe):
                def claim(b, u):
                    if not (isinstance(b, int) and b == 0 and u < NG):
                        pe.wait_ge(g_free, b * PER + u - (NG - 1))
                    return G[u % NG]

                def turn_rows(b):
                    pe.wait_ge(y_ready, b + 1)
                    for k in range(KT):
                        bank = claim(b, U_Y + k)
                        for t in range(TT):
                            last = nc.tensor.transpose(bank[:, t * P:(t + 1) * P], y[:, t, k * P:(k + 1) * P], ident[:, :])
                        last.then_inc(g_ready, 1)

                def score(b):
                    pe.wait_ge(g_free, b * PER + U_P)
                    pe.wait_ge(exps, b * 2)
                    for i in range(2):
                        n = 0
                        for k in range(KT):
                            for a, m in products([t[:, k, i * P:(i + 1) * P] for t in A], [t[:, k, :] for t in yT]):
                                last = nc.tensor.matmul(SC[i][:, :], a, m, start=n == 0, stop=n == 3 * KT - 1)
                                n += 1
                        last.then_inc(scored, 1)

                def turn_probs(b):
                    pe.wait_ge(exps, b * 2)
                    for half_ in range(2):
                        bank = claim(b, U_P + half_)
                        for t in range(2):
                            for i in range(2):
                                tok = (2 * half_ + t) * P
                                last = nc.tensor.transpose(bank[:, t * HS + i * P:t * HS + (i + 1) * P], prob[:, i, tok:tok + P], ident[:, :])
                        last.then_inc(g_ready, 1)

                def sums(b, prev):
                    pe.wait_ge(g_free, b * PER + U_Z)
                    pe.wait_ge(yn_lo_done, b)
                    for i in range(2):
                        bank = claim(b, U_Z + i)
                        n = 0
                        for t in range(TT):
                            for a, m in products([x[:, t, i * P:(i + 1) * P] for x in pT], [slot(x, prev) for x in yn]):
                                last = nc.tensor.matmul(bank[:, :], a, m[:, t, :], start=n == 0, stop=n == 3 * TT - 1)
                                n += 1
                        last.then_inc(g_ready, 1)
                    pe.wait_ge(g_free, b * PER + U_ZT)
                    for half_ in range(2):
                        bank = claim(b, U_ZT + half_)
                        for k in range(2):
                            for i in range(2):
                                d = (2 * half_ + k) * P
                                last = nc.tensor.transpose(bank[:, k * HS + i * P:k * HS + (i + 1) * P], z[:, i, d:d + P], ident[:, :])
                        last.then_inc(g_ready, 1)

                turn_rows(0)
                pe.drain().then_inc(g_ready, PER - U_P)
                score(0)
                with pe.Fori(1, B) as b:
                    turn_rows(b)
                    turn_probs(b)
                    score(b)
                    sums(b, b - 1)
                pe.drain().then_inc(g_ready, U_P)
                turn_probs(B)
                sums(B, B - 1)

            @block.scalar
            def _(act):
                def front(b):
                    act.wait_ge(y_ready, b + 1)
                    if not (isinstance(b, int) and b == 0):
                        act.wait_ge(g_ready, (b - 1) * PER + U_ZT)
                    nc.scalar.copy(slot(yn[0], b), y[:, :, :]).then_inc(yn_hi_done, 1)
                    if not (isinstance(b, int) and b == 0):
                        act.wait_ge(yT_out, b * 32)
                        act.wait_ge(scored, b * 2)
                    for k in range(KT):
                        act.wait_ge(g_ready, b * PER + U_Y + k + 1)
                        nc.scalar.copy(yT[0][:, k, :], G[(U_Y + k) % NG][:, :]).then_inc(g_hi, 1)

                def probs(b):
                    for i in range(2):
                        act.wait_ge(g_ready, b * PER + U_P + i + 1)
                        nc.scalar.copy(pT[0][:, 2 * i:2 * i + 2, :].rearrange("p t n -> p (t n)"), G[(U_P + i) % NG][:, :]).then_inc(g_hi, 1)

                def exp(b):
                    act.wait_ge(nb_ready, b + 1)
                    for i in range(2):
                        nc.scalar.activation(prob[:, i, :], SC[i][:, :], ACT.Exp, bias=nb[:, i:i + 1], accum_out=total[:, i:i + 1]).then_inc(exps, 1)

                front(0)
                act.drain().then_inc(g_hi, 2)
                exp(0)
                with act.Fori(1, B) as b:
                    front(b)
                    probs(b)
                    exp(b)
                act.drain().then_inc(g_hi, KT)
                probs(B)

            @block.gpsimd
            def _(pool):
                with pool.Fori(0, B) as b:
                    pool.wait_ge(yn_hi_done, b + 1)
                    nc.gpsimd.tensor_tensor(slot(yn[1], b), y[:, :, :], plain(slot(yn[0], b)), ALU.subtract).then_inc(yn_lo_done, 1)

            @block.vector
            def _(dve):
                def norm(b):
                    dve.wait_ge(x_in, b * 16 + 16)
                    dve.wait_ge(yn_lo_done, b)
                    for t in range(TT):
                        n = b * TT + t
                        last = nc.vector.tensor_scalar(y[:, t, :], xin[:, t, :], mean[:, bass.ds(n, 1)], rstd[:, bass.ds(n, 1)], ALU.subtract, ALU.mult)
                    last.then_inc(y_ready, 1)

                def front(b):
                    for k in range(KT):
                        dve.wait_ge(g_hi, b * HI + k + 1)
                        nc.vector.tensor_tensor(yT[1][:, k, :], G[(U_Y + k) % NG][:, :], plain(yT[0][:, k, :]), ALU.subtract).then_inc(g_free, 1)

                def probs(b):
                    for i in range(2):
                        dve.wait_ge(g_hi, b * HI + KT + i + 1)
                        flat = lambda x: x[:, 2 * i:2 * i + 2, :].rearrange("p t n -> p (t n)")
                        nc.vector.tensor_tensor(flat(pT[1]), G[(U_P + i) % NG][:, :], plain(flat(pT[0])), ALU.subtract).then_inc(g_free, 1)

                def maxima(b):
                    for i in range(2):
                        dve.wait_ge(scored, b * 2 + i + 1)
                        nc.vector.tensor_reduce(top[:, i:i + 1], SC[i][:, :], AX.X, ALU.max)
                    nc.vector.drain()
                    nc.vector.tensor_tensor(top[:, :], top[:, :], shift[:, :], ALU.add)
                    nc.vector.drain()
                    nc.vector.tensor_tensor(nb[:, :], shift[:, :], top[:, :], ALU.subtract).then_inc(nb_ready, 1)

                def inverse(b):
                    dve.wait_ge(exps, b * 2)
                    nc.vector.reciprocal(inv[:, :], total[:, :])
                    nc.vector.drain()

                def sums(b, prev):
                    for i in range(2):
                        dve.wait_ge(g_ready, b * PER + U_Z + i + 1)
                        nc.vector.tensor_scalar(z[:, i, :], G[(U_Z + i) % NG][:, :], inv[:, i:i + 1], None, ALU.mult).then_inc(g_free, 1)
                    for i in range(2):
                        dve.wait_ge(g_ready, b * PER + U_ZT + i + 1)
                        to = zT[:, 2 * i:2 * i + 2, :, prev, :] if isinstance(prev, int) else \
                            zT[:, 2 * i:2 * i + 2, :, bass.ds(prev, 1), :].rearrange("p k h o s -> p k h (o s)")
                        nc.vector.tensor_copy(to, G[(U_ZT + i) % NG][:, :].rearrange("p (k h s) -> p k h s", k=2, h=SH)).then_inc(g_free, 1)

                norm(0)
                front(0)
                nc.vector.drain().then_inc(g_free, PER - U_P)
                norm(1)
                maxima(0)
                with dve.Fori(1, B - 1) as b:
                    front(b)
                    inverse(b)
                    probs(b)
                    norm(b + 1)
                    maxima(b)
                    sums(b, b - 1)
                front(B - 1)
                inverse(B - 1)
                probs(B - 1)
                maxima(B - 1)
                sums(B - 1, B - 2)
                nc.vector.drain().then_inc(g_free, U_P)
                inverse(B)
                probs(B)
                sums(B, B - 1)

        o_att, oT = mem.sbuf("o_att", [P, D]), mem.sbuf("oT_s", [P, KT, P])
        stat1, mv, sd = mem.sbuf("o_stats", [P, 6]), mem.sbuf("o_mv", [P, 2]), mem.sbuf("o_sd", [P, 1])
        e_gain, e_shift, h_in = (mem.sbuf(n, [P, D]) for n in ("e_gain", "e_shift", "h_in"))
        gains_in, pe2, dve2, act2 = (mem.sem(f"d2_{n}") for n in ("gains_in", "pe", "dve", "act"))
        with nc.Block() as block:
            @block.sync
            def _(sp):
                for b in range(B):
                    sp.dma_start(e_gain[b * NS:(b + 1) * NS, :], I["L0_ffn_e_ln_g"]).then_inc(gains_in, 16)
                    sp.dma_start(e_shift[b * NS:(b + 1) * NS, :], I["L0_ffn_e_ln_b"]).then_inc(gains_in, 16)
                sp.wait_ge(gains_in, 2 * B * 16)

            @block.tensor
            def _(pe):
                nc.tensor.matmul(G[0][:, :], ones[0:1, :], bias["v"][:, :], start=True, stop=False)
                for h in range(SH):
                    cols = slice(h * SD, (h + 1) * SD)
                    for k in range(KT):
                        last = nc.tensor.matmul(G[0][:, cols], zT[:, k, h, :, :].rearrange("p b s -> p (b s)"), wv[:, k, cols],
                                                start=False, stop=h == SH - 1 and k == KT - 1)
                last.then_inc(pe2, 1)
                pe.wait_ge(dve2, 1)
                for k in range(KT):
                    last = nc.tensor.transpose(G[1][:, k * P:(k + 1) * P], o_att[:, k * P:(k + 1) * P], ident[:, :])
                last.then_inc(pe2, 1)
                pe.wait_ge(dve2, 2)
                nc.tensor.matmul(G[2][:, :], ones[0:1, :], bias["o"][:, :], start=True, stop=False)
                nc.tensor.matmul(G[2][:, :], every[:, :], sq[:, :], start=False, stop=False)
                for k in range(KT):
                    last = nc.tensor.matmul(G[2][:, :], oT[:, k, :], wo[:, k, :], start=False, stop=k == KT - 1)
                last.then_inc(pe2, 1)
                pe.wait_ge(dve2, 4)
                for k in range(KT):
                    last = nc.tensor.transpose(G[3][:, k * P:(k + 1) * P], h_in[:, :].rearrange("r (p k) -> r k p", k=KT)[:, k, :], ident[:, :])
                last.then_inc(pe2, 1)

            @block.scalar
            def _(act):
                act.wait_ge(dve2, 3)
                nc.scalar.activation(sd[:, :], sd[:, :], ACT.Sqrt).then_inc(act2, 1)

            @block.vector
            def _(dve):
                dve.wait_ge(pe2, 1)
                nc.vector.tensor_copy(o_att[:, :], G[0][:, :]).then_inc(dve2, 1)
                dve.wait_ge(pe2, 2)
                nc.vector.tensor_copy(oT[:, :, :].rearrange("p k n -> p (k n)"), G[1][:, :]).then_inc(dve2, 1)
                dve.wait_ge(pe2, 3)
                nc.vector.tensor_copy(o1[:, :], G[2][:, :])
                nc.vector.drain()
                nc.vector.bn_stats(stat1[:, :], o1[:, :])
                nc.vector.drain()
                nc.vector.bn_aggr(mv[:, :], stat1[:, :])
                nc.vector.drain()
                nc.vector.tensor_scalar(sd[:, :], mv[:, 1:2], EPS, None, ALU.add).then_inc(dve2, 1)
                dve.wait_ge(act2, 1)
                nc.vector.reciprocal(sd[:, :], sd[:, :])
                nc.vector.drain()
                nc.vector.tensor_scalar(h_in[:, :], o1[:, :], mv[:, 0:1], sd[:, 0:1], ALU.subtract, ALU.mult)
                dve.wait_ge(gains_in, 2 * B * 16)
                nc.vector.drain()
                nc.vector.tensor_tensor(h_in[:, :], h_in[:, :], e_gain[:, :], ALU.mult)
                nc.vector.drain()
                nc.vector.tensor_tensor(h_in[:, :], h_in[:, :], e_shift[:, :], ALU.add).then_inc(dve2, 1)
                dve.wait_ge(pe2, 4)
                for k in range(KT):
                    nc.vector.tensor_copy(hT[:, k, :, :], G[3][:, k * P:(k + 1) * P].rearrange("p (b e) -> p e b", e=E))


def experts(nc, whole, I, ident, hT, y_d):
    with ExitStack() as stage:
        mem = Memory(nc, stage, whole)
        FT = FF // P
        Q, QW = 4, 32
        C = FF // Q
        J = C // P
        w1 = [mem.sbuf(f"e_w1_{i}", [P, KT, FF]) for i in range(2)]
        wg = [mem.sbuf(f"e_wg_{i}", [P, KT, FF]) for i in range(2)]
        w2 = [mem.sbuf(f"e_w2_{i}", [P, FT, D]) for i in range(2)]
        bias_rows = [w2[1][0:E, 4 * i:4 * i + 4, :].rearrange("e a n -> e (a n)") for i in range(2)]
        block_at = [q * C + j * P for j in range(J) for q in range(Q)]
        biasT = [mem.sbuf(f"e_{n}T", [P, FT, E]) for n in ("b1", "bg")]
        h = mem.sbuf("e_h", [P, KT, QW])
        rows = [mem.sbuf(f"e_{n}_rows", [P, C]) for n in "ug"]
        pre = rows[0][:, 0:2 * FT * B].rearrange("p (n f b) -> p n f b", n=2, f=FT)
        ug = mem.sbuf("e_ug", [P, FT, QW])
        y_parts = mem.sbuf("e_y_parts", [P, D])
        ys = y_parts[0:B, :]
        fold = mem.sbuf("e_fold", [P, B])
        UP = [mem.bank(f"e_{n}") for n in "ug"]
        TB = [mem.bank(f"e_turned{i}") for i in range(2)]
        YB, YS = mem.bank("e_down"), mem.bank("e_folded")

        bias_in, bias_turned, bias_ready, fold_ready = (mem.sem(f"e_{n}") for n in ("bias_in", "bias_turned", "bias_ready", "fold_ready"))
        w1_in, wg_in, w2_in = ([mem.sem(f"e_{n}_in{i}") for i in range(2)] for n in ("w1", "wg", "w2"))
        h_ready, u_ready, g_ready, u_taken, g_taken, turned, pre_ready, silu_ready, ug_ready = (
            mem.sem(f"e_{n}") for n in ("h_ready", "u_ready", "g_ready", "u_taken", "g_taken", "turned", "pre_ready",
                                        "silu_ready", "ug_ready"))
        down_ready, parts_taken, folded, y_done, y_out = (
            mem.sem(f"e_{n}") for n in ("down_ready", "parts_taken", "folded", "y_done", "y_out"))

        def of(ap, e):
            return ap[e] if isinstance(e, int) else ap[bass.ds(e, 1)].rearrange("o a b -> (o a) b")

        def arrived(e, i):
            return e * 8 + (16 - 8 * i)

        def skewed(eng, start, body, finish):
            start(0, 0)
            with eng.Fori(0, E // 2 - 1) as pair:
                for i in range(2):
                    body(pair * 2 + i, i)
            body(E - 2, 0)
            finish(E - 1, 1)

        with nc.Block() as block:
            @block.sync
            def _(sp):
                def load(e, i, turn):
                    later = not (isinstance(turn, int) and turn == 0)
                    if later:
                        sp.wait_ge(u_ready, turn * 2 + (i - 1))
                    sp.dma_start(w1[i][:, :, :].rearrange("p k n -> p (k n)"), of(I["L0_ffn_e_W1"], e).rearrange("(p k) n -> p (k n)", k=KT)).then_inc(w1_in[i], 16)
                    if later:
                        sp.wait_ge(g_ready, turn * 2 + (i - 1))
                    sp.dma_start(wg[i][:, :, :].rearrange("p k n -> p (k n)"), of(I["L0_ffn_e_Wg"], e).rearrange("(p k) n -> p (k n)", k=KT)).then_inc(wg_in[i], 16)
                    if later:
                        sp.wait_ge(down_ready, turn * 2 + (i - 1))
                    elif i == 1:
                        sp.wait_ge(bias_turned, 2)
                    sp.dma_start(w2[i][:, :, :], of(I["L0_ffn_e_W2"], e).rearrange("(f p) n -> p f n", p=P)).then_inc(w2_in[i], 16)

                def store(e):
                    sp.wait_ge(y_done, e + 1)
                    sp.dma_start(of(y_d, e), ys).then_inc(y_out, 16)

                for i, n in enumerate(("b1", "bg")):
                    sp.dma_start(bias_rows[i], I[f"L0_ffn_e_{n}"]).then_inc(bias_in, 16)
                load(0, 0, 0)
                load(1, 1, 0)
                with sp.Fori(1, E // 2) as turn:
                    for i in range(2):
                        load(turn * 2 + i, i, turn)
                        store(turn * 2 + (i - 2))
                store(E - 2)
                store(E - 1)
                sp.wait_ge(y_out, E * 16)

            @block.tensor
            def _(pe):
                def grow(e, i):
                    pe.wait_ge(h_ready, e + 1)
                    for bank, w, arrival, taken, ready in ((UP[0], w1[i], w1_in[i], u_taken, u_ready), (UP[1], wg[i], wg_in[i], g_taken, g_ready)):
                        pe.wait_ge(arrival, arrived(e, i))
                        pe.wait_ge(taken, e)
                        for k in range(KT):
                            for q in range(Q):
                                last = nc.tensor.matmul(bank[q * QW:(q + 1) * QW, :], h[:, k, :], w[:, k, q * C:(q + 1) * C], start=k == 0, stop=k == KT - 1)
                        last.then_inc(ready, 1)

                def turn(e):
                    pe.wait_ge(pre_ready, e)
                    for n, taken in enumerate((u_taken, g_taken)):
                        pe.wait_ge(taken, e + 1)
                        for j in range(J):
                            last = nc.tensor.transpose(TB[n][:, j * P:(j + 1) * P], rows[n][:, j * P:(j + 1) * P], ident[:, :])
                    last.then_inc(turned, 1)

                def shrink(e, i):
                    pe.wait_ge(ug_ready, e + 1)
                    pe.wait_ge(w2_in[i], arrived(e, i))
                    pe.wait_ge(parts_taken, e)
                    for j in range(J):
                        for q in range(Q):
                            last = nc.tensor.matmul(YB[q * QW:(q + 1) * QW, :], ug[:, j * Q + q, :], w2[i][:, q * J + j, :], start=j == 0, stop=j == J - 1)
                    last.then_inc(down_ready, 1)

                def add_parts(e):
                    pe.wait_ge(parts_taken, e + 1)
                    pe.wait_ge(y_done, e)
                    nc.tensor.matmul(YS[0:B, :], fold[:, :], y_parts[:, :], start=True, stop=True).then_inc(folded, 1)

                def both(e, i):
                    grow(e + 1, 1 - i)
                    shrink(e, i)
                    turn(e + 1)
                    add_parts(e)

                def start(e, i):
                    grow(e, i)
                    turn(e)

                def finish(e, i):
                    shrink(e, i)
                    add_parts(e)

                pe.wait_ge(bias_in, 32)
                for n in range(2):
                    for f, at in enumerate(block_at):
                        last = nc.tensor.transpose(TB[n][:, f * E:(f + 1) * E], bias_rows[n][:, at:at + P], ident[0:E, 0:E])
                    last.then_inc(bias_turned, 1)
                pe.wait_ge(bias_ready, 2)
                pe.wait_ge(fold_ready, 1)
                skewed(pe, start, both, finish)

            @block.scalar
            def _(act):
                def start(e, i):
                    act.wait_ge(u_ready, e + 1)
                    act.wait_ge(ug_ready, e)
                    nc.scalar.copy(rows[0][:, :], UP[0][:, :]).then_inc(u_taken, 1)

                def finish(e, i):
                    act.wait_ge(down_ready, e + 1)
                    act.wait_ge(y_out, e * 16)
                    nc.scalar.copy(y_parts[:, :], YB[:, :]).then_inc(parts_taken, 1)

                def gates_of(e):
                    act.wait_ge(pre_ready, e + 1)
                    nc.scalar.activation(pre, pre, ACT.Silu).then_inc(silu_ready, 1)

                def both(e, i):
                    start(e + 1, 1 - i)
                    finish(e, i)
                    gates_of(e + 1)

                def first(e, i):
                    start(e, i)
                    gates_of(e)

                skewed(act, first, both, finish)

            @block.vector
            def _(dve):
                def take_h(e):
                    src = hT[:, :, e, :] if isinstance(e, int) else hT[:, :, bass.ds(e, 1), :].rearrange("p k o b -> p k (o b)")
                    nc.vector.tensor_copy(h[:, :, 0:B], src).then_inc(h_ready, 1)

                def start(e, i):
                    dve.wait_ge(g_ready, e + 1)
                    dve.wait_ge(turned, e)
                    nc.vector.tensor_copy(rows[1][:, :], UP[1][:, :]).then_inc(g_taken, 1)
                    if not (isinstance(e, int) and e == E - 1):
                        take_h(e + 1)

                def product(e):
                    dve.wait_ge(turned, e + 1)
                    for n in range(2):
                        cols = TB[n][:, :].rearrange("p (f r) -> p f r", r=QW)[:, :, 0:B]
                        add = biasT[n][:, :, e:e + 1] if isinstance(e, int) else biasT[n][:, :, bass.ds(e, 1)]
                        last = nc.vector.tensor_tensor(pre[:, n, :, :], cols, add.to_broadcast([P, FT, B]), ALU.add)
                    last.then_inc(pre_ready, 1)
                    dve.wait_ge(silu_ready, e + 1)
                    dve.wait_ge(down_ready, e)
                    nc.vector.tensor_tensor(ug[:, :, 0:B], pre[:, 0, :, :], pre[:, 1, :, :], ALU.mult).then_inc(ug_ready, 1)

                def finish(e, i):
                    dve.wait_ge(folded, e + 1)
                    nc.vector.tensor_copy(ys, YS[0:B, :]).then_inc(y_done, 1)

                def both(e, i):
                    start(e + 1, 1 - i)
                    product(e + 1)
                    finish(e, i)

                def first(e, i):
                    start(e, i)
                    product(e)

                nc.vector.memset(h[:, :, :], 0.0)
                nc.vector.memset(ug[:, :, :], 0.0)
                nc.vector.tensor_tensor(fold[:, :], ident[:, 0:B], ident[:, QW:QW + B], ALU.add)
                for q in range(2, Q):
                    nc.vector.drain()
                    last = nc.vector.tensor_tensor(fold[:, :], fold[:, :], ident[:, q * QW:q * QW + B], ALU.add)
                last.then_inc(fold_ready, 1)
                take_h(0)
                for n in range(2):
                    dve.wait_ge(bias_turned, n + 1)
                    nc.vector.tensor_copy(biasT[n][:, :, :].rearrange("p f e -> p (f e)"), TB[n][:, 0:FT * E]).then_inc(bias_ready, 1)
                skewed(dve, first, both, finish)


def token_attention(nc, whole, I, ident, gates, o1, x1_d, yT_d, y_d, out):
    with ExitStack() as stage:
        mem = Memory(nc, stage, whole)
        HT = HS // P
        CH = P // SD
        x_v = x1_d.rearrange("b (t p) d -> b p t d", p=P)
        out_v = out.rearrange("b (t p) d -> b p t d", p=P)
        by_rows = lambda w: w.rearrange("(k p) n -> p k n", p=P)
        WK = [mem.sbuf(f"WK_{part}", [P, KT, B, HS], F32R) for part in ("hi", "lo")]
        VW_hi = mem.sbuf("VW_hi", [P, B, HT, D], F32R)
        with nc.sbuf_tensor("c_lent", [P, 4, KT, D], F32) as lent:
            wq, wk, wv = (lent[:, i, :, :] for i in range(3))
            o2, o2T, y_rows, b2_rows = (lent[:, 3, i, :] for i in range(4))
        VW = [VW_hi, mem.sbuf("VW_lo", [P, B, HT, D], F32R)]
        bias_k = mem.sbuf("bias_k", [P, B, HS])
        bo_gate = mem.sbuf("bo_gate", [P, D])

        slots_in, c_small_in, c_weights_in = (mem.sem(f"c_{n}") for n in ("slots_in", "small_in", "weights_in"))
        o2_ready, blocks_zero, w_ready, w_hi, w_free = (mem.sem(f"c_{n}") for n in ("o2_ready", "blocks_zero", "w_ready", "w_hi", "w_free"))
        with ExitStack() as early:
            first = Memory(nc, early, whole)
            wo, wqT = first.sbuf("c_wo", [P, KT, D]), first.sbuf("c_wqT", [P, KT, D])
            k_diag = first.sbuf("k_diag", [P, KT, B, CH * NS])
            v_diag = first.sbuf("v_diag", [P, KT, B, P])
            bias = {n: first.sbuf(f"c_b{n}_col", [P, KT]) for n in "qkv"}
            banks = [first.bank(f"c_general{i}") for i in range(8)]
            U_WQ, U_O2, U_K, U_V, U_BK = 0, KT, KT + 1, KT + 2, KT + 3
            U_WK = U_BK + KT
            U_VW = U_WK + KT * KT
            of_bank = lambda u: banks[u % 8]

            with nc.Block() as block:
                @block.sync
                def _(sp):
                    sp.dma_start(wq, by_rows(I["L0_ffn_c_Wq"])).then_inc(c_weights_in, 16)
                    for b in range(B):
                        sp.dma_start(y_rows[b * NS:(b + 1) * NS, :], y_d[:, b, :]).then_inc(slots_in, 16)
                        sp.dma_start(b2_rows[b * NS:(b + 1) * NS, :], I["L0_ffn_e_b2"]).then_inc(slots_in, 16)
                    for n in "qkv":
                        sp.dma_start(bias[n][:, :], I[f"L0_ffn_c_b{n}"].rearrange("(k p) -> p k", p=P), allow_slow_non_contiguous=True).then_inc(c_small_in, 16)
                    sp.dma_start(bo_gate[:, :], I["L0_ffn_c_bo"].unsqueeze(0).to_broadcast([P, D])).then_inc(c_small_in, 16)
                    sp.wait_ge(c_weights_in, 16)
                    for n, w in zip("kvo", (wk, wv, wo)):
                        dst = w if n != "o" else w[:, :, :]
                        sp.dma_start(dst, by_rows(I[f"L0_ffn_c_W{n}"])).then_inc(c_weights_in, 16)

                @block.tensor
                def _(pe):
                    def claim(u):
                        if u >= 8:
                            pe.wait_ge(w_free, u - 7)
                        return of_bank(u)

                    pe.wait_ge(c_weights_in, 16)
                    for c in range(KT):
                        bank = claim(U_WQ + c)
                        for k in range(KT):
                            last = nc.tensor.transpose(bank[:, k * P:(k + 1) * P], wq[:, k, c * P:(c + 1) * P], ident[:, :])
                        last.then_inc(w_ready, 1)
                    pe.wait_ge(o2_ready, 1)
                    bank = claim(U_O2)
                    for k in range(KT):
                        last = nc.tensor.transpose(bank[:, k * P:(k + 1) * P], o2[:, k * P:(k + 1) * P], ident[:, :])
                    last.then_inc(w_ready, 1)
                    pe.wait_ge(c_weights_in, 64)
                    pe.wait_ge(w_free, U_O2 + 1)
                    for u, w in ((U_K, wk), (U_V, wv)):
                        bank = claim(u)
                        for c in range(KT):
                            for k in range(KT):
                                last = nc.tensor.matmul(bank[:, c * P:(c + 1) * P], w[:, k, c * P:(c + 1) * P], o2T[:, k * P:(k + 1) * P],
                                                        start=k == 0, stop=k == KT - 1)
                        last.then_inc(w_ready, 1)
                    pe.wait_ge(w_free, U_K + 1)
                    keys = lambda c: k_diag[:, c, :, :].rearrange("p b n -> p (b n)")
                    for c in range(KT):
                        nc.tensor.matmul(claim(U_BK + c)[:, :], bias["q"][:, c:c + 1].to_broadcast([P, P]), keys(c), start=True, stop=True).then_inc(w_ready, 1)
                    for k in range(KT):
                        for c in range(KT):
                            nc.tensor.matmul(claim(U_WK + k * KT + c)[:, :], wqT[:, c, k * P:(k + 1) * P], keys(c), start=True, stop=True).then_inc(w_ready, 1)
                    for b in range(B):
                        for t in range(HT):
                            bank = claim(U_VW + b * HT + t)
                            for c in (2 * t, 2 * t + 1):
                                last = nc.tensor.matmul(bank[:, :], v_diag[:, c, b, :], wo[:, c, :], start=c == 2 * t, stop=c == 2 * t + 1)
                            last.then_inc(w_ready, 1)

                def split_places():
                    for k in range(KT):
                        for c in range(KT):
                            cols = slice(c * CH * NS, (c + 1) * CH * NS)
                            yield U_WK + k * KT + c, [t[:, k, :, cols] for t in WK], True
                    for b in range(B):
                        for t in range(HT):
                            yield U_VW + b * HT + t, [x[:, b, t, :] for x in VW], False

                def as_place(u, heads):
                    return of_bank(u)[:, :].rearrange("p (b n) -> p b n", b=B) if heads else of_bank(u)[:, :]

                @block.gpsimd
                def _(pool):
                    nc.gpsimd.memset(k_diag[:, :, :, :], 0.0).then_inc(blocks_zero, 1)
                    nc.gpsimd.memset(v_diag[:, :, :, :], 0.0).then_inc(blocks_zero, 1)

                @block.scalar
                def _(act):
                    for u, (hi, _), heads in split_places():
                        act.wait_ge(w_ready, u + 1)
                        nc.scalar.copy(hi, as_place(u, heads)).then_inc(w_hi, 1)

                @block.vector
                def _(dve):
                    for c in range(KT):
                        dve.wait_ge(w_ready, U_WQ + c + 1)
                        nc.vector.tensor_copy(wqT[:, c, :], of_bank(U_WQ + c)[:, :]).then_inc(w_free, 1)
                    dve.wait_ge(slots_in, 2 * B * 16)
                    nc.vector.tensor_tensor(o2, o1[:, :], y_rows, ALU.add)
                    nc.vector.drain()
                    nc.vector.tensor_tensor(o2, o2, b2_rows, ALU.add).then_inc(o2_ready, 1)
                    dve.wait_ge(c_small_in, 4 * 16)
                    nc.vector.tensor_scalar(bo_gate[:, :], bo_gate[:, :], gates[:, 1:2], None, ALU.mult)
                    dve.wait_ge(w_ready, U_O2 + 1)
                    nc.vector.tensor_copy(o2T, of_bank(U_O2)[:, :]).then_inc(w_free, 1)
                    dve.wait_ge(blocks_zero, 2)
                    for u, n in ((U_K, "k"), (U_V, "v")):
                        dve.wait_ge(w_ready, u + 1)
                        for c in range(KT):
                            for g in range(CH):
                                rows = slice(g * SD, (g + 1) * SD)
                                src = of_bank(u)[rows, c * P:(c + 1) * P].rearrange("p (b s) -> p b s", b=B)
                                add = bias[n][rows, c:c + 1]
                                if n == "k":
                                    last = nc.vector.tensor_scalar(k_diag[rows, c, :, g * NS:(g + 1) * NS], src, add, SD ** -0.5, ALU.add, ALU.mult)
                                else:
                                    at = (c % 2) * CH * NS + g * NS
                                    last = nc.vector.tensor_scalar(v_diag[rows, c, :, at:at + NS], src, add, None, ALU.add)
                        last.then_inc(w_free, 1)
                    for c in range(KT):
                        dve.wait_ge(w_ready, U_BK + c + 1)
                        nc.vector.tensor_copy(bias_k[:, :, c * CH * NS:(c + 1) * CH * NS], as_place(U_BK + c, True)).then_inc(w_free, 1)
                    for n, (u, (hi, lo), heads) in enumerate(split_places()):
                        dve.wait_ge(w_hi, n + 1)
                        nc.vector.tensor_tensor(lo, as_place(u, heads), plain(hi), ALU.subtract).then_inc(w_free, 1)

        PB = TT // 2
        yT = [[mem.sbuf(f"c_yT_{part}{i}", [P, KT, S], F32R) for part in ("hi", "lo")] for i in range(2)]
        xs = [mem.sbuf(f"c_x{i}", [P, TT, D]) for i in range(2)]
        prob = [mem.sbuf(f"c_prob{i}", [P, PB, 2, HS]) for i in range(2)]
        pT = [mem.sbuf(f"c_pT_{part}", [P, PB, 2, HT, P], F32R) for part in ("hi", "lo")]
        top, total = (mem.sbuf(f"c_{n}", [P, PB, 2 * SH]) for n in ("top", "total"))
        SC = [mem.bank(f"c_scores{i}") for i in range(PB)]
        TB = [mem.bank(f"c_turned{i}") for i in range(PB)]
        OB = [mem.bank(f"c_out{i}") for i in range(TT)]
        yT_in, x_in, x_out = ([mem.sem(f"c_{n}{i}") for i in range(2)] for n in ("yT_in", "x_in", "x_out"))
        scored, shifted, exps, probs_ready, turned, p_hi, p_lo = (
            mem.sem(f"c_{n}") for n in ("scored", "shifted", "exps", "probs_ready", "turned", "p_hi", "p_lo"))
        bo_added, summed, x_done = (mem.sem(f"c_{n}") for n in ("bo_added", "summed", "x_done"))

        def of(ap, b):
            return ap[b] if isinstance(b, int) else ap[bass.ds(b, 1)].rearrange("o p t d -> (o p) t d")

        def arrived(b, i, size):
            return b * (size // 2) + (size - (size // 2) * i)

        def skewed(eng, front, back):
            front(0, 0)
            with eng.Fori(0, B // 2 - 1) as pair:
                for i in range(2):
                    front(pair * 2 + i + 1, 1 - i)
                    back(pair * 2 + i, i)
            front(B - 1, 1)
            back(B - 2, 0)
            back(B - 1, 1)

        with nc.Block() as block:
            @block.sync
            def _(sp):
                def load_y(b, i):
                    for part in range(2):
                        sp.dma_start(plain(yT[i][part][:, :, :]), of(yT_d[part], b)).then_inc(yT_in[i], 16)

                def load_x(b, i):
                    sp.dma_start(xs[i][:, :, :], of(x_v, b)).then_inc(x_in[i], 16)

                def after(b, i):
                    again, ahead = b + 2, b + 3
                    if not (isinstance(b, int) and ahead >= B):
                        sp.wait_ge(scored, (b + 2) * PB)
                        load_y(ahead, 1 - i)
                    sp.wait_ge(x_done, (b + 1) * TT)
                    sp.dma_start(of(out_v, b), xs[i][:, :, :]).then_inc(x_out[i], 16)
                    if not (isinstance(b, int) and again >= B):
                        sp.wait_ge(x_out[i], arrived(b, i, 16))
                        load_x(again, i)

                for i in range(2):
                    load_y(i, i)
                    load_x(i, i)
                sp.wait_ge(scored, PB)
                load_y(2, 0)
                with sp.Fori(0, B // 2 - 2) as pair:
                    for i in range(2):
                        after(pair * 2 + i, i)
                for b in range(B - 4, B):
                    after(b, b % 2)
                for i in range(2):
                    sp.wait_ge(x_out[i], B // 2 * 16)

            @block.gpsimd
            def _(pool):
                with pool.Fori(0, B // 2) as pair:
                    for i in range(2):
                        pool.wait_ge(x_in[i], pair * 16 + 16)
                        nc.gpsimd.tensor_tensor(xs[i][:, :, :], xs[i][:, :, :], bo_gate[:, :].unsqueeze(1).to_broadcast([P, TT, D]), ALU.add).then_inc(bo_added, 1)

            @block.tensor
            def _(pe):
                def scores(b, i):
                    pe.wait_ge(yT_in[i], arrived(b, i, 32))
                    for j in range(PB):
                        if not (isinstance(b, int) and b == 0):
                            pe.wait_ge(shifted, (b - 1) * PB + j + 1)
                        for t in range(2):
                            n = 0
                            tok = (2 * j + t) * P
                            for k in range(KT):
                                of_b = [w[:, k, b, :] if isinstance(b, int) else w[:, k, bass.ds(b, 1), :].rearrange("p o n -> p (o n)") for w in WK]
                                for a, w in products([y[:, k, tok:tok + P] for y in yT[i]], of_b):
                                    last = nc.tensor.matmul(SC[j][:, t * HS:(t + 1) * HS], a, w, start=n == 0, stop=n == 3 * KT - 1)
                                    n += 1
                        last.then_inc(scored, 1)

                def sums(b, i):
                    pe.wait_ge(p_lo, b * PB)
                    for j in range(PB):
                        pe.wait_ge(probs_ready, b * PB + j + 1)
                        for t in range(2):
                            for r in range(HT):
                                at = (t * HT + r) * P
                                last = nc.tensor.transpose(TB[j][:, at:at + P], prob[i][:, j, t, r * P:(r + 1) * P], ident[:, :])
                        last.then_inc(turned, 1)
                    pe.wait_ge(x_done, b * TT)
                    for t in range(TT):
                        j = t // 2
                        pe.wait_ge(p_lo, b * PB + j + 1)
                        n = 0
                        for r in range(HT):
                            of_b = [w[:, b, r, :] if isinstance(b, int) else w[:, bass.ds(b, 1), r, :].rearrange("p o n -> p (o n)") for w in VW]
                            for a, w in products([p[:, j, t % 2, r, :] for p in pT], of_b):
                                last = nc.tensor.matmul(OB[t][:, :], a, w, start=n == 0, stop=n == 3 * HT - 1)
                                n += 1
                        last.then_inc(summed, 1)

                skewed(pe, scores, sums)

            @block.scalar
            def _(act):
                def exp(b, i):
                    for j in range(PB):
                        act.wait_ge(shifted, b * PB + j + 1)
                        nc.scalar.activation(prob[i][:, j, :, :], prob[i][:, j, :, :], ACT.Exp).then_inc(exps, 1)

                def split(b, i):
                    if not (isinstance(b, int) and b == 0):
                        act.wait_ge(summed, b * TT)
                    for j in range(PB):
                        act.wait_ge(turned, b * PB + j + 1)
                        nc.scalar.copy(pT[0][:, j, :, :, :].rearrange("p t r n -> p (t r n)"), TB[j][:, :]).then_inc(p_hi, 1)

                skewed(act, exp, split)

            @block.vector
            def _(dve):
                by_head = lambda j, i: prob[i][:, j, :, :].rearrange("p t (h s) -> p (t h) s", s=NS)
                per_slot = lambda a: a.unsqueeze(2).to_broadcast([P, 2 * SH, NS])

                def shift(b, i):
                    for j in range(PB):
                        dve.wait_ge(scored, b * PB + j + 1)
                        add = bias_k[:, b:b + 1, :] if isinstance(b, int) else bias_k[:, bass.ds(b, 1), :]
                        nc.vector.tensor_tensor(prob[i][:, j, :, :], SC[j][:, :].rearrange("p (t n) -> p t n", t=2),
                                                add.to_broadcast([P, 2, HS]), ALU.add)
                        nc.vector.drain()
                        nc.vector.tensor_reduce(top[:, j, :], by_head(j, i), AX.X, ALU.max)
                        nc.vector.drain()
                        nc.vector.tensor_tensor(by_head(j, i), by_head(j, i), per_slot(top[:, j, :]), ALU.subtract).then_inc(shifted, 1)

                def normalise(b, i):
                    for j in range(PB):
                        dve.wait_ge(exps, b * PB + j + 1)
                        nc.vector.tensor_reduce(total[:, j, :], by_head(j, i), AX.X, ALU.add)
                        nc.vector.drain()
                        nc.vector.reciprocal(total[:, j, :], total[:, j, :])
                        nc.vector.drain()
                        nc.vector.tensor_tensor(by_head(j, i), by_head(j, i), per_slot(total[:, j, :]), ALU.mult).then_inc(probs_ready, 1)

                def finish(b, i):
                    for j in range(PB):
                        dve.wait_ge(p_hi, b * PB + j + 1)
                        flat = [p[:, j, :, :, :].rearrange("p t r n -> p (t r n)") for p in pT]
                        nc.vector.tensor_tensor(flat[1], TB[j][:, :], plain(flat[0]), ALU.subtract).then_inc(p_lo, 1)
                    dve.wait_ge(bo_added, b + 1)
                    for t in range(TT):
                        dve.wait_ge(summed, b * TT + t + 1)
                        nc.vector.scalar_tensor_tensor(xs[i][:, t, :], OB[t][:, :], gates[:, 1:2], xs[i][:, t, :], ALU.mult, ALU.add).then_inc(x_done, 1)

                shift(0, 0)
                normalise(0, 0)
                with dve.Fori(0, B // 2 - 1) as pair:
                    for i in range(2):
                        shift(pair * 2 + i + 1, 1 - i)
                        finish(pair * 2 + i, i)
                        normalise(pair * 2 + i + 1, 1 - i)
                shift(B - 1, 1)
                finish(B - 2, 0)
                normalise(B - 1, 1)
                finish(B - 1, 1)


def gated_block(nc, I, out):
    scratch = lambda name, shape: nc.dram_tensor(name, shape, F32, kind="Internal").ap()
    x1_d = scratch("x1", [B, S, D])
    xnT_d = scratch("xnT", [2, B, P, KT, S])
    y_d = scratch("slot_y", [E, B, D])
    with ExitStack() as whole:
        sbuf = lambda stack, name, shape: stack.enter_context(nc.sbuf_tensor(name, shape, F32))
        ident, ones, gates = sbuf(whole, "ident", [P, P]), sbuf(whole, "ones", [1, P]), sbuf(whole, "gates", [P, 2])
        cross_attention(nc, whole, I, ident, ones, gates, x1_d, xnT_d)
        o1 = sbuf(whole, "o1", [P, D])
        with ExitStack() as until_experts:
            hT = sbuf(until_experts, "hT", [P, KT, E, B])
            with ExitStack() as until_slots:
                x_stats = sbuf(until_slots, "x_stats", [P, B * TT, 6])
                feed_forward(nc, whole, I, gates, x_stats, x1_d, xnT_d)
                slot_attention(nc, whole, I, ident, ones, x_stats, o1, hT, x1_d, xnT_d)
            experts(nc, whole, I, ident, hT, y_d)
        token_attention(nc, whole, I, ident, gates, o1, x1_d, xnT_d, y_d, out)


INPUTS = ["x", "ctx_1024", "mask_BxS2_ik0", "g_xattn", "g_ffn"] + [f"L0_xattn_{n}" for n in (
    "gamma", "ctx_gamma", "Wq", "Wkv", "Wout", "Wff1", "Wff2")] + ["L0_ffn_slot_query"] + [
    f"L0_ffn_{a}_{w}{n}" for a in "dc" for w in "Wb" for n in "qkvo"] + [
    f"L0_ffn_e_{n}" for n in ("ln_g", "ln_b", "W1", "b1", "Wg", "bg", "W2", "b2")]


def kernel(**inputs):
    import numpy as np
    import concourse.bacc as bacc
    from concourse.bass_utils import run_bass_kernel_spmd

    nc = bacc.Bacc("TRN2", target_bir_lowering=False, num_devices=1)
    arrays, I = {}, {}
    for name in INPUTS:
        a = np.ascontiguousarray(inputs[name])
        arrays[f"in_{name}"] = a
        I[name] = nc.dram_tensor(f"in_{name}", a.shape, mybir.dt.from_np(a.dtype), kind="ExternalInput").ap()
    out = nc.dram_tensor("out", [B, S, D], F32, kind="ExternalOutput").ap()
    gated_block(nc, I, out)
    return run_bass_kernel_spmd(nc, [arrays], core_ids=[0]).results[0]["out"]
```

```python
import concourse.bass as bass
from concourse import mybir
from contextlib import ExitStack

F32 = mybir.dt.float32
F32R = mybir.dt.float32r
I32 = mybir.dt.int32
ALU = mybir.AluOpType
ACT = mybir.ActivationFunctionType
AX = mybir.AxisListType

P = 128
B, S, D = 8, 512, 512
KT = D // P
TT = S // P
H, DH = 16, 64
HP = H // 2
FF = 2048
NS, E = 16, 16
SH, SD = 16, 32
HS = SH * NS
EPS = 1e-5
MASKED = -1e30


def plain(ap):
    return ap.bitcast(F32)


def products(hi_lo_w, hi_lo_m):
    (w_hi, w_lo), (m_hi, m_lo) = hi_lo_w, hi_lo_m
    return ((w_hi, m_hi), (w_hi, m_lo), (w_lo, m_hi))


class Memory:

    def __init__(self, nc, stage, whole):
        self.nc, self.stage, self.whole = nc, stage, whole

    def sbuf(self, name, shape, dtype=F32):
        return self.stage.enter_context(self.nc.sbuf_tensor(name, shape, dtype))

    def bank(self, name):
        return self.stage.enter_context(self.nc.psum_tensor(name, [P, 512], F32))

    def sem(self, name):
        return self.whole.enter_context(self.nc.semaphore(name))


def rows_mean_var(nc, stats, mean, var, half):
    col = lambda i: stats[:, :, i:i + 1].rearrange("p n o -> p (n o)")
    v = nc.vector
    v.tensor_tensor(half, col(1), col(4), ALU.subtract)
    v.tensor_tensor(mean, col(1), col(4), ALU.add)
    v.tensor_tensor(var, col(2), col(5), ALU.add)
    v.drain()
    v.tensor_scalar(mean, mean, 0.5, None, ALU.mult)
    v.tensor_scalar(half, half, 0.5, None, ALU.mult)
    v.tensor_scalar(var, var, 1.0 / D, None, ALU.mult)
    v.drain()
    v.tensor_tensor(half, half, half, ALU.mult)
    v.drain()
    v.tensor_tensor(var, var, half, ALU.add)
    v.drain()


def cross_attention(nc, whole, I, ident, gates, load_wff1, x1_d, xnT_d):
    with ExitStack() as stage:
        mem = Memory(nc, stage, whole)
        x_v = I["x"].rearrange("b (t p) d -> b p t d", p=P)
        c_v = I["ctx_1024"].rearrange("b (t p) d -> b p t d", p=P)
        x1_v = x1_d.rearrange("b (t p) d -> b p t d", p=P)
        mask = I["mask_BxS2_ik0"]

        wq_hi = mem.sbuf("wq_hi", [P, KT, H * DH], F32R)
        wq_lo = mem.sbuf("wq_lo", [P, KT, H * DH], F32R)
        wkv_hi = mem.sbuf("wkv_hi", [P, KT, 4 * DH], F32R)
        wkv_lo = mem.sbuf("wkv_lo", [P, KT, 4 * DH], F32R)
        wo_hi = mem.sbuf("wo_hi", [P, HP, D], F32R)
        wo_lo = mem.sbuf("wo_lo", [P, HP, D], F32R)
        gam = mem.sbuf("gam", [P, 2, KT])
        sel_max = mem.sbuf("sel_max", [P, H, P], F32R)
        sel_sum = mem.sbuf("sel_sum", [P, 2 * P - 1], F32R)
        sel_pair = mem.sbuf("sel_pair", [P, HP, P], F32R)
        key_bias = mem.sbuf("key_bias", [P, B * TT])
        block_bias = mem.sbuf("block_bias", [P, TT])
        live = mem.sbuf("live", [1, B * TT], I32)
        more = mem.sbuf("more", [1, B * TT], I32)
        many = mem.sbuf("many", [1, B], I32)
        start = mem.sbuf("start", [1, B], I32)
        first_live = mem.sbuf("first_live", [P, P])
        kk_max = mem.sbuf("kk_max", [P, P], F32R)
        k_sum, k_count = (mem.sbuf(n, [P, 1]) for n in ("k_sum", "k_count"))
        stats = mem.sbuf("stats", [P, 2 * TT, 6])
        mean, var, spread, rstd = (mem.sbuf(n, [P, 2 * TT]) for n in ("mean", "var", "spread", "rstd"))
        cin = mem.sbuf("cin", [P, TT, D])
        xin = mem.sbuf("xin", [P, TT, D])
        nT_hi = mem.sbuf("nT_hi", [P, KT, S], F32R)
        nT_lo = mem.sbuf("nT_lo", [P, KT, S], F32R)
        kk_hi = mem.sbuf("kk_hi", [P, S], F32R)
        kk_lo = mem.sbuf("kk_lo", [P, S], F32R)
        vT = mem.sbuf("vT", [P, S])
        val = mem.sbuf("val", [P, TT, 4, P], F32R)
        qs = mem.sbuf("qs", [P, H, S], F32R)
        oT_hi, oT_lo = qs[:, 0:HP, :], qs[:, HP:H, :]
        mask_b = mem.sbuf("mask_b", [P, S])
        mask_i = mask_b[:, :].bitcast(I32)
        m_rows = mem.sbuf("m_rows", [P, TT, H])
        m_heads = mem.sbuf("m_heads", [P, S], F32R)
        prob = mem.sbuf("prob", [P, 2, S])
        prob_hi = mem.sbuf("prob_hi", [P, 2, S], F32R)
        prob_lo = mem.sbuf("prob_lo", [P, 2, S], F32R)
        acc = mem.sbuf("acc", [P, HP, S])
        acc_sum = mem.sbuf("acc_sum", [P, S])
        inv_hi = mem.sbuf("inv_hi", [P, S], F32R)
        inv_lo = mem.sbuf("inv_lo", [P, S], F32R)
        xres = mem.sbuf("xres", [P, 2, D])
        live_col = block_bias[0:B * TT, 0:1]
        mask_rows, bias_rows = acc_sum[0:B * TT, 0:P].bitcast(I32), vT[0:B * TT, 0:P]
        x_rows = [xres[:, 0, :], xres[:, 1, :], prob[:, 0, :], prob[:, 1, :]]
        live_f, rank, from_end, is_first = (xres[0:1, 0, i * B * TT:(i + 1) * B * TT].rearrange("o (b j) -> o b j", j=TT) for i in range(4))
        best, begin = (xres[0:1, 1, i * B:(i + 1) * B] for i in range(2))
        raw = [acc[:, 2 * i:2 * i + 2, :].rearrange("p i s -> p (i s)") for i in range(HP // 2)]
        RAW = len(raw)

        G = [mem.bank(f"att_general{i}") for i in range(3)]
        SC = [mem.bank(f"att_scores{i}") for i in range(2)]
        OB = [mem.bank(f"att_out{i}") for i in range(2)]
        SUM = mem.bank("att_sum")
        OUT = OB + [SUM, SC[1]]
        MX = SC + OB

        ctx_in, x_in, mask_b_in = (mem.sem(n) for n in ("ctx_in", "x_in", "mask_b_in"))
        var_ready, sd_ready, rstd_ready, norm_begun = (mem.sem(n) for n in ("var_ready", "sd_ready", "rstd_ready", "norm_begun"))
        normed = mem.sem("normed")
        raw_in = [mem.sem(f"raw_in{i}") for i in range(RAW)]
        w_hi_done, w_lo_done = mem.sem("w_hi_done"), mem.sem("w_lo_done")
        small_in, mask_in, masks_ready, masks_turned = (mem.sem(n) for n in ("small_in", "mask_in", "masks_ready", "masks_turned"))
        ident_zero, ident_ready = mem.sem("ident_zero"), mem.sem("ident_ready")

        wkv_v = I["L0_xattn_Wkv"].rearrange("(k p) n -> p k n", p=P)
        wo_v = I["L0_xattn_Wout"].rearrange("(i p) n -> p i n", p=P)
        chunks = [(wkv_hi[:, :, :].rearrange("p k n -> p (k n)"), wkv_lo[:, :, :].rearrange("p k n -> p (k n)"))]
        chunks += [(wq_hi[:, k, :], wq_lo[:, k, :]) for k in range(KT)]
        chunks += [(wo_hi[:, 2 * i:2 * i + 2, :].rearrange("p i n -> p (i n)"),
                    wo_lo[:, 2 * i:2 * i + 2, :].rearrange("p i n -> p (i n)")) for i in range(HP // 2)]
        arrivals, landed = [0] * RAW, []
        for c in range(len(chunks)):
            arrivals[c % RAW] += 64 if c == 0 else 16
            landed.append(arrivals[c % RAW])
        POOL_FROM = RAW + 2
        ahead = 2

        def context_statistics(dve, b, t):
            if t == 0:
                dve.wait_ge(ctx_in, b * 16 + 16)
            nc.vector.bn_stats(stats[:, t, :], cin[:, t, :])

        def statistics(dve, b):
            dve.wait_ge(x_in, b * 16 + 16)
            for t in range(TT):
                nc.vector.bn_stats(stats[:, TT + t, :], xin[:, t, :])
            nc.vector.drain()
            rows_mean_var(nc, stats[:, :, :], mean[:, :], var[:, :], spread[:, :])
            nc.vector.tensor_scalar(spread[:, 0:TT], var[:, 0:TT], EPS, None, ALU.add)
            nc.vector.tensor_scalar(spread[:, TT:2 * TT], var[:, TT:2 * TT], 1 + EPS, EPS * EPS, ALU.mult, ALU.add).then_inc(var_ready, 1)

        def deviations(dve, b):
            dve.wait_ge(sd_ready, b + 1)
            nc.vector.reciprocal(rstd[:, :], spread[:, :]).then_inc(rstd_ready, 1)

        def norm(engine):
            for c, src in enumerate((cin, xin)):
                for t in range(TT):
                    n = c * TT + t
                    last = engine.tensor_scalar(src[:, t, :], src[:, t, :], mean[:, n:n + 1], rstd[:, n:n + 1], ALU.subtract, ALU.mult)
                last.then_inc(normed, 1)

        with nc.Block() as block:
            @block.sync
            def _(sp):
                sp.dma_start(mask_rows, mask.rearrange("b (j p) -> (b j) p", p=P)).then_inc(mask_in, 16)
                sp.dma_start(cin[:, :, :], c_v[0]).then_inc(ctx_in, 16)
                sp.dma_start(xin[:, :, :], x_v[0]).then_inc(x_in, 16)
                for c in range(len(chunks)):
                    if c >= RAW:
                        sp.wait_ge(w_lo_done, c - RAW + 1)
                    slot = raw[c % RAW]
                    if c == 0:
                        four = slot.rearrange("p (k n) -> p k n", k=KT)
                        for n in range(4):
                            sp.dma_start(four[:, :, n * DH:(n + 1) * DH],
                                         wkv_v[:, :, (n // 2) * DH:(n // 2 + 1) * DH]).then_inc(raw_in[c % RAW], 16)
                    elif c <= KT:
                        sp.dma_start(slot, I["L0_xattn_Wq"][(c - 1) * P:c * P, :]).then_inc(raw_in[c % RAW], 16)
                    else:
                        i = 2 * (c - KT - 1)
                        sp.dma_start(slot.rearrange("p (i n) -> p i n", i=2), wo_v[:, i:i + 2, :]).then_inc(raw_in[c % RAW], 16)
                    if c == 0:
                        sp.dma_start(gates[:, 0:1], I["g_xattn"].unsqueeze(0).to_broadcast([P, 1])).then_inc(small_in, 16)
                        sp.dma_start(gates[:, 1:2], I["g_ffn"].unsqueeze(0).to_broadcast([P, 1])).then_inc(small_in, 16)
                        sp.dma_start(gam[:, 0, :], I["L0_xattn_gamma"].rearrange("(k p) -> p k", p=P), allow_slow_non_contiguous=True).then_inc(small_in, 16)
                        sp.dma_start(gam[:, 1, :], I["L0_xattn_ctx_gamma"].rearrange("(k p) -> p k", p=P), allow_slow_non_contiguous=True).then_inc(small_in, 16)

            @block.gpsimd
            def _(pool):
                nc.gpsimd.memset(ident[:, :], 0.0).then_inc(ident_zero, 1)
                pool.wait_ge(ident_zero, 1)
                nc.gpsimd.affine_select(out=ident[:, :], in_=ident[:, :], compare_op=ALU.not_equal, fill=1.0,
                                        base=0, pattern=[[-1, P]], channel_multiplier=1).then_inc(ident_ready, 1)
                nc.gpsimd.memset(prob[:, 0, 0:P], 0.0)
                nc.gpsimd.memset(plain(sel_sum[:, :]), 0.0)
                nc.gpsimd.drain()
                nc.gpsimd.memset(plain(sel_sum[:, P - 1:P]), 1.0)
                zeros = prob[:, 0, 0:P]
                for h in range(H):
                    nc.gpsimd.tensor_scalar(sel_max[:, h, :], zeros, ident[:, h:h + 1], -1.0, ALU.add, ALU.mult)
                    nc.gpsimd.tensor_scalar(sel_pair[:, h // 2, (h % 2) * DH:(h % 2 + 1) * DH], zeros[:, 0:DH],
                                            ident[:, h:h + 1], None, ALU.add)
                for t in (m_heads[:, :], inv_hi[:, :], inv_lo[:, :], val[:, :, :, :]):
                    nc.gpsimd.memset(plain(t), 0.0)
                for c in range(POOL_FROM, len(chunks)):
                    hi, lo = chunks[c]
                    pool.wait_ge(w_hi_done, c + 1)
                    nc.gpsimd.tensor_tensor(lo, raw[c % RAW], plain(hi), ALU.subtract)

            @block.scalar
            def _(act):
                for c, (hi, _) in enumerate(chunks):
                    if c == ahead:
                        act.wait_ge(var_ready, 1)
                        nc.scalar.activation(spread[:, :], spread[:, :], ACT.Sqrt).then_inc(sd_ready, 1)
                    act.wait_ge(raw_in[c % RAW], landed[c])
                    nc.scalar.copy(hi, raw[c % RAW]).then_inc(w_hi_done, 1)
                act.wait_ge(small_in, 64)
                nc.scalar.activation(gates[:, :], gates[:, :], ACT.Tanh)

            @block.vector
            def _(dve):
                dve.wait_ge(mask_in, 16)
                nc.vector.tensor_scalar(bias_rows, mask_rows, 0.0, MASKED, ALU.is_equal, ALU.mult)
                nc.vector.drain()
                nc.vector.tensor_reduce(live_col, bias_rows, AX.X, ALU.max).then_inc(masks_ready, 1)
                dve.wait_ge(masks_turned, 1)
                nc.vector.tensor_copy(key_bias[:, :], G[0][:, 0:B * TT])
                flat = lambda a: a.rearrange("o b j -> o (b j)")
                for j in range(TT):
                    nc.vector.memset(from_end[:, :, j:j + 1], float(TT - j))
                nc.vector.tensor_scalar(flat(live_f), G[1][0:1, 0:B * TT], MASKED / 2, None, ALU.is_ge)
                nc.vector.drain()
                nc.vector.tensor_copy(live[:, :], flat(live_f))
                nc.vector.tensor_tensor(rank, live_f, from_end, ALU.mult)
                nc.vector.drain()
                nc.vector.tensor_reduce(best, rank, AX.X, ALU.max)
                nc.vector.drain()
                nc.vector.tensor_scalar(best, best, 1.0, None, ALU.max)
                nc.vector.drain()
                nc.vector.tensor_scalar(begin, best, float(-P), float(S), ALU.mult, ALU.add)
                nc.vector.tensor_tensor(is_first, rank, best.unsqueeze(2).to_broadcast([1, B, TT]), ALU.is_equal)
                nc.vector.drain()
                nc.vector.tensor_copy(start[:, :], begin)
                nc.vector.tensor_tensor(rank, live_f, is_first, ALU.subtract)
                nc.vector.drain()
                nc.vector.tensor_copy(more[:, :], flat(rank))
                nc.vector.tensor_reduce(best, rank, AX.X, ALU.max)
                nc.vector.drain()
                nc.vector.tensor_copy(many[:, :], best)

                def split(c):
                    hi, lo = chunks[c]
                    dve.wait_ge(w_hi_done, c + 1)
                    nc.vector.tensor_tensor(lo, raw[c % RAW], plain(hi), ALU.subtract).then_inc(w_lo_done, 1)

                for t in range(TT):
                    context_statistics(dve, 0, t)
                statistics(dve, 0)
                for c in range(ahead):
                    split(c)
                deviations(dve, 0)
                nc.vector.drain()
                norm(nc.vector)
                for c in range(ahead, POOL_FROM):
                    split(c)

            @block.tensor
            def _(pe):
                pe.wait_ge(masks_ready, 1)
                pe.wait_ge(ident_ready, 1)
                nc.tensor.transpose(G[0][:, 0:B * TT], bias_rows, ident[0:B * TT, 0:B * TT])
                nc.tensor.matmul(G[1][0:1, 0:B * TT], live_col, ident[0:B * TT, 0:B * TT], start=True, stop=True).then_inc(masks_turned, 1)

        xres_in, x1_out, xnT_out = (mem.sem(n) for n in ("xres_in", "x1_out", "xnT_out"))
        g_ready, g_free = mem.sem("g_ready"), mem.sem("g_free")
        g_hi = mem.sem("g_hi")
        max_scores, max_taken, m_ready, m_turned, m_heads_ready = (
            mem.sem(n) for n in ("max_scores", "max_taken", "m_ready", "m_turned", "m_heads_ready"))
        max_begun = mem.sem("max_begun")
        scores, exps, low_probs, head_out, out_taken = (
            mem.sem(n) for n in ("scores", "exps", "low_probs", "head_out", "out_taken"))
        acc_begun, acc_clear, inv_ready, o_hi_done, o_lo_done, out_ready, x_added = (
            mem.sem(n) for n in ("acc_begun", "acc_clear", "inv_ready", "o_hi_done", "o_lo_done", "out_ready", "x_added"))

        U_V, U_VAL = 0, 3
        U_SPREAD = [1, 2, 4, 6, 8, 10, 12, 13]
        U_X = [5, 7, 9, 11]
        U_Q = 14
        U_CTX = U_Q + HP
        U_K = U_CTX + KT
        PER = U_K + 1
        NG = len(G)
        assert PER % NG == 0
        HI_K, HI_VAL, HI_X, HI_Q = 0, 1, 3, 3 + KT
        HI_CTX = HI_Q + 2 * HP
        HI = HI_CTX + KT
        MAXES = (TT + 1) * HP
        OUTS = HP + 1
        q_scale = DH ** -0.5

        def of(ap, b):
            return ap[b] if isinstance(b, int) else ap[bass.ds(b, 1)].rearrange("o p t d -> (o p) t d")

        def first(b):
            return isinstance(b, int) and b == 0

        def last_batch(b):
            return isinstance(b, int) and b == B - 1

        def used(b, u):
            return (b + 1) * PER + u

        def tail_steps(begin, end, values, x):
            begin(0)
            begin(1)
            values()
            for i in range(HP):
                end(i)
                if i + 2 < HP:
                    begin(i + 2)
                if i < KT:
                    x(i)

        with nc.Block() as block:
            @block.sync
            def _(sp):
                def context(b, nxt):
                    sp.wait_ge(g_ready, used(b, U_K))
                    sp.dma_start(cin[:, :, :], of(c_v, nxt)).then_inc(ctx_in, 16)

                def rows(b, nxt):
                    sp.wait_ge(g_ready, used(b, U_X[-1] + 1))
                    sp.dma_start(xin[:, :, :], of(x_v, nxt)).then_inc(x_in, 16)

                def next_mask(b, nxt):
                    sp.wait_ge(max_taken, (b + 1) * MAXES)
                    src = mask[nxt:nxt + 1, :] if isinstance(nxt, int) else mask[bass.ds(nxt, 1), :]
                    sp.dma_start(mask_i, src.to_broadcast([P, S])).then_inc(mask_b_in, 16)

                def keep_xnT(b):
                    sp.wait_ge(g_free, used(b, U_X[-1] + 1))
                    for part, t in enumerate((nT_hi, nT_lo)):
                        sp.dma_start(of(xnT_d[part], b), plain(t[:, :, :])).then_inc(xnT_out, 16)

                def residual(b, prev):
                    sp.wait_ge(out_taken, b * (TT * OUTS))
                    for t in range(TT):
                        sp.dma_start(x_rows[t], of(x_v, prev)[:, t, :]).then_inc(xres_in, 16)

                def store(b, prev):
                    for t in range(TT):
                        sp.wait_ge(x_added, (b - 1) * TT + t + 1)
                        sp.dma_start(of(x1_v, prev)[:, t, :], x_rows[t]).then_inc(x1_out, 16)

                sp.dma_start(mask_i, mask[0:1, :].to_broadcast([P, S])).then_inc(mask_b_in, 16)
                context(-1, 1)
                rows(0, 1)
                keep_xnT(0)
                context(0, 2)
                next_mask(0, 1)
                with sp.Fori(1, B - 2) as b:
                    residual(b, b - 1)
                    rows(b, b + 1)
                    keep_xnT(b)
                    store(b, b - 1)
                    context(b, b + 2)
                    next_mask(b, b + 1)
                residual(B - 2, B - 3)
                rows(B - 2, B - 1)
                keep_xnT(B - 2)
                store(B - 2, B - 3)
                next_mask(B - 2, B - 1)
                residual(B - 1, B - 2)
                keep_xnT(B - 1)
                store(B - 1, B - 2)
                sp.wait_ge(g_ready, used(B - 1, U_Q + HP))
                load_wff1(sp)
                residual(B, B - 1)
                store(B, B - 1)
                sp.wait_ge(xnT_out, B * 32)

            @block.tensor
            def _(pe):
                def claim(b, u):
                    pe.wait_ge(g_free, used(b, u - (NG - 1)))
                    return G[u % NG]

                def skip(uses):
                    pe.drain().then_inc(g_ready, uses)

                def turn(b, u, src, k):
                    bank = claim(b, u)
                    for t in range(TT):
                        last = nc.tensor.transpose(bank[:, t * P:(t + 1) * P], src[:, t, k * P:(k + 1) * P], ident[:, :])
                    last.then_inc(g_ready, 1)

                def project(bank, cols, w_hi, w_lo):
                    n = 0
                    for k in range(KT):
                        for w, m in products((w_hi, w_lo), (nT_hi, nT_lo)):
                            last = nc.tensor.matmul(bank[:, :], w[:, k, cols], m[:, k, :], start=n == 0, stop=n == 3 * KT - 1)
                            n += 1
                    return last

                def context(b):
                    pe.wait_ge(normed, 2 * b + 3)
                    for k in range(KT):
                        turn(b, U_CTX + k, cin, k)

                def keys(b):
                    pe.wait_ge(g_free, used(b, U_K))
                    project(claim(b, U_K), slice(0, 2 * DH), wkv_hi, wkv_lo).then_inc(g_ready, 1)

                def values(b):
                    project(claim(b, U_V), slice(2 * DH, 4 * DH), wkv_hi, wkv_lo).then_inc(g_ready, 1)

                def tail(b):
                    def spread_inverse(i):
                        if first(b):
                            skip(1)
                            return
                        if i == 0:
                            pe.wait_ge(inv_ready, b)
                        bank = claim(b, U_SPREAD[i])
                        nc.tensor.matmul(bank[:, :], sel_pair[:, i, :], inv_hi[:, :], start=True, stop=False)
                        nc.tensor.matmul(bank[:, :], sel_pair[:, i, :], inv_lo[:, :], start=False, stop=True).then_inc(g_ready, 1)

                    def output(i):
                        if first(b):
                            return
                        pe.wait_ge(o_lo_done, (b - 1) * HP + i + 1)
                        for t in range(TT):
                            for n, (o, w) in enumerate(products((oT_hi, oT_lo), (wo_hi, wo_lo))):
                                last = nc.tensor.matmul(OUT[t][:, :], o[:, i, t * P:(t + 1) * P], w[:, i, :],
                                                        start=i == 0 and n == 0, stop=i == HP - 1 and n == 2)
                        if i == HP - 1:
                            last.then_inc(out_ready, 1)

                    def turn_values():
                        if b is B:
                            skip(1)
                            return
                        bank = claim(b, U_VAL)
                        for j in range(TT):
                            last = nc.tensor.transpose(bank[:, j * P:(j + 1) * P], vT[:, j * P:(j + 1) * P], ident[:, :])
                        last.then_inc(g_ready, 1)

                    def turn_x(k):
                        if b is B:
                            skip(1)
                            return
                        if k == 0:
                            pe.wait_ge(normed, 2 * b + 2)
                        turn(b, U_X[k], xin, k)

                    tail_steps(spread_inverse, output, turn_values, turn_x)

                def pair_scores(b, i, m, keys):
                    pe.wait_ge(g_free, used(b, U_Q + i + 1))
                    pe.wait_ge(max_taken, m - 1 if i else m)
                    for h in (2 * i, 2 * i + 1):
                        for t in range(TT):
                            last = nc.tensor.matmul(MX[h % 4][:, t * P:(t + 1) * P], qs[:, h, t * P:(t + 1) * P], keys, start=True, stop=True)
                    last.then_inc(max_scores, 1)

                def queries(b):
                    pe.wait_ge(g_free, used(b, U_X[-1] + 1))
                    for i in range(HP + KT):
                        if i < HP:
                            project(claim(b, U_Q + i), slice(i * P, (i + 1) * P), wq_hi, wq_lo).then_inc(g_ready, 1)
                        elif last_batch(b):
                            skip(1)
                        else:
                            if i == HP:
                                pe.wait_ge(normed, 2 * b + 3)
                            turn(b, U_CTX + i - HP, cin, i - HP)
                        if i == 2:
                            pe.wait_ge(exps, b * (TT * H))
                            if not first(b):
                                pe.wait_ge(x_added, b * TT)
                        if 2 <= i < HP + 2:
                            pair_scores(b, i - 2, b * MAXES + (i - 2), kk_max[:, :])

                def other_maxima(b):
                    n = b * MAXES + HP
                    with pe.If(pe.value_load(many[0:1, bass.ds(b, 1)]) == 1):
                        on = [pe.value_load(more[0:1, bass.ds(b * TT + j, 1)]) for j in range(TT)]
                        for j in range(TT):
                            with pe.If(on[j] == 1):
                                for i in range(HP):
                                    pair_scores(b, i, n + (j * HP + i), kk_hi[:, j * P:(j + 1) * P])
                            with pe.Else():
                                pe.drain().then_inc(max_scores, HP)
                                pe.drain().then_inc(max_taken, HP)
                    with pe.Else():
                        pe.drain().then_inc(max_scores, TT * HP)
                        pe.drain().then_inc(max_taken, TT * HP)

                def turn_maxima(b):
                    pe.wait_ge(m_ready, b + 1)
                    for t in range(TT):
                        last = nc.tensor.transpose(SC[0][0:H, t * P:(t + 1) * P], m_rows[:, t, :], ident[:, :])
                    last.then_inc(m_turned, 1)

                def attend(b, on):
                    pe.wait_ge(m_heads_ready, b + 1)
                    pe.wait_ge(max_taken, (b + 1) * MAXES)
                    for j in range(TT):
                        n = b * TT + j
                        keys = slice(j * P, (j + 1) * P)
                        with pe.If(on[j] == 1):
                            for h in range(H + 1):
                                if h < H:
                                    pe.wait_ge(exps, n * H + max(h - 1, 0))
                                    bank = SC[h % 2]
                                    nc.tensor.matmul(bank[:, :], kk_hi[:, keys], qs[:, h, :], start=True, stop=False)
                                    nc.tensor.matmul(bank[:, :], kk_lo[:, keys], qs[:, h, :], start=False, stop=False)
                                    nc.tensor.matmul(bank[:, :], sel_max[:, h, :], m_heads[:, :], start=False, stop=True).then_inc(scores, 1)
                                if h >= 1:
                                    g = h - 1
                                    i, odd, s = g // 2, g % 2, g % 2
                                    pe.wait_ge(exps, n * H + g + 1)
                                    if odd == 0:
                                        pe.wait_ge(out_taken, n * OUTS + max(i - 1, 0))
                                    v_hi, v_lo = val[:, j, odd, :], val[:, j, 2 + odd, :]
                                    one = sel_sum[:, P - 1 - g:2 * P - 1 - g]
                                    nc.tensor.matmul(OB[i % 2][:, :], v_hi, prob_hi[:, s, :], start=not odd, stop=False)
                                    nc.tensor.matmul(OB[i % 2][:, :], v_lo, prob_hi[:, s, :], start=False, stop=False)
                                    nc.tensor.matmul(SUM[:, :], one, prob_hi[:, s, :], start=g == 0, stop=False)
                                    pe.wait_ge(low_probs, n * H + g + 1)
                                    nc.tensor.matmul(OB[i % 2][:, :], v_hi, prob_lo[:, s, :], start=False, stop=bool(odd))
                                    nc.tensor.matmul(SUM[:, :], one, prob_lo[:, s, :], start=False, stop=g == H - 1).then_inc(head_out, 1)
                        with pe.Else():
                            pe.drain().then_inc(scores, H)
                            pe.drain().then_inc(head_out, H)

                def flags(b):
                    return [pe.value_load(live[0:1, bass.ds(b * TT + j, 1)]) for j in range(TT)]

                def batch(b):
                    values(b)
                    tail(b)
                    on = flags(b)
                    queries(b)
                    other_maxima(b)
                    if last_batch(b):
                        skip(1)
                    else:
                        keys(b)
                    turn_maxima(b)
                    attend(b, on)

                skip(U_CTX)
                context(-1)
                keys(-1)
                batch(0)
                with pe.Fori(1, B - 1) as b:
                    batch(b)
                batch(B - 1)
                skip(1)
                tail(B)

            @block.scalar
            def _(act):
                def context(b):
                    if not (isinstance(b, int) and b < 0):
                        act.wait_ge(xnT_out, (b + 1) * 32)
                    for k in range(KT):
                        act.wait_ge(g_ready, used(b, U_CTX + k + 1))
                        nc.scalar.activation(nT_hi[:, k, :], G[(U_CTX + k) % NG][:, :], ACT.Copy, scale=gam[:, 1, k:k + 1]).then_inc(g_hi, 1)

                def keys(b):
                    act.wait_ge(g_ready, used(b, U_V + 1))
                    nc.scalar.copy(kk_hi[:, :], G[U_K % NG][:, :]).then_inc(g_hi, 1)

                def tail(b):
                    def high(i):
                        if first(b):
                            return
                        act.wait_ge(g_free, used(b, U_SPREAD[i] + 1))
                        nc.scalar.copy(oT_hi[:, i, :], acc[:, i, :]).then_inc(o_hi_done, 1)

                    def values():
                        if b is B:
                            return
                        act.wait_ge(g_ready, used(b, U_VAL + 1))
                        turned = G[U_VAL % NG][:, :].rearrange("p (j v) -> p j v", j=TT)
                        for odd in range(2):
                            cols = slice(odd * DH, (odd + 1) * DH)
                            nc.scalar.copy(val[:, :, odd, cols], turned[:, :, cols]).then_inc(g_hi, 1)

                    def x(k):
                        if b is B:
                            return
                        act.wait_ge(g_ready, used(b, U_X[k] + 1))
                        nc.scalar.activation(nT_hi[:, k, :], G[U_X[k] % NG][:, :], ACT.Copy, scale=gam[:, 0, k:k + 1]).then_inc(g_hi, 1)

                    tail_steps(high, lambda i: None, values, x)

                def deviations(b):
                    act.wait_ge(var_ready, b + 1)
                    nc.scalar.activation(spread[:, :], spread[:, :], ACT.Sqrt).then_inc(sd_ready, 1)

                def queries(b):
                    for i in range(HP):
                        if i == HP - 1 and not first(b):
                            act.wait_ge(x1_out, b * (TT * 16))
                        act.wait_ge(g_ready, used(b, U_Q + i + 1))
                        for odd in range(2):
                            half = slice(odd * DH, (odd + 1) * DH)
                            nc.scalar.activation(qs[half, 2 * i + odd, :], G[(U_Q + i) % NG][half, :], ACT.Copy, scale=q_scale).then_inc(g_hi, 1)

                def attend(b, on):
                    for j in range(TT):
                        n = b * TT + j
                        with act.If(on[j] == 1):
                            bias = block_bias[:, j:j + 1]
                            nc.scalar.copy(bias, key_bias[:, bass.ds(n, 1)])
                            act.drain()
                            for h in range(H):
                                act.wait_ge(scores, n * H + h + 1)
                                act.wait_ge(head_out, n * H + max(h - 1, 0))
                                nc.scalar.activation(prob[:, h % 2, :], SC[h % 2][:, :], ACT.Exp, bias=bias)
                                nc.scalar.activation(prob_hi[:, h % 2, :], SC[h % 2][:, :], ACT.Exp, bias=bias).then_inc(exps, 1)
                        with act.Else():
                            act.drain().then_inc(exps, H)

                def flags(b):
                    return [act.value_load(live[0:1, bass.ds(b * TT + j, 1)]) for j in range(TT)]

                def batch(b):
                    keys(b)
                    tail(b)
                    if not last_batch(b):
                        deviations(b + 1)
                    queries(b)
                    if not last_batch(b):
                        context(b)
                    attend(b, flags(b))

                act.drain().then_inc(g_hi, HI_CTX)
                context(-1)
                batch(0)
                with act.Fori(1, B - 1) as b:
                    batch(b)
                batch(B - 1)
                tail(B)

            @block.gpsimd
            def _(pool):
                def clear():
                    nc.gpsimd.memset(acc[:, :, :], 0.0).then_inc(acc_clear, 1)

                def norm_rows(b):
                    pool.wait_ge(rstd_ready, b + 1)
                    pool.sem_inc(norm_begun, 1)
                    norm(nc.gpsimd)

                def clear_after(b):
                    pool.wait_ge(o_lo_done, b * HP)
                    pool.sem_inc(acc_begun, 1)
                    clear()

                clear()
                norm_rows(1)
                with pool.Fori(1, B - 1) as b:
                    clear_after(b)
                    norm_rows(b + 1)
                clear_after(B - 1)

            @block.vector
            def _(dve):
                def context(b, k):
                    dve.wait_ge(g_hi, (b + 1) * HI + HI_CTX + k + 1)
                    nc.vector.scalar_tensor_tensor(nT_lo[:, k, :], G[(U_CTX + k) % NG][:, :], gam[:, 1, k:k + 1],
                                                   plain(nT_hi[:, k, :]), ALU.mult, ALU.subtract).then_inc(g_free, 1)

                def inverse(b):
                    nc.vector.reciprocal(acc_sum[0:H, :], acc_sum[0:H, :])
                    nc.vector.drain()
                    nc.vector.tensor_copy(inv_hi[0:H, :], acc_sum[0:H, :])
                    nc.vector.drain()
                    nc.vector.tensor_tensor(inv_lo[0:H, :], acc_sum[0:H, :], plain(inv_hi[0:H, :]), ALU.subtract).then_inc(inv_ready, 1)
                    nc.vector.drain()

                def keys_values(b):
                    dve.wait_ge(g_hi, (b + 1) * HI + HI_K + 1)
                    nc.vector.tensor_tensor(kk_lo[:, :], G[U_K % NG][:, :], plain(kk_hi[:, :]), ALU.subtract).then_inc(g_free, 1)
                    dve.wait_ge(g_ready, used(b, U_V + 1))
                    nc.vector.tensor_copy(vT[:, :], G[U_V % NG][:, :]).then_inc(g_free, 1)

                def mask_biases(b):
                    first_block = dve.value_load(start[0:1, bass.ds(b, 1)])
                    dve.wait_ge(mask_b_in, b * 16 + 16)
                    nc.vector.tensor_scalar(mask_b[:, :], mask_i, 0.0, MASKED, ALU.is_equal, ALU.mult)
                    nc.vector.drain()
                    nc.vector.tensor_scalar(first_live[:, :], mask_b[:, bass.ds(first_block, P)], MASKED / 2, None, ALU.is_ge)
                    nc.vector.tensor_copy(kk_max[:, :], kk_hi[:, bass.ds(first_block, P)])
                    nc.vector.drain()
                    nc.vector.tensor_reduce(k_count[:, :], first_live[:, :], AX.X, ALU.add)
                    nc.vector.tensor_tensor(kk_max[:, :], plain(kk_max[:, :]), first_live[:, :], ALU.mult)
                    nc.vector.drain()
                    nc.vector.tensor_reduce(k_sum[:, :], plain(kk_max[:, :]), AX.X, ALU.add)
                    nc.vector.tensor_scalar(k_count[:, :], k_count[:, :], 1.0, None, ALU.max)
                    nc.vector.tensor_scalar(first_live[:, :], first_live[:, :], -1.0, 1.0, ALU.mult, ALU.add)
                    nc.vector.drain()
                    nc.vector.reciprocal(k_count[:, :], k_count[:, :])
                    nc.vector.drain()
                    nc.vector.tensor_tensor(k_sum[:, :], k_sum[:, :], k_count[:, :], ALU.mult)
                    nc.vector.drain()
                    nc.vector.scalar_tensor_tensor(kk_max[:, :], first_live[:, :], k_sum[:, 0:1], plain(kk_max[:, :]), ALU.mult, ALU.add)

                def skip(uses):
                    nc.vector.drain().then_inc(g_free, uses)

                def tail(b):
                    def normalise(i):
                        if first(b):
                            skip(1)
                            return
                        dve.wait_ge(g_ready, used(b, U_SPREAD[i] + 1))
                        nc.vector.tensor_tensor(acc[:, i, :], acc[:, i, :], G[U_SPREAD[i] % NG][:, :], ALU.mult).then_inc(g_free, 1)
                        for pair in {0: (), 1: (0, 1)}.get(i, (i,)):
                            low(pair)

                    def low(i):
                        dve.wait_ge(o_hi_done, (b - 1) * HP + i + 1)
                        nc.vector.tensor_tensor(oT_lo[:, i, :], acc[:, i, :], plain(oT_hi[:, i, :]), ALU.subtract).then_inc(o_lo_done, 1)

                    def values():
                        if b is B:
                            skip(1)
                            return
                        dve.wait_ge(g_hi, (b + 1) * HI + HI_VAL + 2)
                        turned = G[U_VAL % NG][:, :].rearrange("p (j v) -> p j v", j=TT)
                        for odd in range(2):
                            cols = slice(odd * DH, (odd + 1) * DH)
                            last = nc.vector.tensor_tensor(val[:, :, 2 + odd, cols], turned[:, :, cols], plain(val[:, :, odd, cols]), ALU.subtract)
                        last.then_inc(g_free, 1)

                    def x(k):
                        if b is B:
                            skip(1)
                            return
                        dve.wait_ge(g_hi, (b + 1) * HI + HI_X + k + 1)
                        nc.vector.scalar_tensor_tensor(nT_lo[:, k, :], G[U_X[k] % NG][:, :], gam[:, 0, k:k + 1],
                                                       plain(nT_hi[:, k, :]), ALU.mult, ALU.subtract).then_inc(g_free, 1)
                        if k == 0:
                            mask_biases(b)
                        if not last_batch(b):
                            context_statistics(dve, b + 1, k)

                    tail_steps(normalise, lambda i: None, values, x)

                def add_rows(b):
                    dve.wait_ge(xres_in, b * (TT * 16))
                    dve.wait_ge(out_ready, b)
                    for t in range(TT):
                        nc.vector.scalar_tensor_tensor(x_rows[t], OUT[t][:, :], gates[:, 0:1], x_rows[t], ALU.mult, ALU.add).then_inc(x_added, 1)

                def split_queries(b, i):
                    dve.wait_ge(g_hi, (b + 1) * HI + HI_Q + 2 * i + 2)
                    bank = G[(U_Q + i) % NG]
                    for odd in range(2):
                        here, there = slice(odd * DH, (odd + 1) * DH), slice((1 - odd) * DH, (2 - odd) * DH)
                        last = nc.vector.scalar_tensor_tensor(qs[there, 2 * i + odd, :], bank[here, :], q_scale,
                                                              plain(qs[here, 2 * i + odd, :]), ALU.mult, ALU.subtract)
                    last.then_inc(g_free, 1)

                def pair_maxima(i, m, bias):
                    dve.wait_ge(max_scores, m + 1)
                    dve.sem_inc(max_begun, 1)
                    for h in (2 * i, 2 * i + 1):
                        for t in range(TT):
                            here = MX[h % 4][:, t * P:(t + 1) * P]
                            top = m_rows[:, t, h:h + 1]
                            last = nc.vector.tensor_tensor_reduce(here, here, bias, 1.0, top, ALU.add, ALU.max, top)
                    last.then_inc(max_taken, 1)

                def first_maxima(i, m):
                    dve.wait_ge(max_scores, m + 1)
                    for h in (2 * i, 2 * i + 1):
                        top = m_rows[:, :, h:h + 1].rearrange("p t o -> p (t o)")
                        last = nc.vector.tensor_reduce(top, MX[h % 4][:, :].rearrange("p (t k) -> p t k", t=TT), AX.X, ALU.max)
                    last.then_inc(max_taken, 1)

                def queries(b):
                    for i in range(HP + KT):
                        if i < HP:
                            split_queries(b, i)
                        elif last_batch(b):
                            skip(1)
                        else:
                            context(b, i - HP)
                        if 2 <= i < HP + 2:
                            first_maxima(i - 2, b * MAXES + (i - 2))
                    nc.vector.drain()

                def other_maxima(b):
                    n = b * MAXES + HP
                    with dve.If(dve.value_load(many[0:1, bass.ds(b, 1)]) == 1):
                        on = [dve.value_load(more[0:1, bass.ds(b * TT + j, 1)]) for j in range(TT)]
                        for j in range(TT):
                            with dve.If(on[j] == 1):
                                for i in range(HP):
                                    pair_maxima(i, n + (j * HP + i), mask_b[:, j * P:(j + 1) * P])
                                nc.vector.drain()
                    nc.vector.drain().then_inc(m_ready, 1)

                def maxima_by_head(b):
                    dve.wait_ge(m_turned, b + 1)
                    nc.vector.tensor_copy(m_heads[0:H, :], SC[0][0:H, :]).then_inc(m_heads_ready, 1)

                def attend(b, on):
                    dve.wait_ge(acc_clear, b + 1)
                    nc.vector.memset(acc_sum[0:H, :], 0.0)
                    nc.vector.drain()
                    for j in range(TT):
                        n = b * TT + j
                        with dve.If(on[j] == 1):
                            def add(i):
                                dve.wait_ge(head_out, n * H + 2 * i + 2)
                                nc.vector.tensor_tensor(acc[:, i, :], acc[:, i, :], OB[i % 2][:, :], ALU.add).then_inc(out_taken, 1)

                            for h in range(H):
                                dve.wait_ge(exps, n * H + h + 1)
                                nc.vector.tensor_tensor(prob_lo[:, h % 2, :], prob[:, h % 2, :], plain(prob_hi[:, h % 2, :]),
                                                        ALU.subtract).then_inc(low_probs, 1)
                                if h >= 2 and h % 2 == 0:
                                    add(h // 2 - 1)
                            add(HP - 1)
                            nc.vector.tensor_tensor(acc_sum[0:H, :], acc_sum[0:H, :], SUM[0:H, :], ALU.add).then_inc(out_taken, 1)
                            nc.vector.drain()
                        with dve.Else():
                            nc.vector.drain().then_inc(low_probs, H)
                            nc.vector.drain().then_inc(out_taken, OUTS)

                def flags(b):
                    return [dve.value_load(live[0:1, bass.ds(b * TT + j, 1)]) for j in range(TT)]

                def batch(b):
                    if not first(b):
                        inverse(b - 1)
                    keys_values(b)
                    tail(b)
                    if not last_batch(b):
                        statistics(dve, b + 1)
                    if not first(b):
                        add_rows(b)
                    if not last_batch(b):
                        deviations(dve, b + 1)
                    on = flags(b)
                    queries(b)
                    other_maxima(b)
                    if last_batch(b):
                        skip(1)
                    maxima_by_head(b)
                    attend(b, on)

                skip(U_CTX)
                for k in range(KT):
                    context(-1, k)
                batch(0)
                with dve.Fori(1, B - 1) as b:
                    batch(b)
                batch(B - 1)
                inverse(B - 1)
                skip(1)
                tail(B)
                add_rows(B)
        return x1_out, B * (TT * 16)


FFQ = 4


def wff1_block(I, q, k, c):
    v = I["L0_xattn_Wff1"].rearrange("(k p) (g q n) -> k q g p n", p=P, g=2, q=FFQ)[:, q, c]
    return v if k is None else v[k]


def feed_forward(nc, whole, I, gates, first_w1, first_w1_in, x_stats, slot_w, slot_w_in, x1_begun, x1_d, xnT_d):
    with ExitStack() as stage:
        mem = Memory(nc, stage, whole)
        x_v = x1_d.rearrange("b (t p) d -> b p t d", p=P)
        Q = FFQ
        FT = FF // P // Q
        FQ = FT * P
        w2_v = I["L0_xattn_Wff2"].rearrange("(q f p) n -> f q p n", p=P, q=Q)
        PAIRS = B // 2

        w1 = [[mem.sbuf(f"w1_{part}{i}", [P, KT, 2, FQ], F32R) for part in ("hi", "lo")] for i in range(2)]
        w2 = [[mem.sbuf(f"w2_{part}{i}", [P, FT, D], F32R) for part in ("hi", "lo")] for i in range(2)]
        raw = mem.sbuf("ff_raw", [P, 3, FQ])
        nT = [[mem.sbuf(f"ff_nT_{part}{i}", [P, KT, S], F32R) for part in ("hi", "lo")] for i in range(2)]
        u = [[mem.sbuf(f"u_{part}{i}", [P, FT, S], F32R) for part in ("hi", "lo")] for i in range(2)]
        sig = mem.sbuf("ff_sig", [P, 2, S])
        u32 = mem.sbuf("u32", [P, 2, S])
        xs = [mem.sbuf(f"ff_x{i}", [P, TT, D]) for i in range(2)]
        early_w2 = [t[:, i, :] for t in (sig, u32) for i in range(2)]
        early_place = lambda k, c: first_w1[:, k, c, :] if c < 2 else early_w2[k]
        UP = [[mem.bank(f"ff_{n}{i}") for n in ("a", "gate")] for i in range(2)]
        DN = [mem.bank(f"ff_down{i}") for i in range(2)]

        raw_in = [mem.sem(f"ff_raw_in{i}") for i in range(3)]
        early_in = [*first_w1_in, mem.sem("ff_early_in")]
        raw_hi, raw_lo = mem.sem("ff_raw_hi"), mem.sem("ff_raw_lo")
        nT_in = [mem.sem(f"ff_nT_in{i}") for i in range(2)]
        x_in = [mem.sem(f"ff_x_in{i}") for i in range(2)]
        x_out = [mem.sem(f"ff_x_out{i}") for i in range(2)]
        up_ready, sig_ready, u_ready, u_hi_done, u_lo_done = (
            mem.sem(f"ff_{n}") for n in ("up_ready", "sig_ready", "u_ready", "u_hi_done", "u_lo_done"))
        down_ready, down_taken, rows_seen = (mem.sem(f"ff_{n}") for n in ("down_ready", "down_taken", "rows_seen"))

        def chunk(q, k, c):
            one = lambda ap: ap[k] if isinstance(k, int) else ap[bass.ds(k, 1)].rearrange("o a b -> (o a) b")
            to = lambda t: t[:, k] if isinstance(k, int) else t[:, bass.ds(k, 1)].rearrange("p o n -> p (o n)")
            if c < 2:
                return one(wff1_block(I, q, None, c)), [to(t[:, :, c, :]) for t in w1[q % 2]]
            return one(w2_v[:, q]), [to(t[:, :, :]) for t in w2[q % 2]]

        with nc.Block() as block:
            @block.sync
            def _(sp):
                def load_weights(q, k, n):
                    for c in range(3):
                        sp.wait_ge(raw_lo, n * 3)
                        sp.dma_start(raw[:, c, :], chunk(q, k, c)[0]).then_inc(raw_in[c], 16)

                def load_rows(b, i):
                    for part in range(2):
                        src = xnT_d[part]
                        src = src[b] if isinstance(b, int) else src[bass.ds(b, 1)].rearrange("o p k s -> (o p) k s")
                        sp.dma_start(plain(nT[i][part][:, :, :]), src).then_inc(nT_in[i], 16)

                def load_x(b, i):
                    src = x_v[b] if isinstance(b, int) else x_v[bass.ds(b, 1)].rearrange("o p t d -> (o p) t d")
                    sp.dma_start(xs[i][:, :, :], src).then_inc(x_in[i], 16)

                def store_x(b, i):
                    dst = x_v[b] if isinstance(b, int) else x_v[bass.ds(b, 1)].rearrange("o p t d -> (o p) t d")
                    sp.dma_start(dst, xs[i][:, :, :]).then_inc(x_out[i], 16)

                def step(q, pair, following):
                    n = pair + q * PAIRS
                    here = [pair * 2 + i for i in range(2)]
                    there = [following * 2 + i for i in range(2)] if following is not None else None
                    if q + 1 < Q:
                        load_weights(q + 1, pair, n + PAIRS)
                    for i in range(2):
                        sp.wait_ge(x_out[i], n * 16)
                        load_x(here[i], i)
                    if there is not None:
                        for i in range(2):
                            sp.wait_ge(up_ready, n * (2 * FT) + (i + 1) * FT)
                            load_rows(there[i], i)
                    for i in range(2):
                        if q == Q - 1:
                            sp.wait_ge(rows_seen, here[i] + 1)
                        else:
                            sp.wait_ge(down_taken, (n * 2 + i + 1) * TT)
                        store_x(here[i], i)

                load_rows(0, 0)
                for k in range(PAIRS):
                    sp.dma_start(early_place(k, 2), chunk(0, k, 2)[0]).then_inc(early_in[2], 16)
                load_rows(1, 1)
                sp.wait_ge(raw_lo, PAIRS * 3)
                x1_out, all_stores = x1_begun
                sp.wait_ge(x1_out, all_stores)
                for q in range(Q):
                    if q == Q - 1:
                        sp.wait_ge(up_ready, q * PAIRS * 2 * FT)
                        for n in "qkvo":
                            sp.dma_start(slot_w[n][:, :, :], I[f"L0_ffn_d_W{n}"].rearrange("(k p) n -> p k n", p=P)).then_inc(slot_w_in, 16)
                    with sp.Fori(0, PAIRS - 1) as pair:
                        step(q, pair, pair + 1)
                    step(q, PAIRS - 1, 0 if q + 1 < Q else None)

            @block.tensor
            def _(pe):
                def up(q, n, i):
                    pe.wait_ge(nT_in[i], (n + 1) * 32)
                    for f in range(FT):
                        m = n * (2 * FT) + i * FT + f
                        if f >= 2:
                            pe.wait_ge(u_ready, m - 1)
                        else:
                            pe.wait_ge(u_ready, n * (2 * FT) + i * FT)
                        for g in (1, 0):
                            c = 0
                            for k in range(KT):
                                for w, m_ in products([t[:, k, g, f * P:(f + 1) * P] for t in w1[q % 2]], [t[:, k, :] for t in nT[i]]):
                                    last = nc.tensor.matmul(UP[f % 2][g][:, :], w, m_, start=c == 0, stop=c == 3 * KT - 1)
                                    c += 1
                        last.then_inc(up_ready, 1)

                def down(q, n, i):
                    if q == 0:
                        pe.wait_ge(raw_lo, PAIRS * 3)
                    pe.wait_ge(u_lo_done, n * (2 * FT) + (i + 1) * FT)
                    for t in range(TT):
                        m = n * (2 * TT) + i * TT
                        pe.wait_ge(down_taken, m + max(t - 1, 0))
                        c = 0
                        for f in range(FT):
                            for a, w in products([x[:, f, t * P:(t + 1) * P] for x in u[i]], [x[:, f, :] for x in w2[q % 2]]):
                                last = nc.tensor.matmul(DN[t % 2][:, :], a, w, start=c == 0, stop=c == 3 * FT - 1)
                                c += 1
                        last.then_inc(down_ready, 1)

                for q in range(Q):
                    pe.wait_ge(raw_lo, (q + 1) * PAIRS * 3 if q else 2 * PAIRS)
                    with pe.Fori(0, PAIRS) as pair:
                        n = pair + q * PAIRS
                        up(q, n, 0)
                        up(q, n, 1)
                        down(q, n, 0)
                        down(q, n, 1)

            @block.scalar
            def _(act):
                def split_weights(q, k, n):
                    for c in range(3):
                        act.wait_ge(raw_in[c], (n + 1 - PAIRS) * 16)
                        nc.scalar.copy(chunk(q, k, c)[1][0], raw[:, c, :]).then_inc(raw_hi, 1)

                def hidden(n, i):
                    for f in range(FT):
                        m = n * (2 * FT) + i * FT + f
                        act.wait_ge(up_ready, m + 1)
                        if f >= 2:
                            act.wait_ge(u_ready, m - 1)
                        nc.scalar.activation(sig[:, f % 2, :], UP[f % 2][1][:, :], ACT.Silu).then_inc(sig_ready, 1)
                        act.wait_ge(u_ready, m + 1)
                        if f == 0:
                            act.wait_ge(down_ready, n * (2 * TT))
                        nc.scalar.copy(u[i][0][:, f, :], u32[:, f % 2, :]).then_inc(u_hi_done, 1)

                for c in range(3):
                    act.wait_ge(early_in[c], PAIRS * 16)
                    for k in range(PAIRS):
                        nc.scalar.copy(chunk(0, k, c)[1][0], early_place(k, c)).then_inc(raw_hi, 1)
                act.wait_ge(raw_lo, PAIRS * 3)
                for q in range(Q):
                    with act.Fori(0, PAIRS) as pair:
                        n = pair + q * PAIRS
                        hidden(n, 0)
                        if q + 1 < Q:
                            split_weights(q + 1, pair, n + PAIRS)
                        hidden(n, 1)

            @block.gpsimd
            def _(pool):
                def split_weights(q, k, n):
                    for c in range(3):
                        pool.wait_ge(raw_hi, n * 3 + c + 1)
                        hi, lo = chunk(q, k, c)[1]
                        nc.gpsimd.tensor_tensor(lo, raw[:, c, :], plain(hi), ALU.subtract).then_inc(raw_lo, 1)

                for q in range(Q - 1):
                    with pool.Fori(0, PAIRS) as pair:
                        split_weights(q + 1, pair, pair + (q + 1) * PAIRS)

            @block.vector
            def _(dve):
                def hidden(n, i):
                    for f in range(FT):
                        m = n * (2 * FT) + i * FT + f
                        dve.wait_ge(sig_ready, m + 1)
                        dve.wait_ge(u_lo_done, n * (2 * FT) + i * FT + max(f - 1, 0))
                        nc.vector.tensor_tensor(u32[:, f % 2, :], sig[:, f % 2, :], UP[f % 2][0][:, :], ALU.mult).then_inc(u_ready, 1)
                        dve.wait_ge(u_hi_done, m + 1)
                        nc.vector.tensor_tensor(u[i][1][:, f, :], u32[:, f % 2, :], plain(u[i][0][:, f, :]), ALU.subtract).then_inc(u_lo_done, 1)

                def residual(q, n, i, b):
                    dve.wait_ge(x_in[i], (n + 1) * 16)
                    for t in range(TT):
                        dve.wait_ge(down_ready, n * (2 * TT) + i * TT + t + 1)
                        nc.vector.scalar_tensor_tensor(xs[i][:, t, :], DN[t % 2][:, :], gates[:, 0:1], xs[i][:, t, :],
                                                       ALU.mult, ALU.add).then_inc(down_taken, 1)
                    if q == Q - 1:
                        nc.vector.drain()
                        for t in range(TT):
                            last = nc.vector.bn_stats(x_stats[:, bass.ds(b * TT + t, 1), :].rearrange("p o n -> p (o n)"), xs[i][:, t, :])
                        last.then_inc(rows_seen, 1)

                for c in range(3):
                    for k in range(PAIRS):
                        dve.wait_ge(raw_hi, c * PAIRS + k + 1)
                        hi, lo = chunk(0, k, c)[1]
                        nc.vector.tensor_tensor(lo, early_place(k, c), plain(hi), ALU.subtract).then_inc(raw_lo, 1)
                nc.vector.drain()
                for q in range(Q):
                    with dve.Fori(0, PAIRS) as pair:
                        n = pair + q * PAIRS
                        hidden(n, 0)
                        hidden(n, 1)
                        residual(q, n, 0, pair * 2)
                        residual(q, n, 1, pair * 2 + 1)
        return x_out, Q * PAIRS * 16


def slot_attention(nc, whole, I, ident, x_stats, slot_w, weights_in, x1_stored, low_bytes, o1, hT, x1_d, yT_d):
    with ExitStack() as stage:
        mem = Memory(nc, stage, whole)
        x_v = x1_d.rearrange("b (t p) d -> b p t d", p=P)
        mem.sbuf("slot_weights_place", [P, 4, KT, D])
        o_att, oT = mem.sbuf("o_att", [P, D]), mem.sbuf("oT_s", [P, KT, P])
        e_gain, h_in = (mem.sbuf(n, [P, D]) for n in ("e_gain", "h_in"))
        ones = mem.sbuf("ones", [1, P])
        every = mem.sbuf("every", [NS, P])
        used = 4 * (B * TT * 6 + 4 * KT * D + 4 * D + 2 * P)
        mem.sbuf("slot_filler", [P, (low_bytes - used) // 4])
        with nc.sbuf_tensor("e_w1_0", [P, KT, FF], F32) as first_w1:
            pass
        first_w1_in = mem.sem("e_w1_in0")
        A = [mem.sbuf(f"A_{part}", [P, KT, HS], F32R) for part in ("hi", "lo")]
        wkT = mem.sbuf("wkT", [P, KT, D])
        xin = mem.sbuf("y_xin", [P, TT, D])
        y = mem.sbuf("y", [P, TT, D])
        yn = [mem.sbuf(f"yn_{part}", [P, 2, TT, D], F32R) for part in ("hi", "lo")]
        yT = [mem.sbuf(f"yT_{part}", [P, KT, S], F32R) for part in ("hi", "lo")]
        pT = [mem.sbuf(f"pT_{part}", [P, TT, HS], F32R) for part in ("hi", "lo")]
        prob = mem.sbuf("d_prob", [P, 2, S])
        z = mem.sbuf("z", [P, 2, D])
        wq, wk, wv, wo = (slot_w[n] for n in "qkvo")
        bias = {n: mem.sbuf(f"d_b{n}", [1, D]) for n in "qvo"}
        bk_col = mem.sbuf("d_bk_col", [P, KT])
        sq = mem.sbuf("sq", [NS, D])
        sqT = mem.sbuf("sqT", [P, KT, NS])
        q16 = mem.sbuf("q16", [NS, D])
        q_diag = mem.sbuf("q_diag", [P, KT, 4 * NS])
        shift = mem.sbuf("shift", [P, 2])
        mean, var, rstd, half = (mem.sbuf(f"y_{n}", [P, B * TT]) for n in ("mean", "var", "rstd", "half"))
        top, nb, total, inv = (mem.sbuf(f"d_{n}", [P, 2]) for n in ("top", "nb", "total", "inv"))
        e_shift = mem.sbuf("e_shift", [P, D])
        stat1, mv, sd = mem.sbuf("o_stats", [P, 6]), mem.sbuf("o_mv", [P, 2]), mem.sbuf("o_sd", [P, 1])
        zT = mem.sbuf("zT", [P, KT, SH, B, NS])
        G = [mem.bank(f"slot_general{i}") for i in range(5)]
        SC = [mem.bank(f"slot_scores{i}") for i in range(2)]

        small_in, gains_in = mem.sem("d_small_in"), mem.sem("d_gains_in")
        pe_step, dve_step, act_step = (mem.sem(f"d_{n}_step") for n in ("pe", "dve", "act"))
        sd_ready = mem.sem("d_sd_ready")
        x_in, y_ready, yn_hi_done, yn_lo_done, yT_out = (mem.sem(f"d_{n}") for n in ("x_in", "y_ready", "yn_hi", "yn_lo", "yT_out"))

        def norm_rows(b):
            for t in range(TT):
                n = b * TT + t
                col = slice(n, n + 1) if isinstance(b, int) else bass.ds(n, 1)
                last = nc.vector.tensor_scalar(y[:, t, :], xin[:, t, :], mean[:, col], rstd[:, col], ALU.subtract, ALU.mult)
            last.then_inc(y_ready, 1)

        with nc.Block() as block:
            @block.sync
            def _(sp):
                sp.dma_start(sq[:, :], I["L0_ffn_slot_query"].rearrange("o s d -> (o s) d")).then_inc(small_in, 16)
                sp.dma_start(bk_col[:, :], I["L0_ffn_d_bk"].rearrange("(k p) -> p k", p=P), allow_slow_non_contiguous=True).then_inc(small_in, 16)
                for n in "qvo":
                    sp.dma_start(bias[n][:, :], I[f"L0_ffn_d_b{n}"].unsqueeze(0)).then_inc(small_in, 16)
                x_out, all_stores = x1_stored
                for i in range(2):
                    sp.wait_ge(x_out[i], all_stores)
                sp.dma_start(xin[:, :, :], x_v[0]).then_inc(x_in, 16)
                for b in range(B):
                    sp.dma_start(e_gain[b * NS:(b + 1) * NS, :], I["L0_ffn_e_ln_g"]).then_inc(gains_in, 16)
                    sp.dma_start(e_shift[b * NS:(b + 1) * NS, :], I["L0_ffn_e_ln_b"]).then_inc(gains_in, 16)
                sp.wait_ge(weights_in, 64)

            @block.tensor
            def _(pe):
                pe.wait_ge(weights_in, 64)
                for c in range(KT):
                    if c >= 2:
                        pe.wait_ge(act_step, c - 1)
                    for k in range(KT):
                        last = nc.tensor.transpose(G[2 + c % 2][:, k * P:(k + 1) * P], wk[:, k, c * P:(c + 1) * P], ident[:, :])
                    last.then_inc(pe_step, 1)
                pe.wait_ge(small_in, 80)
                for k in range(KT):
                    last = nc.tensor.transpose(G[0][:, k * NS:(k + 1) * NS], sq[:, k * P:(k + 1) * P], ident[0:NS, 0:NS])
                last.then_inc(pe_step, 1)
                pe.wait_ge(dve_step, 2)
                nc.tensor.matmul(G[1][0:NS, :], ones[0:1, 0:NS], bias["q"][:, :], start=True, stop=False)
                for k in range(KT):
                    last = nc.tensor.matmul(G[1][0:NS, :], sqT[:, k, :], wq[:, k, :], start=False, stop=k == KT - 1)
                last.then_inc(pe_step, 1)
                pe.wait_ge(dve_step, 3)
                for k in range(KT):
                    last = nc.tensor.transpose(G[0][:, k * NS:(k + 1) * NS], q16[:, k * P:(k + 1) * P], ident[0:NS, 0:NS])
                last.then_inc(pe_step, 1)
                pe.wait_ge(dve_step, 4)
                pe.wait_ge(act_step, KT)
                for k in range(KT):
                    for c in range(KT):
                        at = (k % 2) * HS + c * 4 * NS
                        last = nc.tensor.matmul(SC[k // 2][:, at:at + 4 * NS], wkT[:, c, k * P:(k + 1) * P], q_diag[:, c, :], start=True, stop=True)
                for c in range(KT):
                    at = (c % 2) * 4 * NS
                    last = nc.tensor.matmul(G[4][at:at + 4 * NS, c // 2:c // 2 + 1], q_diag[:, c, :], bk_col[:, c:c + 1], start=True, stop=True)
                last.then_inc(pe_step, 1)

            @block.scalar
            def _(act):
                act.wait_ge(dve_step, 1)
                nc.scalar.activation(rstd[:, :], var[:, :], ACT.Sqrt).then_inc(sd_ready, 1)
                for c in range(KT):
                    act.wait_ge(pe_step, 1 + c)
                    nc.scalar.copy(wkT[:, c, :], G[2 + c % 2][:, :]).then_inc(act_step, 1)
                act.wait_ge(pe_step, KT + 4)
                for i in range(2):
                    nc.scalar.copy(A[0][:, 2 * i:2 * i + 2, :].rearrange("p k n -> p (k n)"), SC[i][:, :]).then_inc(act_step, 1)

            @block.vector
            def _(dve):
                nc.vector.memset(ones[:, :], 1.0)
                nc.vector.memset(q_diag[:, :, :], 0.0)
                for b in range(B):
                    nc.vector.tensor_copy(every[:, b * NS:(b + 1) * NS], ident[0:NS, 0:NS])
                rows_mean_var(nc, x_stats[:, :, :], mean[:, :], var[:, :], half[:, :])
                nc.vector.tensor_scalar(var[:, :], var[:, :], EPS, None, ALU.add).then_inc(dve_step, 1)
                dve.wait_ge(sd_ready, 1)
                nc.vector.reciprocal(rstd[:, :], rstd[:, :])
                dve.wait_ge(pe_step, KT + 1)
                nc.vector.tensor_copy(sqT[:, :, :].rearrange("p k s -> p (k s)"), G[0][:, 0:KT * NS]).then_inc(dve_step, 1)
                dve.wait_ge(pe_step, KT + 2)
                nc.vector.tensor_scalar(q16[:, :], G[1][0:NS, :], SD ** -0.5, None, ALU.mult).then_inc(dve_step, 1)
                dve.wait_ge(pe_step, KT + 3)
                for g in range(4):
                    rows = slice(g * SD, (g + 1) * SD)
                    last = nc.vector.tensor_copy(q_diag[rows, :, g * NS:(g + 1) * NS], G[0][rows, 0:KT * NS].rearrange("p (k s) -> p k s", k=KT))
                last.then_inc(dve_step, 1)
                dve.wait_ge(x_in, 16)
                norm_rows(0)
                dve.wait_ge(pe_step, KT + 4)
                nc.vector.tensor_copy(shift[:, :], G[4][:, 0:2])
                for i in range(2):
                    dve.wait_ge(act_step, KT + i + 1)
                    nc.vector.tensor_tensor(A[1][:, 2 * i:2 * i + 2, :].rearrange("p k n -> p (k n)"), SC[i][:, :],
                                            plain(A[0][:, 2 * i:2 * i + 2, :].rearrange("p k n -> p (k n)")), ALU.subtract)

        g_ready, g_hi, g_free = (mem.sem(f"d_{n}") for n in ("g_ready", "g_hi", "g_free"))
        scored, nb_ready, exps = (mem.sem(f"d_{n}") for n in ("scored", "nb_ready", "exps"))
        U_Y, U_P, U_Z, U_ZT, PER = 0, KT, KT + 2, KT + 4, KT + 6
        NG = len(G)
        assert PER % NG == 0
        HI = KT + 2

        def of(ap, b):
            return ap[b] if isinstance(b, int) else ap[bass.ds(b, 1)].rearrange("o p t d -> (o p) t d")

        def slot(t, b):
            return t[:, b % 2] if isinstance(b, int) else t[:, bass.ds(b % 2, 1)].rearrange("p o t d -> p (o t) d")

        with nc.Block() as block:
            @block.sync
            def _(sp):
                def keep(b):
                    sp.wait_ge(g_free, b * PER + U_P)
                    for part in range(2):
                        sp.dma_start(of(yT_d[part], b), plain(yT[part][:, :, :])).then_inc(yT_out, 16)

                with sp.Fori(0, B - 1) as b:
                    sp.wait_ge(y_ready, b + 1)
                    sp.dma_start(xin[:, :, :], of(x_v, b + 1)).then_inc(x_in, 16)
                    keep(b)
                keep(B - 1)
                sp.wait_ge(yn_lo_done, B)
                sp.wait_ge(scored, B * 2)
                load_w1(sp, first_w1, I["L0_ffn_e_W1"][0], first_w1_in)
                sp.wait_ge(yT_out, B * 32)

            @block.tensor
            def _(pe):
                def claim(b, u):
                    if not (isinstance(b, int) and b == 0 and u < NG):
                        pe.wait_ge(g_free, b * PER + u - (NG - 1))
                    return G[u % NG]

                def turn_rows(b):
                    pe.wait_ge(y_ready, b + 1)
                    for k in range(KT):
                        bank = claim(b, U_Y + k)
                        for t in range(TT):
                            last = nc.tensor.transpose(bank[:, t * P:(t + 1) * P], y[:, t, k * P:(k + 1) * P], ident[:, :])
                        last.then_inc(g_ready, 1)

                def score(b):
                    pe.wait_ge(g_free, b * PER + U_P)
                    pe.wait_ge(exps, b * 2)
                    for i in range(2):
                        n = 0
                        for k in range(KT):
                            for a, m in products([t[:, k, i * P:(i + 1) * P] for t in A], [t[:, k, :] for t in yT]):
                                last = nc.tensor.matmul(SC[i][:, :], a, m, start=n == 0, stop=n == 3 * KT - 1)
                                n += 1
                        last.then_inc(scored, 1)

                def turn_probs(b):
                    pe.wait_ge(exps, b * 2)
                    for half_ in range(2):
                        bank = claim(b, U_P + half_)
                        for t in range(2):
                            for i in range(2):
                                tok = (2 * half_ + t) * P
                                last = nc.tensor.transpose(bank[:, t * HS + i * P:t * HS + (i + 1) * P], prob[:, i, tok:tok + P], ident[:, :])
                        last.then_inc(g_ready, 1)

                def sums(b, prev):
                    pe.wait_ge(g_free, b * PER + U_Z)
                    pe.wait_ge(yn_lo_done, b)
                    for i in range(2):
                        bank = claim(b, U_Z + i)
                        n = 0
                        for t in range(TT):
                            for a, m in products([x[:, t, i * P:(i + 1) * P] for x in pT], [slot(x, prev) for x in yn]):
                                last = nc.tensor.matmul(bank[:, :], a, m[:, t, :], start=n == 0, stop=n == 3 * TT - 1)
                                n += 1
                        last.then_inc(g_ready, 1)
                    pe.wait_ge(g_free, b * PER + U_ZT)
                    for half_ in range(2):
                        bank = claim(b, U_ZT + half_)
                        for k in range(2):
                            for i in range(2):
                                d = (2 * half_ + k) * P
                                last = nc.tensor.transpose(bank[:, k * HS + i * P:k * HS + (i + 1) * P], z[:, i, d:d + P], ident[:, :])
                        last.then_inc(g_ready, 1)

                turn_rows(0)
                pe.drain().then_inc(g_ready, PER - U_P)
                score(0)
                with pe.Fori(1, B) as b:
                    turn_rows(b)
                    turn_probs(b)
                    score(b)
                    sums(b, b - 1)
                pe.drain().then_inc(g_ready, U_P)
                turn_probs(B)
                sums(B, B - 1)

            @block.scalar
            def _(act):
                def front(b):
                    act.wait_ge(y_ready, b + 1)
                    if not (isinstance(b, int) and b == 0):
                        act.wait_ge(g_ready, (b - 1) * PER + U_ZT)
                    nc.scalar.copy(slot(yn[0], b), y[:, :, :]).then_inc(yn_hi_done, 1)
                    if not (isinstance(b, int) and b == 0):
                        act.wait_ge(yT_out, b * 32)
                        act.wait_ge(scored, b * 2)
                    for k in range(KT):
                        act.wait_ge(g_ready, b * PER + U_Y + k + 1)
                        nc.scalar.copy(yT[0][:, k, :], G[(U_Y + k) % NG][:, :]).then_inc(g_hi, 1)

                def probs(b):
                    for i in range(2):
                        act.wait_ge(g_ready, b * PER + U_P + i + 1)
                        nc.scalar.copy(pT[0][:, 2 * i:2 * i + 2, :].rearrange("p t n -> p (t n)"), G[(U_P + i) % NG][:, :]).then_inc(g_hi, 1)

                def exp(b):
                    act.wait_ge(nb_ready, b + 1)
                    for i in range(2):
                        nc.scalar.activation(prob[:, i, :], SC[i][:, :], ACT.Exp, bias=nb[:, i:i + 1], accum_out=total[:, i:i + 1]).then_inc(exps, 1)

                front(0)
                act.drain().then_inc(g_hi, 2)
                exp(0)
                with act.Fori(1, B) as b:
                    front(b)
                    probs(b)
                    exp(b)
                act.drain().then_inc(g_hi, KT)
                probs(B)

            @block.gpsimd
            def _(pool):
                with pool.Fori(0, B) as b:
                    pool.wait_ge(yn_hi_done, b + 1)
                    nc.gpsimd.tensor_tensor(slot(yn[1], b), y[:, :, :], plain(slot(yn[0], b)), ALU.subtract).then_inc(yn_lo_done, 1)

            @block.vector
            def _(dve):
                def norm(b):
                    dve.wait_ge(x_in, b * 16 + 16)
                    dve.wait_ge(yn_lo_done, b)
                    norm_rows(b)

                def front(b):
                    for k in range(KT):
                        dve.wait_ge(g_hi, b * HI + k + 1)
                        nc.vector.tensor_tensor(yT[1][:, k, :], G[(U_Y + k) % NG][:, :], plain(yT[0][:, k, :]), ALU.subtract).then_inc(g_free, 1)

                def probs(b):
                    for i in range(2):
                        dve.wait_ge(g_hi, b * HI + KT + i + 1)
                        flat = lambda x: x[:, 2 * i:2 * i + 2, :].rearrange("p t n -> p (t n)")
                        nc.vector.tensor_tensor(flat(pT[1]), G[(U_P + i) % NG][:, :], plain(flat(pT[0])), ALU.subtract).then_inc(g_free, 1)

                def maxima(b):
                    for i in range(2):
                        dve.wait_ge(scored, b * 2 + i + 1)
                        nc.vector.tensor_reduce(top[:, i:i + 1], SC[i][:, :], AX.X, ALU.max)
                    nc.vector.drain()
                    nc.vector.tensor_tensor(top[:, :], top[:, :], shift[:, :], ALU.add)
                    nc.vector.drain()
                    nc.vector.tensor_tensor(nb[:, :], shift[:, :], top[:, :], ALU.subtract).then_inc(nb_ready, 1)

                def inverse(b):
                    dve.wait_ge(exps, b * 2)
                    nc.vector.reciprocal(inv[:, :], total[:, :])
                    nc.vector.drain()

                def sums(b, prev):
                    for i in range(2):
                        dve.wait_ge(g_ready, b * PER + U_Z + i + 1)
                        nc.vector.tensor_scalar(z[:, i, :], G[(U_Z + i) % NG][:, :], inv[:, i:i + 1], None, ALU.mult).then_inc(g_free, 1)
                    for i in range(2):
                        dve.wait_ge(g_ready, b * PER + U_ZT + i + 1)
                        to = zT[:, 2 * i:2 * i + 2, :, prev, :] if isinstance(prev, int) else \
                            zT[:, 2 * i:2 * i + 2, :, bass.ds(prev, 1), :].rearrange("p k h o s -> p k h (o s)")
                        nc.vector.tensor_copy(to, G[(U_ZT + i) % NG][:, :].rearrange("p (k h s) -> p k h s", k=2, h=SH)).then_inc(g_free, 1)

                front(0)
                nc.vector.drain().then_inc(g_free, PER - U_P)
                norm(1)
                maxima(0)
                with dve.Fori(1, B - 1) as b:
                    front(b)
                    inverse(b)
                    probs(b)
                    norm(b + 1)
                    maxima(b)
                    sums(b, b - 1)
                front(B - 1)
                inverse(B - 1)
                probs(B - 1)
                maxima(B - 1)
                sums(B - 1, B - 2)
                nc.vector.drain().then_inc(g_free, U_P)
                inverse(B)
                probs(B)
                sums(B, B - 1)

        def finish(load_first):
            pe2, dve2, act2 = (mem.sem(f"d2_{n}") for n in ("pe", "dve", "act"))
            with nc.Block() as block:
                @block.sync
                def _(sp):
                    load_first(sp)

                @block.tensor
                def _(pe):
                    nc.tensor.matmul(G[0][:, :], ones[0:1, :], bias["v"][:, :], start=True, stop=False)
                    for h in range(SH):
                        cols = slice(h * SD, (h + 1) * SD)
                        for k in range(KT):
                            last = nc.tensor.matmul(G[0][:, cols], zT[:, k, h, :, :].rearrange("p b s -> p (b s)"), wv[:, k, cols],
                                                    start=False, stop=h == SH - 1 and k == KT - 1)
                    last.then_inc(pe2, 1)
                    pe.wait_ge(dve2, 1)
                    for k in range(KT):
                        last = nc.tensor.transpose(G[1][:, k * P:(k + 1) * P], o_att[:, k * P:(k + 1) * P], ident[:, :])
                    last.then_inc(pe2, 1)
                    pe.wait_ge(dve2, 2)
                    nc.tensor.matmul(G[2][:, :], ones[0:1, :], bias["o"][:, :], start=True, stop=False)
                    nc.tensor.matmul(G[2][:, :], every[:, :], sq[:, :], start=False, stop=False)
                    for k in range(KT):
                        last = nc.tensor.matmul(G[2][:, :], oT[:, k, :], wo[:, k, :], start=False, stop=k == KT - 1)
                    last.then_inc(pe2, 1)
                    pe.wait_ge(dve2, 4)
                    for k in range(KT):
                        last = nc.tensor.transpose(G[3][:, k * P:(k + 1) * P], h_in[:, :].rearrange("r (p k) -> r k p", k=KT)[:, k, :], ident[:, :])
                    last.then_inc(pe2, 1)

                @block.scalar
                def _(act):
                    act.wait_ge(dve2, 3)
                    nc.scalar.activation(sd[:, :], sd[:, :], ACT.Sqrt).then_inc(act2, 1)

                @block.vector
                def _(dve):
                    dve.wait_ge(pe2, 1)
                    nc.vector.tensor_copy(o_att[:, :], G[0][:, :]).then_inc(dve2, 1)
                    dve.wait_ge(pe2, 2)
                    nc.vector.tensor_copy(oT[:, :, :].rearrange("p k n -> p (k n)"), G[1][:, :]).then_inc(dve2, 1)
                    dve.wait_ge(pe2, 3)
                    nc.vector.tensor_copy(o1[:, :], G[2][:, :])
                    nc.vector.drain()
                    nc.vector.bn_stats(stat1[:, :], o1[:, :])
                    nc.vector.drain()
                    nc.vector.bn_aggr(mv[:, :], stat1[:, :])
                    nc.vector.drain()
                    nc.vector.tensor_scalar(sd[:, :], mv[:, 1:2], EPS, None, ALU.add).then_inc(dve2, 1)
                    dve.wait_ge(act2, 1)
                    nc.vector.reciprocal(sd[:, :], sd[:, :])
                    nc.vector.drain()
                    nc.vector.tensor_scalar(h_in[:, :], o1[:, :], mv[:, 0:1], sd[:, 0:1], ALU.subtract, ALU.mult)
                    dve.wait_ge(gains_in, 2 * B * 16)
                    nc.vector.drain()
                    nc.vector.tensor_tensor(h_in[:, :], h_in[:, :], e_gain[:, :], ALU.mult)
                    nc.vector.drain()
                    nc.vector.tensor_tensor(h_in[:, :], h_in[:, :], e_shift[:, :], ALU.add).then_inc(dve2, 1)
                    dve.wait_ge(pe2, 4)
                    for k in range(KT):
                        nc.vector.tensor_copy(hT[:, k, :, :], G[3][:, k * P:(k + 1) * P].rearrange("p (b e) -> p e b", e=E))

        return first_w1, first_w1_in, finish


def load_w1(sp, w1, src, arrival):
    sp.dma_start(w1[:, :, :].rearrange("p k n -> p (k n)"), src.rearrange("(p k) n -> p (k n)", k=KT)).then_inc(arrival, 16)


def expert_low_bytes():
    FT = FF // P
    return 4 * (2 * FT * E + KT * 32 + 2 * FF // 4 + FT * 32 + D + B + KT * FF)


def experts(nc, whole, I, ident, hT, y_d, first_w1, first_w1_in, finish_slots):
    with ExitStack() as stage:
        mem = Memory(nc, stage, whole)
        FT = FF // P
        Q, QW = 4, 32
        C = FF // Q
        J = C // P
        block_at = [q * C + j * P for j in range(J) for q in range(Q)]
        biasT = [mem.sbuf(f"e_{n}T", [P, FT, E]) for n in ("b1", "bg")]
        h = mem.sbuf("e_h", [P, KT, QW])
        rows = [mem.sbuf(f"e_{n}_rows", [P, C]) for n in "ug"]
        pre = rows[0][:, 0:2 * FT * B].rearrange("p (n f b) -> p n f b", n=2, f=FT)
        ug = mem.sbuf("e_ug", [P, FT, QW])
        y_parts = mem.sbuf("e_y_parts", [P, D])
        ys = y_parts[0:B, :]
        fold = mem.sbuf("e_fold", [P, B])
        w1, wg, w2 = [None, None], [None, None], [None, None]
        w1[1] = mem.sbuf("e_w1_1", [P, KT, FF])
        for i in range(2):
            if i == 0:
                with nc.sbuf_tensor("c_lent", [P, 4, KT, D], F32) as lent:
                    pass
                mem.sbuf("first_w1_place", [P, KT, FF])
                w1[0] = first_w1
                with nc.sbuf_tensor("c_wo", [P, KT, D], F32) as c_wo:
                    pass
            wg[i] = mem.sbuf(f"e_wg_{i}", [P, KT, FF])
            w2[i] = mem.sbuf(f"e_w2_{i}", [P, FT, D])
        bias_rows = [w2[1][0:E, 4 * i:4 * i + 4, :].rearrange("e a n -> e (a n)") for i in range(2)]
        UP = [mem.bank(f"e_{n}") for n in "ug"]
        TB = [mem.bank(f"e_turned{i}") for i in range(2)]
        YB, YS = mem.bank("e_down"), mem.bank("e_folded")

        bias_in, bias_turned, bias_ready, fold_ready = (mem.sem(f"e_{n}") for n in ("bias_in", "bias_turned", "bias_ready", "fold_ready"))
        w1_in, wg_in, w2_in = ([mem.sem(f"e_{n}_in{i}") for i in range(2)] for n in ("w1_later", "wg", "w2"))
        w1_in[0] = first_w1_in
        h_ready, u_ready, g_ready, u_taken, g_taken, turned, pre_ready, silu_ready, ug_ready = (
            mem.sem(f"e_{n}") for n in ("h_ready", "u_ready", "g_ready", "u_taken", "g_taken", "turned", "pre_ready",
                                        "silu_ready", "ug_ready"))
        down_ready, parts_taken, folded, y_done, y_out = (
            mem.sem(f"e_{n}") for n in ("down_ready", "parts_taken", "folded", "y_done", "y_out"))

        def of(ap, e):
            return ap[e] if isinstance(e, int) else ap[bass.ds(e, 1)].rearrange("o a b -> (o a) b")

        def arrived(e, i):
            return e * 8 + (16 - 8 * i)

        wq_in, c_weights_in, b2_in = (mem.sem(f"c_{n}_in") for n in ("wq", "weights", "b2"))

        def load(sp, e, i, turn):
            later = not (isinstance(turn, int) and turn == 0)
            if later:
                sp.wait_ge(u_ready, turn * 2 + (i - 1))
            if later or i == 1:
                load_w1(sp, w1[i], of(I["L0_ffn_e_W1"], e), w1_in[i])
            if later:
                sp.wait_ge(g_ready, turn * 2 + (i - 1))
            load_w1(sp, wg[i], of(I["L0_ffn_e_Wg"], e), wg_in[i])
            if later:
                sp.wait_ge(down_ready, turn * 2 + (i - 1))
            elif i == 1:
                sp.wait_ge(bias_turned, 2)
            sp.dma_start(w2[i][:, :, :], of(I["L0_ffn_e_W2"], e).rearrange("(f p) n -> p f n", p=P)).then_inc(w2_in[i], 16)

        finish_slots(lambda sp: load(sp, 0, 0, 0))

        def skewed(eng, start, body, finish):
            start(0, 0)
            with eng.Fori(0, E // 2 - 1) as pair:
                for i in range(2):
                    body(pair * 2 + i, i)
            body(E - 2, 0)
            finish(E - 1, 1)

        with nc.Block() as block:
            @block.sync
            def _(sp):
                def store(e):
                    sp.wait_ge(y_done, e + 1)
                    dst = y_d[:, e, :] if isinstance(e, int) else y_d[:, bass.ds(e, 1), :].rearrange("b o d -> (b o) d")
                    sp.dma_start(dst, ys).then_inc(y_out, 16)

                for i, n in enumerate(("b1", "bg")):
                    sp.dma_start(bias_rows[i], I[f"L0_ffn_e_{n}"]).then_inc(bias_in, 16)
                load(sp, 1, 1, 0)
                with sp.Fori(1, E // 2) as turn:
                    for i in range(2):
                        load(sp, turn * 2 + i, i, turn)
                        store(turn * 2 + (i - 2))
                store(E - 2)
                sp.wait_ge(g_ready, E - 1)
                for i, n in enumerate("qkvo"):
                    sp.dma_start(lent[:, i, :, :] if n != "o" else c_wo[:, :, :],
                                 I[f"L0_ffn_c_W{n}"].rearrange("(k p) n -> p k n", p=P)).then_inc(wq_in if n == "q" else c_weights_in, 16)
                for b in range(B):
                    sp.dma_start(lent[b * NS:(b + 1) * NS, 3, 3, :], I["L0_ffn_e_b2"]).then_inc(b2_in, 16)
                store(E - 1)

            @block.tensor
            def _(pe):
                def grow(e, i):
                    pe.wait_ge(h_ready, e + 1)
                    for bank, w, arrival, taken, ready in ((UP[0], w1[i], w1_in[i], u_taken, u_ready), (UP[1], wg[i], wg_in[i], g_taken, g_ready)):
                        pe.wait_ge(arrival, arrived(e, i))
                        pe.wait_ge(taken, e)
                        for k in range(KT):
                            for q in range(Q):
                                last = nc.tensor.matmul(bank[q * QW:(q + 1) * QW, :], h[:, k, :], w[:, k, q * C:(q + 1) * C], start=k == 0, stop=k == KT - 1)
                        last.then_inc(ready, 1)

                def turn(e):
                    pe.wait_ge(pre_ready, e)
                    for n, taken in enumerate((u_taken, g_taken)):
                        pe.wait_ge(taken, e + 1)
                        for j in range(J):
                            last = nc.tensor.transpose(TB[n][:, j * P:(j + 1) * P], rows[n][:, j * P:(j + 1) * P], ident[:, :])
                    last.then_inc(turned, 1)

                def shrink(e, i):
                    pe.wait_ge(ug_ready, e + 1)
                    pe.wait_ge(w2_in[i], arrived(e, i))
                    pe.wait_ge(parts_taken, e)
                    for j in range(J):
                        for q in range(Q):
                            last = nc.tensor.matmul(YB[q * QW:(q + 1) * QW, :], ug[:, j * Q + q, :], w2[i][:, q * J + j, :], start=j == 0, stop=j == J - 1)
                    last.then_inc(down_ready, 1)

                def add_parts(e):
                    pe.wait_ge(parts_taken, e + 1)
                    pe.wait_ge(y_done, e)
                    nc.tensor.matmul(YS[0:B, :], fold[:, :], y_parts[:, :], start=True, stop=True).then_inc(folded, 1)

                def both(e, i):
                    grow(e + 1, 1 - i)
                    shrink(e, i)
                    turn(e + 1)
                    add_parts(e)

                def start(e, i):
                    grow(e, i)
                    pe.wait_ge(bias_in, 32)
                    for n in range(2):
                        for f, at in enumerate(block_at):
                            last = nc.tensor.transpose(TB[n][:, f * E:(f + 1) * E], bias_rows[n][:, at:at + P], ident[0:E, 0:E])
                        last.then_inc(bias_turned, 1)
                    pe.wait_ge(bias_ready, 2)
                    turn(e)

                def finish(e, i):
                    shrink(e, i)
                    add_parts(e)

                pe.wait_ge(fold_ready, 1)
                skewed(pe, start, both, finish)

            @block.scalar
            def _(act):
                def start(e, i):
                    act.wait_ge(u_ready, e + 1)
                    act.wait_ge(ug_ready, e)
                    nc.scalar.copy(rows[0][:, :], UP[0][:, :]).then_inc(u_taken, 1)

                def finish(e, i):
                    act.wait_ge(down_ready, e + 1)
                    act.wait_ge(y_out, e * 16)
                    nc.scalar.copy(y_parts[:, :], YB[:, :]).then_inc(parts_taken, 1)

                def gates_of(e):
                    act.wait_ge(pre_ready, e + 1)
                    nc.scalar.activation(pre, pre, ACT.Silu).then_inc(silu_ready, 1)

                def both(e, i):
                    start(e + 1, 1 - i)
                    finish(e, i)
                    gates_of(e + 1)

                def first(e, i):
                    start(e, i)
                    gates_of(e)

                skewed(act, first, both, finish)

            @block.vector
            def _(dve):
                def take_h(e):
                    src = hT[:, :, e, :] if isinstance(e, int) else hT[:, :, bass.ds(e, 1), :].rearrange("p k o b -> p k (o b)")
                    nc.vector.tensor_copy(h[:, :, 0:B], src).then_inc(h_ready, 1)

                def start(e, i):
                    dve.wait_ge(g_ready, e + 1)
                    dve.wait_ge(turned, e)
                    nc.vector.tensor_copy(rows[1][:, :], UP[1][:, :]).then_inc(g_taken, 1)
                    if not (isinstance(e, int) and e == E - 1):
                        take_h(e + 1)

                def product(e):
                    dve.wait_ge(turned, e + 1)
                    for n in range(2):
                        cols = TB[n][:, :].rearrange("p (f r) -> p f r", r=QW)[:, :, 0:B]
                        add = biasT[n][:, :, e:e + 1] if isinstance(e, int) else biasT[n][:, :, bass.ds(e, 1)]
                        last = nc.vector.tensor_tensor(pre[:, n, :, :], cols, add.to_broadcast([P, FT, B]), ALU.add)
                    last.then_inc(pre_ready, 1)
                    dve.wait_ge(silu_ready, e + 1)
                    dve.wait_ge(down_ready, e)
                    nc.vector.tensor_tensor(ug[:, :, 0:B], pre[:, 0, :, :], pre[:, 1, :, :], ALU.mult).then_inc(ug_ready, 1)

                def finish(e, i):
                    dve.wait_ge(folded, e + 1)
                    nc.vector.tensor_copy(ys, YS[0:B, :]).then_inc(y_done, 1)

                def both(e, i):
                    start(e + 1, 1 - i)
                    product(e + 1)
                    finish(e, i)

                def first(e, i):
                    start(e, i)
                    product(e)

                nc.vector.memset(h[:, :, :], 0.0)
                nc.vector.memset(ug[:, :, :], 0.0)
                nc.vector.tensor_tensor(fold[:, :], ident[:, 0:B], ident[:, QW:QW + B], ALU.add)
                for q in range(2, Q):
                    nc.vector.drain()
                    last = nc.vector.tensor_tensor(fold[:, :], fold[:, :], ident[:, q * QW:q * QW + B], ALU.add)
                last.then_inc(fold_ready, 1)
                take_h(0)
                for n in range(2):
                    dve.wait_ge(bias_turned, n + 1)
                    nc.vector.tensor_copy(biasT[n][:, :, :].rearrange("p f e -> p (f e)"), TB[n][:, 0:FT * E]).then_inc(bias_ready, 1)
                skewed(dve, first, both, finish)
        return lent, c_wo, wq_in, c_weights_in, b2_in, y_out


def token_attention(nc, whole, I, ident, gates, low_bytes, early_weights, o1, x1_d, yT_d, y_d, out):
    lent, wo, wq_in, c_weights_in, b2_in, y_out = early_weights
    wq, wk, wv = (lent[:, i, :, :] for i in range(3))
    o2, o2T, y_rows, b2_rows = (lent[:, 3, i, :] for i in range(4))
    with ExitStack() as stage:
        mem = Memory(nc, stage, whole)
        HT = HS // P
        CH = P // SD
        x_v = x1_d.rearrange("b (t p) d -> b p t d", p=P)
        out_v = out.rearrange("b (t p) d -> b p t d", p=P)
        PB = TT // 2
        bias_k = mem.sbuf("bias_k", [P, B, HS])
        bo_gate = mem.sbuf("bo_gate", [P, D])
        early_yT = [mem.sbuf(f"c_yT_{part}0", [P, KT, S], F32R) for part in ("hi", "lo")]
        early_x = mem.sbuf("c_x0", [P, TT, D])
        with nc.sbuf_tensor("c_wqT", [P, KT, D], F32) as wqT:
            pass
        pT = [mem.sbuf(f"c_pT_{part}", [P, PB, 2, HT, P], F32R) for part in ("hi", "lo")]
        top, total = (mem.sbuf(f"c_{n}", [P, PB, 2 * SH]) for n in ("top", "total"))
        used = 4 * (B * HS + D + 2 * KT * S + TT * D + 4 * PB * HT * P + 4 * PB * SH)
        mem.sbuf("c_filler", [P, (low_bytes - used) // 4])
        VW_lo = mem.sbuf("VW_lo", [P, B, HT, D], F32R)
        xs = [early_x, mem.sbuf("c_x1", [P, TT, D])]
        WK = [mem.sbuf(f"WK_{part}", [P, KT, B, HS], F32R) for part in ("hi", "lo")]
        VW = [mem.sbuf("VW_hi", [P, B, HT, D], F32R), VW_lo]
        yT_in, x_in, x_out = ([mem.sem(f"c_{n}{i}") for i in range(2)] for n in ("yT_in", "x_in", "x_out"))

        def of(ap, b):
            return ap[b] if isinstance(b, int) else ap[bass.ds(b, 1)].rearrange("o p t d -> (o p) t d")

        slots_in, c_small_in = (mem.sem(f"c_{n}") for n in ("slots_in", "small_in"))
        o2_ready, blocks_zero, w_ready, w_hi, w_free = (mem.sem(f"c_{n}") for n in ("o2_ready", "blocks_zero", "w_ready", "w_hi", "w_free"))
        with ExitStack() as early:
            first = Memory(nc, early, whole)
            k_diag = first.sbuf("k_diag", [P, KT, B, CH * NS])
            v_diag = first.sbuf("v_diag", [P, KT, B, P])
            bias = {n: first.sbuf(f"c_b{n}_col", [P, KT]) for n in "qkv"}
            banks = [first.bank(f"c_general{i}") for i in range(8)]
            U_WQ, U_O2, U_K, U_V, U_BK = 0, KT, KT + 1, KT + 2, KT + 3
            U_WK = U_BK + KT
            U_VW = U_WK + KT * KT
            of_bank = lambda u: banks[u % 8]

            with nc.Block() as block:
                @block.sync
                def _(sp):
                    sp.wait_ge(y_out, E * 16)
                    sp.dma_start(y_rows, y_d.rearrange("b e d -> (b e) d")).then_inc(slots_in, 16)
                    for n in "qkv":
                        sp.dma_start(bias[n][:, :], I[f"L0_ffn_c_b{n}"].rearrange("(k p) -> p k", p=P), allow_slow_non_contiguous=True).then_inc(c_small_in, 16)
                    sp.dma_start(bo_gate[:, :], I["L0_ffn_c_bo"].unsqueeze(0).to_broadcast([P, D])).then_inc(c_small_in, 16)
                    for part in range(2):
                        sp.dma_start(plain(early_yT[part][:, :, :]), yT_d[part][0]).then_inc(yT_in[0], 16)
                    sp.dma_start(early_x[:, :, :], x_v[0]).then_inc(x_in[0], 16)

                @block.tensor
                def _(pe):
                    def claim(u):
                        if u >= 8:
                            pe.wait_ge(w_free, u - 7)
                        return of_bank(u)

                    pe.wait_ge(wq_in, 16)
                    for c in range(KT):
                        bank = claim(U_WQ + c)
                        for k in range(KT):
                            last = nc.tensor.transpose(bank[:, k * P:(k + 1) * P], wq[:, k, c * P:(c + 1) * P], ident[:, :])
                        last.then_inc(w_ready, 1)
                    pe.wait_ge(o2_ready, 1)
                    bank = claim(U_O2)
                    for k in range(KT):
                        last = nc.tensor.transpose(bank[:, k * P:(k + 1) * P], o2[:, k * P:(k + 1) * P], ident[:, :])
                    last.then_inc(w_ready, 1)
                    pe.wait_ge(c_weights_in, 48)
                    pe.wait_ge(w_free, U_O2 + 1)
                    for u, w in ((U_K, wk), (U_V, wv)):
                        bank = claim(u)
                        for c in range(KT):
                            for k in range(KT):
                                last = nc.tensor.matmul(bank[:, c * P:(c + 1) * P], w[:, k, c * P:(c + 1) * P], o2T[:, k * P:(k + 1) * P],
                                                        start=k == 0, stop=k == KT - 1)
                        last.then_inc(w_ready, 1)
                    pe.wait_ge(w_free, U_K + 1)
                    keys = lambda c: k_diag[:, c, :, :].rearrange("p b n -> p (b n)")
                    for c in range(KT):
                        nc.tensor.matmul(claim(U_BK + c)[:, :], bias["q"][:, c:c + 1].to_broadcast([P, P]), keys(c), start=True, stop=True).then_inc(w_ready, 1)
                    for k in range(KT):
                        for c in range(KT):
                            nc.tensor.matmul(claim(U_WK + k * KT + c)[:, :], wqT[:, c, k * P:(k + 1) * P], keys(c), start=True, stop=True).then_inc(w_ready, 1)
                    for b in range(B):
                        for t in range(HT):
                            bank = claim(U_VW + b * HT + t)
                            for c in (2 * t, 2 * t + 1):
                                last = nc.tensor.matmul(bank[:, :], v_diag[:, c, b, :], wo[:, c, :], start=c == 2 * t, stop=c == 2 * t + 1)
                            last.then_inc(w_ready, 1)

                def split_places():
                    for k in range(KT):
                        for c in range(KT):
                            cols = slice(c * CH * NS, (c + 1) * CH * NS)
                            yield U_WK + k * KT + c, [t[:, k, :, cols] for t in WK], True
                    for b in range(B):
                        for t in range(HT):
                            yield U_VW + b * HT + t, [x[:, b, t, :] for x in VW], False

                def as_place(u, heads):
                    return of_bank(u)[:, :].rearrange("p (b n) -> p b n", b=B) if heads else of_bank(u)[:, :]

                @block.gpsimd
                def _(pool):
                    nc.gpsimd.memset(k_diag[:, :, :, :], 0.0).then_inc(blocks_zero, 1)
                    nc.gpsimd.memset(v_diag[:, :, :, :], 0.0).then_inc(blocks_zero, 1)

                @block.scalar
                def _(act):
                    for u, (hi, _), heads in split_places():
                        act.wait_ge(w_ready, u + 1)
                        nc.scalar.copy(hi, as_place(u, heads)).then_inc(w_hi, 1)

                @block.vector
                def _(dve):
                    for c in range(KT):
                        dve.wait_ge(w_ready, U_WQ + c + 1)
                        nc.vector.tensor_copy(wqT[:, c, :], of_bank(U_WQ + c)[:, :]).then_inc(w_free, 1)
                    dve.wait_ge(b2_in, B * 16)
                    nc.vector.tensor_tensor(o2, o1[:, :], b2_rows, ALU.add)
                    nc.vector.drain()
                    dve.wait_ge(slots_in, 16)
                    nc.vector.tensor_tensor(o2, o2, y_rows, ALU.add).then_inc(o2_ready, 1)
                    dve.wait_ge(c_small_in, 4 * 16)
                    nc.vector.tensor_scalar(bo_gate[:, :], bo_gate[:, :], gates[:, 1:2], None, ALU.mult)
                    dve.wait_ge(w_ready, U_O2 + 1)
                    nc.vector.tensor_copy(o2T, of_bank(U_O2)[:, :]).then_inc(w_free, 1)
                    dve.wait_ge(blocks_zero, 2)
                    for u, n in ((U_K, "k"), (U_V, "v")):
                        dve.wait_ge(w_ready, u + 1)
                        for c in range(KT):
                            for g in range(CH):
                                rows = slice(g * SD, (g + 1) * SD)
                                src = of_bank(u)[rows, c * P:(c + 1) * P].rearrange("p (b s) -> p b s", b=B)
                                add = bias[n][rows, c:c + 1]
                                if n == "k":
                                    last = nc.vector.tensor_scalar(k_diag[rows, c, :, g * NS:(g + 1) * NS], src, add, SD ** -0.5, ALU.add, ALU.mult)
                                else:
                                    at = (c % 2) * CH * NS + g * NS
                                    last = nc.vector.tensor_scalar(v_diag[rows, c, :, at:at + NS], src, add, None, ALU.add)
                        last.then_inc(w_free, 1)
                    for c in range(KT):
                        dve.wait_ge(w_ready, U_BK + c + 1)
                        nc.vector.tensor_copy(bias_k[:, :, c * CH * NS:(c + 1) * CH * NS], as_place(U_BK + c, True)).then_inc(w_free, 1)
                    for n, (u, (hi, lo), heads) in enumerate(split_places()):
                        dve.wait_ge(w_hi, n + 1)
                        nc.vector.tensor_tensor(lo, as_place(u, heads), plain(hi), ALU.subtract).then_inc(w_free, 1)

        yT = [early_yT, [mem.sbuf(f"c_yT_{part}1", [P, KT, S], F32R) for part in ("hi", "lo")]]
        prob = [mem.sbuf(f"c_prob{i}", [P, PB, 2, HS]) for i in range(2)]
        SC = [mem.bank(f"c_scores{i}") for i in range(PB)]
        TB = [mem.bank(f"c_turned{i}") for i in range(PB)]
        OB = [mem.bank(f"c_out{i}") for i in range(TT)]
        scored, shifted, exps, probs_ready, turned, p_hi, p_lo = (
            mem.sem(f"c_{n}") for n in ("scored", "shifted", "exps", "probs_ready", "turned", "p_hi", "p_lo"))
        bo_added, summed, x_done = (mem.sem(f"c_{n}") for n in ("bo_added", "summed", "x_done"))

        def arrived(b, i, size):
            return b * (size // 2) + (size - (size // 2) * i)

        def skewed(eng, start, body, finish):
            start(0, 0)
            with eng.Fori(0, B // 2 - 1) as pair:
                for i in range(2):
                    body(pair * 2 + i, i)
            body(B - 2, 0)
            finish(B - 1, 1)

        with nc.Block() as block:
            @block.sync
            def _(sp):
                def load_y(b, i):
                    for part in range(2):
                        sp.dma_start(plain(yT[i][part][:, :, :]), of(yT_d[part], b)).then_inc(yT_in[i], 16)

                def load_x(b, i):
                    sp.dma_start(xs[i][:, :, :], of(x_v, b)).then_inc(x_in[i], 16)

                def after(b, i):
                    again, ahead = b + 2, b + 3
                    if not (isinstance(b, int) and ahead >= B):
                        sp.wait_ge(scored, (b + 2) * PB)
                        load_y(ahead, 1 - i)
                    sp.wait_ge(x_done, (b + 1) * TT)
                    sp.dma_start(of(out_v, b), xs[i][:, :, :]).then_inc(x_out[i], 16)
                    if not (isinstance(b, int) and again >= B):
                        sp.wait_ge(x_out[i], arrived(b, i, 16))
                        load_x(again, i)

                load_y(1, 1)
                load_x(1, 1)
                sp.wait_ge(scored, PB)
                load_y(2, 0)
                with sp.Fori(0, B // 2 - 2) as pair:
                    for i in range(2):
                        after(pair * 2 + i, i)
                for b in range(B - 4, B):
                    after(b, b % 2)
                for i in range(2):
                    sp.wait_ge(x_out[i], B // 2 * 16)

            @block.gpsimd
            def _(pool):
                with pool.Fori(0, B // 2) as pair:
                    for i in range(2):
                        pool.wait_ge(x_in[i], pair * 16 + 16)
                        nc.gpsimd.tensor_tensor(xs[i][:, :, :], xs[i][:, :, :], bo_gate[:, :].unsqueeze(1).to_broadcast([P, TT, D]), ALU.add).then_inc(bo_added, 1)

            @block.tensor
            def _(pe):
                def scores(b, i):
                    pe.wait_ge(yT_in[i], arrived(b, i, 32))
                    for j in range(PB):
                        if not (isinstance(b, int) and b == 0):
                            pe.wait_ge(shifted, (b - 1) * PB + j + 1)
                        for t in range(2):
                            n = 0
                            tok = (2 * j + t) * P
                            for k in range(KT):
                                of_b = [w[:, k, b, :] if isinstance(b, int) else w[:, k, bass.ds(b, 1), :].rearrange("p o n -> p (o n)") for w in WK]
                                for a, w in products([y[:, k, tok:tok + P] for y in yT[i]], of_b):
                                    last = nc.tensor.matmul(SC[j][:, t * HS:(t + 1) * HS], a, w, start=n == 0, stop=n == 3 * KT - 1)
                                    n += 1
                        last.then_inc(scored, 1)

                def turn(b, i):
                    pe.wait_ge(p_lo, b * PB)
                    for j in range(PB):
                        pe.wait_ge(probs_ready, b * PB + j + 1)
                        for t in range(2):
                            for r in range(HT):
                                at = (t * HT + r) * P
                                last = nc.tensor.transpose(TB[j][:, at:at + P], prob[i][:, j, t, r * P:(r + 1) * P], ident[:, :])
                        last.then_inc(turned, 1)

                def sums(b, i):
                    pe.wait_ge(x_done, b * TT)
                    for t in range(TT):
                        j = t // 2
                        pe.wait_ge(p_lo, b * PB + j + 1)
                        n = 0
                        for r in range(HT):
                            of_b = [w[:, b, r, :] if isinstance(b, int) else w[:, bass.ds(b, 1), r, :].rearrange("p o n -> p (o n)") for w in VW]
                            for a, w in products([p[:, j, t % 2, r, :] for p in pT], of_b):
                                last = nc.tensor.matmul(OB[t][:, :], a, w, start=n == 0, stop=n == 3 * HT - 1)
                                n += 1
                        last.then_inc(summed, 1)

                def both(b, i):
                    turn(b, i)
                    scores(b + 1, 1 - i)
                    sums(b, i)

                def finish(b, i):
                    turn(b, i)
                    sums(b, i)

                skewed(pe, scores, both, finish)

            @block.scalar
            def _(act):
                def exp(b, i):
                    for j in range(PB):
                        act.wait_ge(shifted, b * PB + j + 1)
                        nc.scalar.activation(prob[i][:, j, :, :], prob[i][:, j, :, :], ACT.Exp).then_inc(exps, 1)

                def split(b, i):
                    if not (isinstance(b, int) and b == 0):
                        act.wait_ge(summed, b * TT)
                    for j in range(PB):
                        act.wait_ge(turned, b * PB + j + 1)
                        nc.scalar.copy(pT[0][:, j, :, :, :].rearrange("p t r n -> p (t r n)"), TB[j][:, :]).then_inc(p_hi, 1)

                def both(b, i):
                    split(b, i)
                    exp(b + 1, 1 - i)

                skewed(act, exp, both, split)

            @block.vector
            def _(dve):
                by_head = lambda j, i: prob[i][:, j, :, :].rearrange("p t (h s) -> p (t h) s", s=NS)
                per_slot = lambda a: a.unsqueeze(2).to_broadcast([P, 2 * SH, NS])

                def shift(b, i):
                    for j in range(PB):
                        dve.wait_ge(scored, b * PB + j + 1)
                        add = bias_k[:, b:b + 1, :] if isinstance(b, int) else bias_k[:, bass.ds(b, 1), :]
                        nc.vector.tensor_tensor(prob[i][:, j, :, :], SC[j][:, :].rearrange("p (t n) -> p t n", t=2),
                                                add.to_broadcast([P, 2, HS]), ALU.add)
                        nc.vector.drain()
                        nc.vector.tensor_reduce(top[:, j, :], by_head(j, i), AX.X, ALU.max)
                        nc.vector.drain()
                        nc.vector.tensor_tensor(by_head(j, i), by_head(j, i), per_slot(top[:, j, :]), ALU.subtract).then_inc(shifted, 1)

                def normalise(b, i):
                    for j in range(PB):
                        dve.wait_ge(exps, b * PB + j + 1)
                        nc.vector.tensor_reduce(total[:, j, :], by_head(j, i), AX.X, ALU.add)
                        nc.vector.drain()
                        nc.vector.reciprocal(total[:, j, :], total[:, j, :])
                        nc.vector.drain()
                        nc.vector.tensor_tensor(by_head(j, i), by_head(j, i), per_slot(total[:, j, :]), ALU.mult).then_inc(probs_ready, 1)

                def low_parts(b, i):
                    for j in range(PB):
                        dve.wait_ge(p_hi, b * PB + j + 1)
                        flat = [p[:, j, :, :, :].rearrange("p t r n -> p (t r n)") for p in pT]
                        nc.vector.tensor_tensor(flat[1], TB[j][:, :], plain(flat[0]), ALU.subtract).then_inc(p_lo, 1)

                def add_to_x(b, i):
                    dve.wait_ge(bo_added, b + 1)
                    for t in range(TT):
                        dve.wait_ge(summed, b * TT + t + 1)
                        nc.vector.scalar_tensor_tensor(xs[i][:, t, :], OB[t][:, :], gates[:, 1:2], xs[i][:, t, :], ALU.mult, ALU.add).then_inc(x_done, 1)

                def start(b, i):
                    shift(b, i)
                    normalise(b, i)

                def both(b, i):
                    low_parts(b, i)
                    start(b + 1, 1 - i)
                    add_to_x(b, i)

                def finish(b, i):
                    low_parts(b, i)
                    add_to_x(b, i)

                skewed(dve, start, both, finish)


def gated_block(nc, I, out):
    scratch = lambda name, shape: nc.dram_tensor(name, shape, F32, kind="Internal").ap()
    x1_d = scratch("x1", [B, S, D])
    xnT_d = scratch("xnT", [2, B, P, KT, S])
    y_d = scratch("slot_y", [B, E, D])
    with ExitStack() as whole:
        sbuf = lambda stack, name, shape: stack.enter_context(nc.sbuf_tensor(name, shape, F32))
        ident, gates = sbuf(whole, "ident", [P, P]), sbuf(whole, "gates", [P, 2])
        with ExitStack() as plan:
            sbuf(plan, "below_first_w1", [P, D + KT * E * B + B * TT * 6 + 2 * KT * FF // FFQ])
            first_w1 = sbuf(plan, "ff_first_w1", [P, KT, 2, FF // FFQ])
        first_w1_in = [whole.enter_context(nc.semaphore(f"ff_first_w1_in{c}")) for c in range(2)]

        def load_wff1(sp):
            for c in range(2):
                for k in range(KT):
                    sp.dma_start(first_w1[:, k, c, :], wff1_block(I, 0, k, c)).then_inc(first_w1_in[c], 16)

        x1_begun = cross_attention(nc, whole, I, ident, gates, load_wff1, x1_d, xnT_d)
        o1 = sbuf(whole, "o1", [P, D])
        with ExitStack() as until_experts:
            hT = sbuf(until_experts, "hT", [P, KT, E, B])
            with ExitStack() as until_slots:
                x_stats = sbuf(until_slots, "x_stats", [P, B * TT, 6])
                slot_w_in = whole.enter_context(nc.semaphore("slot_weights_in"))
                with ExitStack() as place:
                    slot_w = {n: sbuf(place, f"d_w{n}", [P, KT, D]) for n in "qkvo"}
                x1_stored = feed_forward(nc, whole, I, gates, first_w1, first_w1_in, x_stats, slot_w, slot_w_in, x1_begun, x1_d, xnT_d)
                first_w1, first_w1_in, finish_slots = slot_attention(nc, whole, I, ident, x_stats, slot_w, slot_w_in, x1_stored, expert_low_bytes(), o1, hT, x1_d, xnT_d)
            early_weights = experts(nc, whole, I, ident, hT, y_d, first_w1, first_w1_in, finish_slots)
        token_attention(nc, whole, I, ident, gates, 4 * KT * E * B + expert_low_bytes(), early_weights, o1, x1_d, xnT_d, y_d, out)


INPUTS = ["x", "ctx_1024", "mask_BxS2_ik0", "g_xattn", "g_ffn"] + [f"L0_xattn_{n}" for n in (
    "gamma", "ctx_gamma", "Wq", "Wkv", "Wout", "Wff1", "Wff2")] + ["L0_ffn_slot_query"] + [
    f"L0_ffn_{a}_{w}{n}" for a in "dc" for w in "Wb" for n in "qkvo"] + [
    f"L0_ffn_e_{n}" for n in ("ln_g", "ln_b", "W1", "b1", "Wg", "bg", "W2", "b2")]


def kernel(**inputs):
    import numpy as np
    import concourse.bacc as bacc
    from concourse.bass_utils import run_bass_kernel_spmd

    nc = bacc.Bacc("TRN2", target_bir_lowering=False, num_devices=1)
    arrays, I = {}, {}
    for name in INPUTS:
        a = np.ascontiguousarray(inputs[name])
        arrays[f"in_{name}"] = a
        I[name] = nc.dram_tensor(f"in_{name}", a.shape, mybir.dt.from_np(a.dtype), kind="ExternalInput").ap()
    out = nc.dram_tensor("out", [B, S, D], F32, kind="ExternalOutput").ap()
    gated_block(nc, I, out)
    return run_bass_kernel_spmd(nc, [arrays], core_ids=[0]).results[0]["out"]
```
